# Optimizing a Trainium2 kernel written in Bass

```python
import numpy as np
import jax
import jax.numpy as jnp

def _softmax(x, axis=-1):
    return jax.nn.softmax(x, axis=axis)

def _gelu(x):
    return jax.nn.gelu(x, approximate=True)

def _silu(x):
    return jax.nn.silu(x)

def _sigmoid(x):
    return jax.nn.sigmoid(x)

def _layernorm(x, axis=-1, eps=1e-05):
    m = jnp.mean(x, axis=axis, keepdims=True)
    v = jnp.var(x, axis=axis, keepdims=True)
    return (x - m) / jnp.sqrt(v + eps)

def _scatter_add(tgt, idx, src, axis=0):
    return tgt.at[idx].add(src)

def _segment_sum(src, seg, n):
    return jax.ops.segment_sum(src, seg, n)
kernel_name = 'mk_seq_postln_d4_jaxref_r8_fcb296'

def setup_inputs(seed: int=0):
    np.random.seed(seed)
    _w = jnp.asarray

    def _L0_attn_setup():
        import jax, jax.numpy as jnp
        import numpy as np
        DIM = 128
        NUM_HEADS = 16
        HEAD_DIM = DIM // NUM_HEADS
        B, L = (4, 256)

        def _alibi_bias_causal(seq_len, dtype):
            h = jnp.arange(1, NUM_HEADS + 1, dtype=jnp.float32)
            slopes = jnp.power(2.0, -8.0 * h / NUM_HEADS)
            pos = jnp.arange(seq_len, dtype=jnp.float32)
            rel = jnp.abs(pos[:, None] - pos[None, :])
            bias = -slopes[:, None, None] * rel[None, :, :]
            causal = pos[:, None] >= pos[None, :]
            bias = jnp.where(causal[None, :, :], bias, -jnp.inf)
            return bias.astype(dtype)
        key = jax.random.key(seed)
        ks = jax.random.split(key, 9)
        s = 0.02
        return {'x': jax.random.normal(ks[0], (B, L, DIM), jnp.float32), 'Wq': jax.random.normal(ks[1], (DIM, DIM), jnp.float32) * s, 'bq': jax.random.normal(ks[2], (DIM,), jnp.float32) * s, 'Wk': jax.random.normal(ks[3], (DIM, DIM), jnp.float32) * s, 'bk': jax.random.normal(ks[4], (DIM,), jnp.float32) * s, 'Wv': jax.random.normal(ks[5], (DIM, DIM), jnp.float32) * s, 'bv': jax.random.normal(ks[6], (DIM,), jnp.float32) * s, 'Wo': jax.random.normal(ks[7], (DIM, DIM), jnp.float32) * s, 'bo': jax.random.normal(ks[8], (DIM,), jnp.float32) * s}
    _L0_attn_in = _L0_attn_setup()

    def _L0_ffn_setup():
        import jax, jax.numpy as jnp
        import numpy as np
        DIM = 128

        def _reference_tuple_inner(x, W_r, W_k, W_v, mu_r, mu_k):
            B, T, C = x.shape
            x_prev = jnp.concatenate([jnp.zeros((B, 1, C), x.dtype), x[:, :-1, :]], axis=1)
            xr = mu_r * x + (1.0 - mu_r) * x_prev
            xk = mu_k * x + (1.0 - mu_k) * x_prev
            r = jax.nn.sigmoid(jnp.einsum('btc,dc->btd', xr, W_r))
            k = jnp.einsum('btc,dc->btd', xk, W_k)
            k_act = jnp.square(jax.nn.relu(k))
            out = r * jnp.einsum('btc,dc->btd', k_act, W_v)
            new_state = x[:, -1, :]
            return (out, new_state)
        key = jax.random.key(seed)
        ks = jax.random.split(key, 6)
        B, T, C = (8, 256, DIM)
        x = jax.random.normal(ks[0], (B, T, C), dtype=jnp.float32)
        s = 1.0 / np.sqrt(C)
        W_r = jax.random.uniform(ks[1], (C, C), jnp.float32, -s, s)
        W_k = jax.random.uniform(ks[2], (C, C), jnp.float32, -s, s)
        W_v = jax.random.uniform(ks[3], (C, C), jnp.float32, -s, s)
        mu_r = jax.random.uniform(ks[4], (C,), jnp.float32)
        mu_k = jax.random.uniform(ks[5], (C,), jnp.float32)
        return {'x': x, 'W_r': W_r, 'W_k': W_k, 'W_v': W_v, 'mu_r': mu_r, 'mu_k': mu_k}
    _L0_ffn_in = _L0_ffn_setup()

    def _L1_attn_setup():
        import jax, jax.numpy as jnp
        import numpy as np
        import math
        B, T, C = (4, 256, 128)
        H, DQK, DV = (16, 64, 64)
        key = jax.random.key(seed)
        k1, k2, k3, k4, k5 = jax.random.split(key, 5)
        x_q = jax.random.normal(k1, (B, T, C), dtype=jnp.float32)
        w_q = jax.random.normal(k2, (H, DQK, C), dtype=jnp.float32) / math.sqrt(C)
        w_k = jax.random.normal(k3, (H, DQK, C), dtype=jnp.float32) / math.sqrt(C)
        w_v = jax.random.normal(k4, (H, DV, C), dtype=jnp.float32) / math.sqrt(C)
        w_o = jax.random.normal(k5, (DV * H, C), dtype=jnp.float32) / math.sqrt(C)
        return {'x_q': x_q, 'w_q': w_q, 'w_k': w_k, 'w_v': w_v, 'w_o': w_o}
    _L1_attn_in = _L1_attn_setup()

    def _L1_ffn_setup():
        import jax, jax.numpy as jnp
        import numpy as np
        B, S, H, F, G = (8, 256, 128, 512, 128)
        EPS = 1e-05

        def _dequant(q, scales, g):
            K, N = q.shape
            w = (q.astype(jnp.float32) - 128.0).reshape(K // g, g, N) * scales[:, None, :]
            return w.reshape(K, N)
        key = jax.random.key(seed)
        ks = jax.random.split(key, 8)
        x = jax.random.normal(ks[0], (B, S, H), dtype=jnp.float32)
        ln_gamma = jnp.ones((H,), jnp.float32)
        ln_beta = jnp.zeros((H,), jnp.float32)
        fc1_q = jax.random.randint(ks[1], (H, F), 0, 32, dtype=jnp.int32)
        fc2_q = jax.random.randint(ks[2], (F, H), 0, 32, dtype=jnp.int32)
        fc1_scales = jax.random.uniform(ks[3], (H // G, F), jnp.float32) * 0.02 + 0.001
        fc2_scales = jax.random.uniform(ks[4], (F // G, H), jnp.float32) * 0.02 + 0.001
        fc1_bias = jax.random.normal(ks[5], (F,), jnp.float32) * 0.02
        fc2_bias = jax.random.normal(ks[6], (H,), jnp.float32) * 0.02
        return {'x': x, 'ln_gamma': ln_gamma, 'ln_beta': ln_beta, 'fc1_q': fc1_q, 'fc1_scales': fc1_scales, 'fc1_bias': fc1_bias, 'fc2_q': fc2_q, 'fc2_scales': fc2_scales, 'fc2_bias': fc2_bias}
    _L1_ffn_in = _L1_ffn_setup()

    def _L2_attn_setup():
        import jax, jax.numpy as jnp
        import numpy as np
        NUM_HEADS = 16
        key = jax.random.key(seed)
        ks = jax.random.split(key, 5)
        B, N, C = (2, 256, 128)
        x = jax.random.normal(ks[0], (B, N, C), dtype=jnp.float32)
        s_in = 1.0 / np.sqrt(C)
        Wq = jax.random.normal(ks[1], (C, 2 * C), dtype=jnp.float32) * s_in
        Wk = jax.random.normal(ks[2], (C, 2 * C), dtype=jnp.float32) * s_in
        Wv = jax.random.normal(ks[3], (C, 2 * C), dtype=jnp.float32) * s_in
        Wo = jax.random.normal(ks[4], (2 * C, C), dtype=jnp.float32) * (1.0 / np.sqrt(2 * C))
        return {'x': x, 'Wq': Wq, 'Wk': Wk, 'Wv': Wv, 'Wo': Wo}
    _L2_attn_in = _L2_attn_setup()

    def _L2_ffn_setup():
        import jax, jax.numpy as jnp
        import numpy as np
        D_IN, D_HID = (128, 512)

        def _ternary(key, shape):
            return jax.random.randint(key, shape, -1, 2).astype(jnp.float32)

        def _tlin(x, w, s):
            return jnp.einsum('bsi,oi->bso', x, w) * s
        key = jax.random.key(seed)
        ks = jax.random.split(key, 12)
        inv = lambda fan: 1.0 / np.sqrt(fan).astype(np.float32)
        return {'x': jax.random.normal(ks[0], (4, 256, D_IN), dtype=jnp.float32), 'w1_w': _ternary(ks[1], (D_HID, D_IN)), 'w1_s': jax.random.uniform(ks[2], (D_HID,), dtype=jnp.float32) * inv(D_IN), 'w2_w': _ternary(ks[3], (D_HID, D_IN)), 'w2_s': jax.random.uniform(ks[4], (D_HID,), dtype=jnp.float32) * inv(D_IN), 'h1_w': _ternary(ks[5], (D_HID, D_HID)), 'h1_s': jax.random.uniform(ks[6], (D_HID,), dtype=jnp.float32) * inv(D_HID), 'h2_w': _ternary(ks[7], (D_HID, D_HID)), 'h2_s': jax.random.uniform(ks[8], (D_HID,), dtype=jnp.float32) * inv(D_HID), 'w3_w': _ternary(ks[9], (D_IN, D_HID)), 'w3_s': jax.random.uniform(ks[10], (D_IN,), dtype=jnp.float32) * inv(D_HID)}
    _L2_ffn_in = _L2_ffn_setup()

    def _L3_attn_setup():
        import jax, jax.numpy as jnp
        import numpy as np
        import math
        B, T, D = (4, 512, 128)
        H, DK, DV, C = (8, 128, 128, 64)

        def _rms_norm(x, eps=1e-06):
            return x * jax.lax.rsqrt(jnp.mean(x * x, axis=-1, keepdims=True) + eps)
        key = jax.random.key(seed)
        ks = jax.random.split(key, 7)
        s = 0.02
        return {'x': jax.random.normal(ks[0], (B, T, D), jnp.float32), 'Wq': jax.random.normal(ks[1], (H * DK, D), jnp.float32) * s, 'Wk': jax.random.normal(ks[2], (H * DK, D), jnp.float32) * s, 'Wv': jax.random.normal(ks[3], (H * DV, D), jnp.float32) * s, 'Wg': jax.random.normal(ks[4], (H, D), jnp.float32) * s, 'bg': jnp.full((H,), 3.0, jnp.float32), 'Wo': jax.random.normal(ks[5], (D, H * DV), jnp.float32) * s, 'qk_gain': jnp.asarray(4.0, jnp.float32)}
    _L3_attn_in = _L3_attn_setup()

    def _L3_ffn_setup():
        import jax, jax.numpy as jnp
        import numpy as np

        def _bitlinear(x, w_latent):
            scale = jax.lax.stop_gradient(jnp.clip(jnp.mean(jnp.abs(w_latent), axis=1, keepdims=True), 1e-05, None))
            tern = jnp.clip(jnp.round(w_latent / scale), -1.0, 1.0)
            w = w_latent + jax.lax.stop_gradient(tern - w_latent)
            return x @ (w * scale).T
        key = jax.random.key(seed)
        ks = jax.random.split(key, 6)
        dim, hidden, rank = (128, 512, 16)
        B, S = (4, 512)
        x = jax.random.normal(ks[0], (B, S, dim), dtype=jnp.float32)
        w_fc = 0.02 * jax.random.normal(ks[1], (hidden, dim), dtype=jnp.float32)
        w_proj = 0.02 * jax.random.normal(ks[2], (dim, hidden), dtype=jnp.float32)
        u = 0.02 * jax.random.normal(ks[3], (hidden, rank), dtype=jnp.float32)
        v = 0.02 * jax.random.normal(ks[4], (rank, dim), dtype=jnp.float32)
        fast_b = jax.random.normal(ks[5], (rank, rank), dtype=jnp.float32)
        gate = jnp.float32(0.05)
        return {'x': x, 'fast_b': fast_b, 'w_fc': w_fc, 'w_proj': w_proj, 'u': u, 'v': v, 'gate': gate}
    _L3_ffn_in = _L3_ffn_setup()
    _d = {'L0_attn_x': _L0_attn_in['x'], 'L0_attn_Wq': _L0_attn_in['Wq'], 'L0_attn_bq': _L0_attn_in['bq'], 'L0_attn_Wk': _L0_attn_in['Wk'], 'L0_attn_bk': _L0_attn_in['bk'], 'L0_attn_Wv': _L0_attn_in['Wv'], 'L0_attn_bv': _L0_attn_in['bv'], 'L0_attn_Wo': _L0_attn_in['Wo'], 'L0_attn_bo': _L0_attn_in['bo'], 'L0_ffn_W_r': _L0_ffn_in['W_r'], 'L0_ffn_W_k': _L0_ffn_in['W_k'], 'L0_ffn_W_v': _L0_ffn_in['W_v'], 'L0_ffn_mu_r': _L0_ffn_in['mu_r'], 'L0_ffn_mu_k': _L0_ffn_in['mu_k'], 'L1_attn_w_q': _L1_attn_in['w_q'], 'L1_attn_w_k': _L1_attn_in['w_k'], 'L1_attn_w_v': _L1_attn_in['w_v'], 'L1_attn_w_o': _L1_attn_in['w_o'], 'L1_ffn_ln_gamma': _L1_ffn_in['ln_gamma'], 'L1_ffn_ln_beta': _L1_ffn_in['ln_beta'], 'L1_ffn_fc1_q': _L1_ffn_in['fc1_q'], 'L1_ffn_fc1_scales': _L1_ffn_in['fc1_scales'], 'L1_ffn_fc1_bias': _L1_ffn_in['fc1_bias'], 'L1_ffn_fc2_q': _L1_ffn_in['fc2_q'], 'L1_ffn_fc2_scales': _L1_ffn_in['fc2_scales'], 'L1_ffn_fc2_bias': _L1_ffn_in['fc2_bias'], 'L2_attn_Wq': _L2_attn_in['Wq'], 'L2_attn_Wk': _L2_attn_in['Wk'], 'L2_attn_Wv': _L2_attn_in['Wv'], 'L2_attn_Wo': _L2_attn_in['Wo'], 'L2_ffn_w1_w': _L2_ffn_in['w1_w'], 'L2_ffn_w1_s': _L2_ffn_in['w1_s'], 'L2_ffn_w2_w': _L2_ffn_in['w2_w'], 'L2_ffn_w2_s': _L2_ffn_in['w2_s'], 'L2_ffn_h1_w': _L2_ffn_in['h1_w'], 'L2_ffn_h1_s': _L2_ffn_in['h1_s'], 'L2_ffn_h2_w': _L2_ffn_in['h2_w'], 'L2_ffn_h2_s': _L2_ffn_in['h2_s'], 'L2_ffn_w3_w': _L2_ffn_in['w3_w'], 'L2_ffn_w3_s': _L2_ffn_in['w3_s'], 'L3_attn_Wq': _L3_attn_in['Wq'], 'L3_attn_Wk': _L3_attn_in['Wk'], 'L3_attn_Wv': _L3_attn_in['Wv'], 'L3_attn_Wg': _L3_attn_in['Wg'], 'L3_attn_bg': _L3_attn_in['bg'], 'L3_attn_Wo': _L3_attn_in['Wo'], 'L3_attn_qk_gain': _L3_attn_in['qk_gain'], 'L3_ffn_fast_b': _L3_ffn_in['fast_b'], 'L3_ffn_w_fc': _L3_ffn_in['w_fc'], 'L3_ffn_w_proj': _L3_ffn_in['w_proj'], 'L3_ffn_u': _L3_ffn_in['u'], 'L3_ffn_v': _L3_ffn_in['v'], 'L3_ffn_gate': _L3_ffn_in['gate']}
    _x0 = _d['L0_attn_x']
    _d['L0_attn_x'] = jax.random.normal(jax.random.fold_in(jax.random.key(seed), 1), (32, 256, 128), dtype=_x0.dtype)
    del _x0
    return _d

def reference(L0_attn_x, L0_attn_Wq, L0_attn_bq, L0_attn_Wk, L0_attn_bk, L0_attn_Wv, L0_attn_bv, L0_attn_Wo, L0_attn_bo, L0_ffn_W_r, L0_ffn_W_k, L0_ffn_W_v, L0_ffn_mu_r, L0_ffn_mu_k, L1_attn_w_q, L1_attn_w_k, L1_attn_w_v, L1_attn_w_o, L1_ffn_ln_gamma, L1_ffn_ln_beta, L1_ffn_fc1_q, L1_ffn_fc1_scales, L1_ffn_fc1_bias, L1_ffn_fc2_q, L1_ffn_fc2_scales, L1_ffn_fc2_bias, L2_attn_Wq, L2_attn_Wk, L2_attn_Wv, L2_attn_Wo, L2_ffn_w1_w, L2_ffn_w1_s, L2_ffn_w2_w, L2_ffn_w2_s, L2_ffn_h1_w, L2_ffn_h1_s, L2_ffn_h2_w, L2_ffn_h2_s, L2_ffn_w3_w, L2_ffn_w3_s, L3_attn_Wq, L3_attn_Wk, L3_attn_Wv, L3_attn_Wg, L3_attn_bg, L3_attn_Wo, L3_attn_qk_gain, L3_ffn_fast_b, L3_ffn_w_fc, L3_ffn_w_proj, L3_ffn_u, L3_ffn_v, L3_ffn_gate):

    def _L0_attn_ref(x, Wq, bq, Wk, bk, Wv, bv, Wo, bo):
        import jax, jax.numpy as jnp
        import numpy as np
        DIM = 128
        NUM_HEADS = 16
        HEAD_DIM = DIM // NUM_HEADS
        B, L = (4, 256)

        def _alibi_bias_causal(seq_len, dtype):
            h = jnp.arange(1, NUM_HEADS + 1, dtype=jnp.float32)
            slopes = jnp.power(2.0, -8.0 * h / NUM_HEADS)
            pos = jnp.arange(seq_len, dtype=jnp.float32)
            rel = jnp.abs(pos[:, None] - pos[None, :])
            bias = -slopes[:, None, None] * rel[None, :, :]
            causal = pos[:, None] >= pos[None, :]
            bias = jnp.where(causal[None, :, :], bias, -jnp.inf)
            return bias.astype(dtype)
        b, l, d = x.shape
        q = (jnp.einsum('bld,ed->ble', x, Wq) + bq).reshape(b, l, NUM_HEADS, HEAD_DIM).transpose(0, 2, 1, 3)
        k = (jnp.einsum('bld,ed->ble', x, Wk) + bk).reshape(b, l, NUM_HEADS, HEAD_DIM).transpose(0, 2, 1, 3)
        v = (jnp.einsum('bld,ed->ble', x, Wv) + bv).reshape(b, l, NUM_HEADS, HEAD_DIM).transpose(0, 2, 1, 3)
        scale = 1.0 / np.sqrt(HEAD_DIM)
        scores = jnp.einsum('bhqd,bhkd->bhqk', q, k) * scale
        scores = scores + _alibi_bias_causal(l, scores.dtype)[None]
        attn = jax.nn.softmax(scores, axis=-1)
        out = jnp.einsum('bhqk,bhkd->bhqd', attn, v)
        out = out.transpose(0, 2, 1, 3).reshape(b, l, d)
        return jnp.einsum('bld,ed->ble', out, Wo) + bo

    def _L0_ffn_ref(x, W_r, W_k, W_v, mu_r, mu_k):
        import jax, jax.numpy as jnp
        import numpy as np
        DIM = 128

        def _reference_tuple_inner(x, W_r, W_k, W_v, mu_r, mu_k):
            B, T, C = x.shape
            x_prev = jnp.concatenate([jnp.zeros((B, 1, C), x.dtype), x[:, :-1, :]], axis=1)
            xr = mu_r * x + (1.0 - mu_r) * x_prev
            xk = mu_k * x + (1.0 - mu_k) * x_prev
            r = jax.nn.sigmoid(jnp.einsum('btc,dc->btd', xr, W_r))
            k = jnp.einsum('btc,dc->btd', xk, W_k)
            k_act = jnp.square(jax.nn.relu(k))
            out = r * jnp.einsum('btc,dc->btd', k_act, W_v)
            new_state = x[:, -1, :]
            return (out, new_state)
        return _reference_tuple_inner(x, W_r, W_k, W_v, mu_r, mu_k)[0]

    def _L1_attn_ref(x_q, w_q, w_k, w_v, w_o):
        import jax, jax.numpy as jnp
        import numpy as np
        import math
        B, T, C = (4, 256, 128)
        H, DQK, DV = (16, 64, 64)
        q = jnp.einsum('ntc,hdc->nhtd', x_q, w_q)
        k = jnp.einsum('ntc,hdc->nhtd', x_q, w_k)
        v = jnp.einsum('ntc,hdc->nhtd', x_q, w_v)
        a = jnp.einsum('nhtd,nhsd->nhts', q, k) / math.sqrt(q.shape[3])
        t = a.shape[2]
        causal_forbidden = jnp.arange(t)[:, None] < jnp.arange(t)[None, :]
        a = jnp.where(causal_forbidden[None, None], -jnp.inf, a)
        a = jax.nn.softmax(a, axis=3)
        y = jnp.einsum('nhts,nhsd->nthd', a, v).reshape(a.shape[0], t, -1)
        return y @ w_o

    def _L1_ffn_ref(x, ln_gamma, ln_beta, fc1_q, fc1_scales, fc1_bias, fc2_q, fc2_scales, fc2_bias):
        import jax, jax.numpy as jnp
        import numpy as np
        B, S, H, F, G = (8, 256, 128, 512, 128)
        EPS = 1e-05

        def _dequant(q, scales, g):
            K, N = q.shape
            w = (q.astype(jnp.float32) - 128.0).reshape(K // g, g, N) * scales[:, None, :]
            return w.reshape(K, N)
        residual = x
        mu = jnp.mean(x, axis=-1, keepdims=True)
        var = jnp.mean(jnp.square(x - mu), axis=-1, keepdims=True)
        h = (x - mu) * jax.lax.rsqrt(var + EPS) * ln_gamma + ln_beta
        hf = h.reshape(-1, H)
        w1 = _dequant(fc1_q, fc1_scales, G)
        y = hf @ w1 + fc1_bias
        y = jax.nn.silu(y)
        w2 = _dequant(fc2_q, fc2_scales, G)
        z = y @ w2 + fc2_bias
        return residual + 0.5 * z.reshape(residual.shape)

    def _L2_attn_ref(x, Wq, Wk, Wv, Wo):
        import jax, jax.numpy as jnp
        import numpy as np
        NUM_HEADS = 16
        B, N, C = x.shape
        H = NUM_HEADS
        hd = C // H

        def proj(W):
            return (x @ W).reshape(B, N, H, 2 * hd).transpose(0, 2, 1, 3)
        q = proj(Wq)
        k = proj(Wk)
        v = proj(Wv)
        q_r, q_i = (q[..., :hd], q[..., hd:])
        k_r, k_i = (k[..., :hd], k[..., hd:])
        v_r, v_i = (v[..., :hd], v[..., hd:])
        scores = (jnp.einsum('bhnd,bhmd->bhnm', q_r, k_r) + jnp.einsum('bhnd,bhmd->bhnm', q_i, k_i)) / jnp.sqrt(jnp.float32(hd))
        causal = jnp.tril(jnp.ones((N, N), dtype=bool))
        scores = jnp.where(causal[None, None], scores, -jnp.inf)
        probs = jax.nn.softmax(scores, axis=-1)
        out_r = jnp.einsum('bhnm,bhmd->bhnd', probs, v_r)
        out_i = jnp.einsum('bhnm,bhmd->bhnd', probs, v_i)
        out = jnp.concatenate([out_r, out_i], axis=-1)
        out = out.transpose(0, 2, 1, 3).reshape(B, N, 2 * C)
        return out @ Wo

    def _L2_ffn_ref(x, w1_w, w1_s, w2_w, w2_s, h1_w, h1_s, h2_w, h2_s, w3_w, w3_s):
        import jax, jax.numpy as jnp
        import numpy as np
        D_IN, D_HID = (128, 512)

        def _ternary(key, shape):
            return jax.random.randint(key, shape, -1, 2).astype(jnp.float32)

        def _tlin(x, w, s):
            return jnp.einsum('bsi,oi->bso', x, w) * s
        h = jax.nn.silu(_tlin(x, w1_w, w1_s)) * _tlin(x, w2_w, w2_s)
        h = jax.nn.gelu(_tlin(h, h1_w, h1_s), approximate=False)
        h = jax.nn.gelu(_tlin(h, h2_w, h2_s), approximate=False)
        return _tlin(h, w3_w, w3_s)

    def _L3_attn_ref(x, Wq, Wk, Wv, Wg, bg, Wo, qk_gain):
        import jax, jax.numpy as jnp
        import numpy as np
        import math
        B, T, D = (4, 512, 128)
        H, DK, DV, C = (8, 128, 128, 64)

        def _rms_norm(x, eps=1e-06):
            return x * jax.lax.rsqrt(jnp.mean(x * x, axis=-1, keepdims=True) + eps)
        Bs, Ts, Ds = x.shape
        pad = (C - Ts % C) % C
        if pad:
            x = jnp.pad(x, ((0, 0), (0, pad), (0, 0)))
        Tp = x.shape[1]
        n = Tp // C
        q = (x @ Wq.T).reshape(Bs, Tp, H, DK).transpose(0, 2, 1, 3)
        k = (x @ Wk.T).reshape(Bs, Tp, H, DK).transpose(0, 2, 1, 3)
        v = (x @ Wv.T).reshape(Bs, Tp, H, DV).transpose(0, 2, 1, 3)
        g = jax.nn.sigmoid(x @ Wg.T + bg).transpose(0, 2, 1)
        q = _rms_norm(q) * qk_gain
        k = _rms_norm(k)
        q = q.reshape(Bs, H, n, C, DK)
        k = k.reshape(Bs, H, n, C, DK)
        v = v.reshape(Bs, H, n, C, DV)
        g = g.reshape(Bs, H, n, C)
        mask = jnp.tril(jnp.ones((C, C), bool))
        scores = jnp.einsum('bhntd,bhnsd->bhnts', q, k) / math.sqrt(DK)
        scores = jnp.where(mask, scores, -jnp.inf)
        attn = jax.nn.softmax(scores, axis=-1)
        y_in = jnp.einsum('bhnts,bhnsd->bhntd', attn, v)
        kv = jnp.einsum('bhntd,bhnte->bhnde', k, v)
        gamma = jnp.exp(jnp.sum(jnp.log(g), axis=-1))
        qs = jnp.moveaxis(q, 2, 0)
        kvs = jnp.moveaxis(kv, 2, 0)
        gs = jnp.moveaxis(gamma, 2, 0)

        def step(state, inp):
            qn, kvn, gn = inp
            yc = jnp.einsum('bhtd,bhde->bhte', qn, state)
            new_state = state * gn[:, :, None, None] + kvn
            return (new_state, yc)
        state0 = jnp.zeros((Bs, H, DK, DV), x.dtype)
        _, ycs = jax.lax.scan(step, state0, (qs, kvs, gs))
        y_cross = jnp.moveaxis(ycs, 0, 2)
        y = (y_in + y_cross).reshape(Bs, H, Tp, DV).transpose(0, 2, 1, 3).reshape(Bs, Tp, H * DV)
        y = y @ Wo.T
        if pad:
            y = y[:, :Ts, :]
        return y

    def _L3_ffn_ref(x, fast_b, w_fc, w_proj, u, v, gate):
        import jax, jax.numpy as jnp
        import numpy as np

        def _bitlinear(x, w_latent):
            scale = jax.lax.stop_gradient(jnp.clip(jnp.mean(jnp.abs(w_latent), axis=1, keepdims=True), 1e-05, None))
            tern = jnp.clip(jnp.round(w_latent / scale), -1.0, 1.0)
            w = w_latent + jax.lax.stop_gradient(tern - w_latent)
            return x @ (w * scale).T
        h = _bitlinear(x, w_fc) + gate * (x @ v.T @ fast_b.T @ u.T)
        r = jnp.maximum(h, 0.0)
        return _bitlinear(r * r, w_proj)
    x = L0_attn_x
    x = _layernorm(x + _L0_attn_ref(x, L0_attn_Wq, L0_attn_bq, L0_attn_Wk, L0_attn_bk, L0_attn_Wv, L0_attn_bv, L0_attn_Wo, L0_attn_bo), axis=-1)
    x = _layernorm(x + _L0_ffn_ref(x, L0_ffn_W_r, L0_ffn_W_k, L0_ffn_W_v, L0_ffn_mu_r, L0_ffn_mu_k), axis=-1)
    x = _layernorm(x + _L1_attn_ref(x, L1_attn_w_q, L1_attn_w_k, L1_attn_w_v, L1_attn_w_o), axis=-1)
    x = _layernorm(x + _L1_ffn_ref(x, L1_ffn_ln_gamma, L1_ffn_ln_beta, L1_ffn_fc1_q, L1_ffn_fc1_scales, L1_ffn_fc1_bias, L1_ffn_fc2_q, L1_ffn_fc2_scales, L1_ffn_fc2_bias), axis=-1)
    x = _layernorm(x + _L2_attn_ref(x, L2_attn_Wq, L2_attn_Wk, L2_attn_Wv, L2_attn_Wo), axis=-1)
    x = _layernorm(x + _L2_ffn_ref(x, L2_ffn_w1_w, L2_ffn_w1_s, L2_ffn_w2_w, L2_ffn_w2_s, L2_ffn_h1_w, L2_ffn_h1_s, L2_ffn_h2_w, L2_ffn_h2_s, L2_ffn_w3_w, L2_ffn_w3_s), axis=-1)
    x = _layernorm(x + _L3_attn_ref(x, L3_attn_Wq, L3_attn_Wk, L3_attn_Wv, L3_attn_Wg, L3_attn_bg, L3_attn_Wo, L3_attn_qk_gain), axis=-1)
    x = _layernorm(x + _L3_ffn_ref(x, L3_ffn_fast_b, L3_ffn_w_fc, L3_ffn_w_proj, L3_ffn_u, L3_ffn_v, L3_ffn_gate), axis=-1)
    return x

_drawn_inputs = setup_inputs


def setup_inputs(seed=0):
    import zlib

    import numpy as np

    out = dict(_drawn_inputs(seed))
    spreads = {'L1_ffn_ln_gamma': (1.0, 0.2), 'L1_ffn_ln_beta': (0.0, 0.1), 'L3_attn_bg': (3.0, 0.6)}
    factors = {'L0_attn_Wq': 8.0,
     'L0_attn_bq': 8.0,
     'L0_attn_Wk': 8.0,
     'L0_attn_bk': 8.0,
     'L1_ffn_fc1_bias': 8.0,
     'L1_ffn_fc2_bias': 8.0,
     'L2_ffn_w1_w': 8.0,
     'L2_ffn_w1_s': 8.0,
     'L2_ffn_w2_w': 8.0,
     'L2_ffn_w2_s': 8.0,
     'L2_ffn_h1_w': 6.878,
     'L2_ffn_h1_s': 8.0,
     'L2_ffn_h2_w': 7.613,
     'L2_ffn_h2_s': 8.0,
     'L2_ffn_w3_w': 8.0,
     'L2_ffn_w3_s': 8.0,
     'L3_attn_Wg': 4.608,
     'L3_ffn_fast_b': 8.0,
     'L3_ffn_w_fc': 7.048,
     'L3_ffn_w_proj': 6.452,
     'L3_ffn_u': 8.0,
     'L3_ffn_v': 8.0}
    for name, (base, spread) in spreads.items():
        noise = np.random.default_rng([zlib.crc32(name.encode()), seed]).standard_normal(out[name].shape)
        drawn = base * np.exp(spread * noise) if base else spread * noise
        out[name] = jnp.asarray(drawn.astype(out[name].dtype))
    for name, factor in factors.items():
        out[name] = (out[name] * factor).astype(out[name].dtype)
    return out
```

```python
import concourse.bass as bass
from concourse import mybir
from contextlib import ExitStack, contextmanager

FP32 = mybir.dt.float32
F32R = mybir.dt.float32r
BF16 = mybir.dt.bfloat16
I32 = mybir.dt.int32
ACT = mybir.ActivationFunctionType
ALU = mybir.AluOpType
AX = mybir.AxisListType

P = 128
BATCHES, SEQ = 32, 256
TOKENS = BATCHES * SEQ
BANK = 512
UNIT = BANK
UNITS = TOKENS // UNIT
HALF = SEQ // 2
EPS = 1e-5
MASKED = -1e30


def live(unit, total):
    return not isinstance(unit, int) or 0 <= unit < total


def hold(eng, sem, count):
    if not isinstance(count, int) or count > 0:
        eng.wait_ge(sem, count)


def sweep(eng, slots, first, loop_from, loop_to, last, step):
    for i in range(first, loop_from):
        for s in range(slots):
            step(i, s)
    with eng.Fori(loop_from, loop_to) as i:
        for s in range(slots):
            step(i, s)
    for i in range(loop_to, last):
        for s in range(slots):
            step(i, s)


class Scope:

    def __init__(self, nc, stack, layer):
        self.nc, self.stack, self.layer = nc, stack, layer
        self.sems = []

    def sb(self, name, shape, dt=FP32):
        return self.stack.enter_context(self.nc.sbuf_tensor(f"{self.layer}_{name}", shape, dt))

    def bank(self, name, banks=1):
        return self.stack.enter_context(self.nc.psum_tensor(f"{self.layer}_{name}", [P, banks * BANK], FP32))

    def sem(self, name):
        handle = self.stack.enter_context(self.nc.semaphore(f"{self.layer}_{name}"))
        self.sems.append(handle)
        return handle

    @contextmanager
    def block(self):
        with self.nc.Block() as block:
            yield block
        numbers = sorted(s.num for s in self.sems)
        with self.nc.Block() as block:
            @block.gpsimd
            def _(pool):
                first = 0
                for n in range(1, len(numbers) + 1):
                    if n == len(numbers) or numbers[n] != numbers[n - 1] + 1:
                        nc_range = range(numbers[first], numbers[n - 1] + 1)
                        pool.sem_clear(nc_range)
                        first = n


def load_and_split(nc, k, block_name, parts):
    loaded, high_ready = k.sem("w_loaded"), k.sem("w_high")
    with k.block() as block:
        @block.sync
        def _(sp):
            for dram, stage, _, _ in parts:
                sp.dma_start(stage, dram).then_inc(loaded, 16)
            sp.wait_ge(loaded, 16 * len(parts))

        @block.vector
        def _(dve):
            dve.wait_ge(loaded, 16 * len(parts))
            n = 0
            for _, stage, high, low in parts:
                if high is None:
                    continue
                nc.vector.tensor_copy(high, stage).then_inc(high_ready, 1)
                n += 1
                if low is not None:
                    dve.wait_ge(high_ready, n)
                    nc.vector.tensor_tensor(low, stage, high.bitcast(FP32), ALU.subtract)


def layer_norm(nc, layer, c, src, dst, eps=0):
    with ExitStack() as stack:
        k = Scope(nc, stack, layer)
        centred = [k.bank(f"centred{i}") for i in range(2)]
        var = [k.bank(f"var{i}") for i in range(2)]
        sq = k.sb("sq", [P, 2, UNIT])
        lnv = k.sb("lnv", [P, UNIT])
        rstd = k.sb("rstd", [P, 2, UNIT])
        centred_done, sq_ready, var_done, ln_ready, rstd_ready, x_ready = (
            k.sem(n) for n in ("centred_done", "sq_ready", "var_done", "ln_ready", "rstd_ready", "x_ready"))
        block = stack.enter_context(k.block())

        def tokens(buf, n):
            return buf[:, bass.ds(n * UNIT, UNIT)]

        @block.tensor
        def _(pe):
            def step(i, s):
                n, b = 2 * i + s, s % 2
                if live(n, UNITS):
                    hold(pe, x_ready, n - 1)
                    nc.tensor.matmul(centred[b][:, :], c.centre[:, :], tokens(src, n),
                                     start=True, stop=True).then_inc(centred_done, 1)
                if live(n - 1, UNITS):
                    hold(pe, sq_ready, n)
                    hold(pe, ln_ready, n - 2)
                    nc.tensor.matmul(var[1 - b][:, :], c.mean[:, :], sq[:, 1 - b, :],
                                     start=True, stop=True).then_inc(var_done, 1)
            sweep(pe, 2, 0, 2, UNITS // 2, UNITS // 2 + 1, step)

        @block.scalar
        def _(act):
            def step(i, s):
                n, b = 2 * i + s, s % 2
                if live(n, UNITS):
                    hold(act, var_done, n - 1)
                    act.wait_ge(centred_done, n + 1)
                    nc.scalar.activation(sq[:, b, :], centred[b][:, :], ACT.Square).then_inc(sq_ready, 1)
                if live(n - 1, UNITS):
                    hold(act, rstd_ready, n - 1)
                    act.wait_ge(var_done, n)
                    nc.scalar.activation(lnv[:, :], var[1 - b][:, :], ACT.Ln, bias=c.eps[:, eps:eps + 1]).then_inc(ln_ready, 1)
                    hold(act, x_ready, n - 2)
                    act.wait_ge(ln_ready, n)
                    nc.scalar.activation(rstd[:, 1 - b, :], lnv[:, :], ACT.Exp, scale=-0.5).then_inc(rstd_ready, 1)
            sweep(act, 2, 0, 2, UNITS // 2, UNITS // 2 + 1, step)

        @block.vector
        def _(dve):
            def step(i, s):
                n, b = 2 * i + s, s % 2
                if live(n - 1, UNITS):
                    dve.wait_ge(rstd_ready, n)
                    nc.vector.tensor_tensor(tokens(dst, n - 1), centred[1 - b][:, :], rstd[:, 1 - b, :],
                                            ALU.mult).then_inc(x_ready, 1)
            sweep(dve, 2, 0, 1, UNITS // 2, UNITS // 2 + 1, step)


class AttentionShape:

    def __init__(self, dim, rows, tiles, events, split, v_width, scale, q_aug, v_slots, o_tiles, low_col=0):
        self.low_col = low_col
        self.dim, self.rows, self.tiles, self.events, self.split = dim, rows, tiles, events, split
        self.v_width, self.scale, self.q_aug, self.v_slots, self.o_tiles = v_width, scale, q_aug, v_slots, o_tiles
        self.max_row = 3 * dim if split else dim
        self.n_tiles = 16 * rows // P
        self.pv_every = 2 if v_width == 32 else 1


HEADS, STEPS = 16, 8


def attention(nc, layer, c, x, w, a):
    NT, T, R, VW = a.n_tiles, a.tiles, a.rows, a.v_width
    NP = 4 if a.pv_every == 2 else 2
    VD = HEADS * a.dim
    with ExitStack() as stack:
        k = Scope(nc, stack, layer)
        wq = [k.sb(f"wq{p}", [P, NT * P], F32R) for p in range(2)]
        wk = [k.sb(f"wk{p}", [P, NT * P], F32R) for p in range(2)]
        wv = [k.sb(f"wv{p}", [P, VD], F32R) for p in range(2)]
        aug_k = k.sb("aug_k", [3, NT * P], F32R)
        aug_q = k.sb("aug_q", [3, NT * P], F32R)
        wo = k.sb("wo", [P, a.o_tiles, P])
        fbias = k.sb("fbias", [P, 1])
        with ExitStack() as staging:
            ks = Scope(nc, staging, layer + "_s")
            sq_, sk_, sv_ = ks.sb("q", [P, NT * P]), ks.sb("k", [P, NT * P]), ks.sb("v", [P, VD])
            saq, sak = ks.sb("aq", [3, NT * P]), ks.sb("ak", [3, NT * P])
            t_aug = ks.sb("t_aug", [3, NT * P], F32R)
            bvp, bo = ks.sb("bvp", [P, 4]), ks.sb("bo", [P, 1])
            parts = [(w["wq"], sq_[:, :], wq[0][:, :], wq[1][:, :]), (w["wk"], sk_[:, :], wk[0][:, :], wk[1][:, :]),
                     (w["wv"], sv_[:, :], wv[0][:, :], wv[1][:, :]), (w["wo"], wo[:, :, :], None, None),
                     (w["aug_k"], sak[:, :], None, None)]
            if a.q_aug:
                parts.append((w["aug_q"], saq[:, :], None, None))
                parts.append((w["bv"], bvp[:, :], None, None))
                parts.append((w["bo"], bo[:, :], None, None))
            load_and_split(nc, ks, "load", parts)
            high, low, summed = ks.sem("aug_high"), ks.sem("aug_low"), ks.sem("bias_summed")
            pb = ks.bank("pb")
            with ks.block() as block:
                @block.vector
                def _(dve):
                    for n, (src, dst) in enumerate([(sak, aug_k)] + [(saq, aug_q)] * a.q_aug):
                        nc.vector.tensor_scalar(t_aug[:, :], src[:, :], c.aug_low[0:3, 0:1], None, ALU.mult).then_inc(high, 1)
                        dve.wait_ge(high, n + 1)
                        nc.vector.tensor_tensor(dst[:, :], src[:, :], t_aug[:, :].bitcast(FP32), ALU.subtract).then_inc(low, 1)
                        dve.wait_ge(low, n + 1)
                    if a.q_aug:
                        dve.wait_ge(summed, 1)
                        nc.vector.tensor_tensor(fbias[:, :], pb[:, 0:1], bo[:, :], ALU.add)
                    else:
                        nc.vector.memset(fbias[:, :], 0.0)

                @block.tensor
                def _(pe):
                    for g in range(4 * a.q_aug):
                        last = nc.tensor.matmul(pb[:, 0:1], wo[:, g, :], bvp[:, g:g + 1], start=g == 0, stop=g == 3)
                        if g == 3:
                            last.then_inc(summed, 1)

        xs = [k.sb(f"xs{p}", [P, SEQ], F32R) for p in range(2)]
        qk = [k.sb(f"qk{i}", [P, T, 2 * SEQ], F32R if a.split else FP32) for i in range(2)]
        t_low = k.sb("t_low", [P, 2 * SEQ], F32R)
        q2 = [k.sb(f"q2{i}", [P, T, SEQ], F32R if a.split else FP32) for i in range(2)]
        mf = k.sb("mf", [P, 2, 2])
        marr = [k.sb(f"marr{i}", [P, 2, T * P], F32R) for i in range(2)]
        pt = k.sb("pt", [P, NP, 2, 3 * HALF])
        vb = k.sb("vb", [P, 2, HEADS, VW])
        rl = k.sb("rl", [P, SEQ])
        ot = k.sb("ot", [P, a.o_tiles, SEQ])

        b_m, b_p = k.bank("b_m"), k.bank("b_p")
        b_s, b_st = k.bank("b_s", 2), k.bank("b_st", 2)
        b_o, b_v = k.bank("b_o"), k.bank("b_v")
        proj_bank = [b_p, b_m]

        (presets, xs_high, xs_ready, proj_done, t_ready, qk_ready, s_done, mf_ready, mh_ready, m_ready, mt_done,
         q2_ready, st_done, p_ready, pv_done, rl_ready, o_ready, v_done, v_ready, f_done, y_ready) = (
            k.sem(n) for n in ("presets", "xs_high", "xs_ready", "proj_done", "t_ready", "qk_ready", "s_done", "mf_ready",
                               "mh_ready", "m_ready", "mt_done", "q2_ready", "st_done", "p_ready", "pv_done",
                               "rl_ready", "o_ready", "v_done", "v_ready", "f_done", "y_ready"))
        block = stack.enter_context(k.block())
        E, F = a.events, STEPS // a.pv_every
        per = STEPS // E
        NV = len(a.v_slots)

        def event(i, s):
            return E * (i + s // STEPS) + (s % STEPS) // per

        def head_rows(s, hh):
            h = 2 * s + hh
            return (h * R // P) % T if T > 1 else 0, h * R % P

        def run(eng, step):
            sweep(eng, STEPS, -1, 2, BATCHES - 1, BATCHES + 1, step)

        STEPS_ALL = BATCHES * STEPS

        def tri(bank):
            return bank.rearrange("p (b t) -> p b t", t=HALF)[:, 0:4:2, :]

        @block.tensor
        def _(pe):
            pe.wait_ge(presets, 3)

            def step(i, s):
                n = STEPS * i + s
                par = s % 2
                ps = (s - 1) % STEPS
                if live(n - 1, STEPS_ALL):
                    hold(pe, m_ready, n)
                    hold(pe, q2_ready, n - 1)
                    if T > 1:
                        hold(pe, qk_ready, event(i, s) + 1 if live(n, STEPS_ALL) else n)
                    for t in range(T):
                        for qb in range(2):
                            last = nc.tensor.matmul(b_m[:, t * SEQ + qb * HALF:t * SEQ + (qb + 1) * HALF],
                                                    marr[1 - par][:, qb, t * P:(t + 1) * P], c.ident_r[:, :],
                                                    start=t == 0 and qb == 0, stop=True, skip_group_check=True)
                    last.then_inc(mt_done, 1)
                if live(n, STEPS_ALL):
                    hold(pe, m_ready, n)
                    hold(pe, t_ready, event(i, s) + 1)
                    hold(pe, qk_ready, event(i, s) + 1)
                    ops = qk[(s // per) % 2]
                    for hh in range(2):
                        t, r = head_rows(s, hh)
                        bank = b_s[:, hh * BANK:(hh + 1) * BANK]
                        nc.tensor.matmul(tri(bank), c.ident_b[:, :], c.mask_q[:, :, :], start=True, stop=True,
                                         skip_group_check=True)
                        nc.tensor.matmul(bank[:, 0:HALF], ops[r:r + R, t, 0:HALF], ops[r:r + R, t, SEQ:SEQ + HALF],
                                         start=False, stop=True, skip_group_check=True)
                        last = nc.tensor.matmul(bank[:, HALF:3 * HALF], ops[r:r + R, t, HALF:SEQ],
                                                ops[r:r + R, t, SEQ:2 * SEQ], start=False, stop=True,
                                                skip_group_check=True)
                    last.then_inc(s_done, 1)
                if live(n - 1, STEPS_ALL):
                    hold(pe, q2_ready, n)
                    hold(pe, p_ready, n - 1)
                    ops = qk[(ps // per) % 2]
                    for hh in range(2):
                        t, r = head_rows(ps, hh)
                        bank = b_st[:, hh * BANK:(hh + 1) * BANK]
                        nc.tensor.matmul(tri(bank), c.ident_b[:, :], c.mask_k[:, :, :], start=True, stop=True,
                                         skip_group_check=True)
                        nc.tensor.matmul(bank[:, 0:SEQ], ops[r:r + R, t, SEQ:SEQ + HALF], q2[1 - par][r:r + R, t, 0:SEQ],
                                         start=False, stop=True, skip_group_check=True)
                        last = nc.tensor.matmul(bank[:, SEQ:3 * HALF], ops[r:r + R, t, SEQ + HALF:2 * SEQ],
                                                q2[1 - par][r:r + R, t, HALF:SEQ], start=False, stop=True,
                                                skip_group_check=True)
                    last.then_inc(st_done, 1)
                s1 = (s + 1) % STEPS
                if live(n + 1, STEPS_ALL) and s1 % per == 0:
                    e1 = event(i, s + 1)
                    hold(pe, xs_ready, i + (2 if s == STEPS - 1 else 1))
                    hold(pe, t_ready, e1)
                    hold(pe, qk_ready, e1)
                    if T > 1:
                        hold(pe, q2_ready, n)
                    for t in range(T):
                        tile = slice(((s1 // per) * T + t) * P, ((s1 // per) * T + t + 1) * P)
                        bank = proj_bank[t]
                        for q, (wt, aug, has_aug) in enumerate(((wq, aug_q, a.q_aug), (wk, aug_k, True))):
                            out = bank[:, q * SEQ:(q + 1) * SEQ]
                            for m, (wi, xi) in enumerate(((0, 0), (0, 1), (1, 0))):
                                last = nc.tensor.matmul(out, wt[wi][:, tile], xs[xi][:, :], start=m == 0 and q == 0,
                                                        stop=m == 2, skip_group_check=True)
                            if has_aug:
                                last = nc.tensor.matmul(out, aug[0:3, tile], c.aug_x[0:3, :], start=False, stop=True,
                                                        skip_group_check=True)
                    last.then_inc(proj_done, 1)
                if live(n - 2, STEPS_ALL) and (s - 1) % a.pv_every == 0:
                    hold(pe, p_ready, n - 1)
                    hold(pe, v_ready, NV * i + sum(v < s for v in a.v_slots) if 1 < s else NV * i)
                    hold(pe, o_ready, F * i + (s - 2) // a.pv_every)
                    heads = []
                    for d in range(a.pv_every - 1, -1, -1):
                        for hh in range(2):
                            sl = s - 2 - d
                            heads.append(((2 * (sl % STEPS) + hh), sl % NP, hh))
                    for kb in range(2):
                        for ones in range(2):
                            for g, (h, buf, hh) in enumerate(heads):
                                rows = slice(g * VW, (g + 1) * VW)
                                cols = slice(ones * SEQ + kb * HALF, (ones + 1) * SEQ)
                                src = slice(kb * SEQ, kb * SEQ + SEQ - kb * HALF)
                                lhs = c.ones[:, 0:VW] if ones else vb[:, kb, h, :]
                                last = nc.tensor.matmul(b_o[rows, cols], lhs, pt[:, buf, hh, src],
                                                        start=kb == 0 and ones == 0, stop=kb == 1,
                                                        skip_group_check=True)
                    last.then_inc(pv_done, 1)
                if s in a.v_slots and live(i, BATCHES):
                    j = a.v_slots.index(s)
                    hold(pe, xs_ready, i + 1)
                    hold(pe, v_ready, NV * i + j)
                    hold(pe, y_ready, i - (s < 2))
                    half, tbs = v_chunk(a, j)
                    width = VD // 2
                    for q, tb in enumerate(tbs):
                        out = b_v[:, q * width:(q + 1) * width]
                        for m, (xi, wi) in enumerate(((0, 0), (1, 0), (0, 1))):
                            last = nc.tensor.matmul(out, xs[xi][:, tb * HALF:(tb + 1) * HALF],
                                                    wv[wi][:, half * width:(half + 1) * width],
                                                    start=m == 0 and q == 0, stop=m == 2, skip_group_check=True)
                    last.then_inc(v_done, 1)
                if s == 2 and live(i - 1, BATCHES):
                    hold(pe, o_ready, F * i)
                    hold(pe, v_ready, NV * i + sum(v < 2 for v in a.v_slots) * live(i, BATCHES))
                    for g in range(a.o_tiles):
                        last = nc.tensor.matmul(b_v[:, 0:SEQ], wo[:, g, :], ot[:, g, :], start=g == 0,
                                                stop=g == a.o_tiles - 1)
                    last.then_inc(f_done, 1)
            run(pe, step)

        @block.gpsimd
        def _(pool):
            for m in marr:
                nc.gpsimd.memset(m[:, :, :].bitcast(FP32), 0.0).then_inc(presets, 1)
            nc.gpsimd.memset(vb[:, :, :, :], 0.0).then_inc(presets, 1)

        @block.scalar
        def _(act):
            act.wait_ge(presets, 3)

            def step(i, s):
                n = STEPS * i + s
                if live(n - 1, STEPS_ALL):
                    hold(act, st_done, n)
                    old = s - 1 - NP
                    hold(act, pv_done, F * i + old // a.pv_every + 1 if not isinstance(n, int) or n - 1 - NP >= 0 else 0)
                    nc.scalar.activation(pt[:, (s - 1) % NP, :, :],
                                         b_st[:, :].rearrange("p (h t) -> p h t", t=BANK)[:, :, 0:3 * HALF],
                                         ACT.Exp, scale=a.scale).then_inc(p_ready, 1)
                s1 = (s + 1) % STEPS
                if live(n + 1, STEPS_ALL) and s1 % per == 0:
                    e1 = event(i, s + 1)
                    hold(act, proj_done, e1 + 1)
                    if a.split:
                        hold(act, qk_ready, e1)
                        nc.scalar.activation(t_low[:, 0:SEQ], b_p[:, 0:SEQ], ACT.Copy, scale=c.low_rows[:, a.low_col:a.low_col + 1])
                        nc.scalar.activation(t_low[:, SEQ:2 * SEQ], b_p[:, SEQ:2 * SEQ], ACT.Copy,
                                             scale=c.low_rows[:, a.low_col + 1:a.low_col + 2]).then_inc(t_ready, 1)
                    else:
                        hold(act, st_done, per * (e1 - 1))
                        nc.scalar.activation(qk[(s1 // per) % 2][:, 0, :], b_p[:, :], ACT.Copy).then_inc(t_ready, 1)
                if s in a.v_slots and live(i, BATCHES):
                    j = a.v_slots.index(s)
                    half, tbs = v_chunk(a, j)
                    act.wait_ge(v_done, NV * i + j + 1)
                    hold(act, pv_done, F * i - (F // 2 if half == 0 else 0) if half == 0 else F * i)
                    width = VD // 2
                    nc.scalar.activation(vb[:, tbs[0]:tbs[-1] + 1, half * 8:half * 8 + 8, 0:a.dim],
                                         b_v[:, 0:len(tbs) * width].rearrange("p (b h d) -> p b h d", h=8, d=a.dim),
                                         ACT.Copy).then_inc(v_ready, 1)
            run(act, step)

        @block.vector
        def _(dve):
            dve.wait_ge(presets, 3)

            def step(i, s):
                n = STEPS * i + s
                par = s % 2
                if live(n - 1, STEPS_ALL):
                    ps = (s - 1) % STEPS
                    hold(dve, mt_done, n)
                    hold(dve, st_done, n - 2)
                    q_part = qk[(ps // per) % 2][:, :, 0:SEQ]
                    nc.vector.tensor_tensor(q2[1 - par][:, :, :], b_m[:, 0:T * SEQ].rearrange("p (t q) -> p t q", q=SEQ),
                                            q_part.bitcast(FP32) if a.split else q_part, ALU.add).then_inc(q2_ready, 1)
                if live(n, STEPS_ALL):
                    banks = b_s[:, :].rearrange("p (h t) -> p h t", t=BANK)
                    dve.wait_ge(s_done, n + 1)
                    hold(dve, m_ready, n)
                    nc.vector.tensor_reduce(mf[:, 0, :], banks[:, :, 0:HALF], AX.X, ALU.max, negate=True).then_inc(mf_ready, 1)
                    nc.vector.tensor_reduce(mf[:, 1, :], banks[:, :, HALF:3 * HALF], AX.X, ALU.max, negate=True).then_inc(mf_ready, 1)
                    t0, r0 = head_rows(s, 0)
                    t1, r1 = head_rows(s, 1)
                    stride = (t1 * P + r1) - (t0 * P + r0)
                    lo_col = t0 * P + r0 + a.max_row
                    high = marr[par][:, :, lo_col:lo_col + stride + 1:stride]
                    low = marr[par][:, :, lo_col + 1:lo_col + 2 + stride:stride]
                    hold(dve, mt_done, n - 1)
                    dve.wait_ge(mf_ready, 2 * n + 2)
                    nc.vector.tensor_copy(high, mf[:, :, :]).then_inc(mh_ready, 1)
                    dve.wait_ge(mh_ready, n + 1)
                    nc.vector.tensor_tensor(low, mf[:, :, :], high.bitcast(FP32), ALU.subtract).then_inc(m_ready, 1)
                if s == STEPS - 1 and live(i + 1, BATCHES):
                    hold(dve, proj_done, E * (i + 1))
                    hold(dve, v_done, NV * (i + 1))
                    xb = x[:, bass.ds((i + 1) * SEQ, SEQ)]
                    nc.vector.tensor_scalar(xs[0][:, :], xb, 1.0, None, ALU.mult).then_inc(xs_high, 1)
                    hold(dve, xs_high, i + 2)
                    nc.vector.tensor_tensor(xs[1][:, :], xb, xs[0][:, :].bitcast(FP32), ALU.subtract).then_inc(xs_ready, 1)
                s1 = (s + 1) % STEPS
                if live(n + 1, STEPS_ALL) and s1 % per == 0:
                    e1 = event(i, s + 1)
                    ops = qk[(s1 // per) % 2]
                    hold(dve, st_done, per * (e1 - 1))
                    if a.split:
                        dve.wait_ge(t_ready, e1 + 1)
                        nc.vector.tensor_tensor(ops[:, 0, :], b_p[:, :], t_low[:, :].bitcast(FP32),
                                                ALU.subtract).then_inc(qk_ready, 1)
                    else:
                        hold(dve, proj_done, e1 + 1)
                        nc.vector.tensor_copy(ops[:, 1, :], b_m[:, :]).then_inc(qk_ready, 1)
                if live(n - 2, STEPS_ALL) and (s - 1) % a.pv_every == 0:
                    f = F * i + (s - 2) // a.pv_every
                    g = ((s - 2) % STEPS) // a.pv_every
                    hold(dve, pv_done, f + 1)
                    hold(dve, f_done, i - (s < 2))
                    nc.vector.reciprocal(rl[:, :], b_o[:, SEQ:2 * SEQ]).then_inc(rl_ready, 1)
                    hold(dve, rl_ready, f + 1)
                    nc.vector.tensor_tensor(ot[:, g, :], b_o[:, 0:SEQ], rl[:, :], ALU.mult).then_inc(o_ready, 1)
                if s == 2 and live(i - 1, BATCHES):
                    hold(dve, f_done, i)
                    xb = x[:, bass.ds((i - 1) * SEQ, SEQ)]
                    nc.vector.scalar_tensor_tensor(xb, b_v[:, 0:SEQ], fbias[:, 0:1], xb, ALU.add, ALU.add)\
                        .then_inc(y_ready, 1)
            run(dve, step)


def v_chunk(a, j):
    if len(a.v_slots) == 2:
        return j, (0, 1)
    return j // 2, (j % 2,)


def reglu(nc, layer, c, x, w):
    with ExitStack() as stack:
        k = Scope(nc, stack, layer)
        wm = k.sb("wm", [P, 2, 2, 2, P], F32R)
        wv = k.sb("wv", [P, P])
        with ExitStack() as staging:
            ks = Scope(nc, staging, layer + "_s")
            raw, mu = ks.sb("raw", [P, 2, P]), ks.sb("mu", [P, 2])
            rest, mixed = ks.sb("rest", [P, 2]), ks.sb("mixed", [P, 2, 2, P])
            loaded, rest_ready, mixed_ready, high_ready = (
                ks.sem(n) for n in ("loaded", "rest_ready", "mixed_ready", "high_ready"))
            with ks.block() as block:
                @block.sync
                def _(sp):
                    for dst, src in ((raw[:, :, :], w["w"]), (mu[:, :], w["mu"]), (wv[:, :], w["wv"])):
                        sp.dma_start(dst, src).then_inc(loaded, 16)

                @block.vector
                def _(dve):
                    dve.wait_ge(loaded, 48)
                    nc.vector.tensor_scalar(rest[:, :], mu[:, :], -1.0, 1.0, ALU.mult, ALU.add).then_inc(rest_ready, 1)
                    dve.wait_ge(rest_ready, 1)
                    for m in range(2):
                        for t, share in enumerate((mu, rest)):
                            nc.vector.tensor_scalar(mixed[:, m, t, :], raw[:, m, :], share[:, m:m + 1], None,
                                                    ALU.mult).then_inc(mixed_ready, 1)
                    dve.wait_ge(mixed_ready, 4)
                    nc.vector.tensor_copy(wm[:, :, :, 0, :], mixed[:, :, :, :]).then_inc(high_ready, 1)
                    dve.wait_ge(high_ready, 1)
                    nc.vector.tensor_tensor(wm[:, :, :, 1, :], mixed[:, :, :, :], wm[:, :, :, 0, :].bitcast(FP32), ALU.subtract)

        xs = [[k.sb(f"xs{b}{p}", [P, 2, SEQ + 1], F32R) for p in range(2)] for b in range(2)]
        kr = k.sb("kr", [P, UNIT])
        kk = [k.sb(f"kk{b}", [P, UNIT]) for b in range(2)]
        sg = [k.sb(f"sg{b}", [P, UNIT]) for b in range(2)]
        gated = k.sb("gated", [P, UNIT])
        b_k, b_r, b_v = k.bank("b_k"), k.bank("b_r"), k.bank("b_v")
        presets, xs_high, xs_ready, k_done, r_done, kr_ready, kk_ready, sg_ready, v_done, gated_ready, y_ready = (
            k.sem(n) for n in ("presets", "xs_high", "xs_ready", "k_done", "r_done", "kr_ready", "kk_ready", "sg_ready",
                               "v_done", "gated_ready", "y_ready"))
        block = stack.enter_context(k.block())

        def run(eng, step):
            sweep(eng, 2, -1, 2, UNITS // 2 - 1, UNITS // 2 + 1, step)

        @block.gpsimd
        def _(pool):
            for b in range(2):
                for p in range(2):
                    nc.gpsimd.memset(xs[b][p][:, :, 0:1].bitcast(FP32), 0.0).then_inc(presets, 1)

        @block.tensor
        def _(pe):
            pe.wait_ge(presets, 4)

            def step(i, s):
                n, b = 2 * i + s, s % 2
                if live(n, UNITS):
                    hold(pe, xs_ready, n + 1)
                    for m, bank, done in ((1, b_k, k_done), (0, b_r, r_done)):
                        hold(pe, kk_ready if m else sg_ready, n)
                        q = 0
                        for t, off in ((0, 1), (1, 0)):
                            for wi, xi in ((0, 0), (0, 1), (1, 0)):
                                last = nc.tensor.matmul(bank[:, :], wm[:, m, t, wi, :], xs[b][xi][:, :, off:off + SEQ],
                                                        start=q == 0, stop=q == 5)
                                q += 1
                        last.then_inc(done, 1)
                if live(n - 1, UNITS):
                    hold(pe, kk_ready, n)
                    hold(pe, gated_ready, n - 1)
                    nc.tensor.matmul(b_v[:, :], wv[:, :], kk[1 - b][:, :], start=True, stop=True).then_inc(v_done, 1)
            run(pe, step)

        @block.scalar
        def _(act):
            def step(i, s):
                n, b = 2 * i + s, s % 2
                if live(n, UNITS):
                    hold(act, k_done, n + 1)
                    hold(act, kk_ready, n)
                    nc.scalar.activation(kr[:, :], b_k[:, :], ACT.Relu).then_inc(kr_ready, 1)
                    hold(act, r_done, n + 1)
                    hold(act, gated_ready, n - 1)
                    nc.scalar.activation(sg[b][:, :], b_r[:, :], ACT.Sigmoid).then_inc(sg_ready, 1)
            run(act, step)

        @block.vector
        def _(dve):
            def step(i, s):
                n, b = 2 * i + s, s % 2
                if live(n + 1, UNITS):
                    hold(dve, r_done, n)
                    xb = x[:, bass.ds((n + 1) * UNIT, UNIT)].rearrange("p (b t) -> p b t", t=SEQ)
                    high, low = xs[1 - b][0][:, :, 1:SEQ + 1], xs[1 - b][1][:, :, 1:SEQ + 1]
                    nc.vector.tensor_scalar(high, xb, 1.0, None, ALU.mult).then_inc(xs_high, 1)
                    hold(dve, xs_high, n + 2)
                    nc.vector.tensor_tensor(low, xb, high.bitcast(FP32), ALU.subtract).then_inc(xs_ready, 1)
                if live(n, UNITS):
                    hold(dve, kr_ready, n + 1)
                    hold(dve, v_done, n - 1)
                    nc.vector.tensor_tensor(kk[b][:, :], b_k[:, :], kr[:, :], ALU.mult).then_inc(kk_ready, 1)
                if live(n - 1, UNITS):
                    hold(dve, sg_ready, n)
                    hold(dve, v_done, n)
                    hold(dve, y_ready, n - 1)
                    nc.vector.tensor_tensor(gated[:, :], b_v[:, :], sg[1 - b][:, :], ALU.mult).then_inc(gated_ready, 1)
                    hold(dve, gated_ready, n)
                    xb = x[:, bass.ds((n - 1) * UNIT, UNIT)]
                    nc.vector.tensor_tensor(xb, gated[:, :], xb, ALU.add).then_inc(y_ready, 1)
            run(dve, step)


def mlp(nc, layer, c, src, x, w1, w2, kind, b1, out_scale, out_bias):
    M = 4
    with ExitStack() as stack:
        k = Scope(nc, stack, layer)
        xs = [[k.sb(f"xs{b}{p}", [P, UNIT], F32R) for p in range(2)] for b in range(2)]
        hid = k.sb("hid", [P, M, UNIT])
        relu = k.sb("relu", [P, 2, UNIT])
        b_h = [k.bank(f"b_h{m}") for m in range(M)]
        b_z = [k.bank(f"b_z{m}") for m in range(2)]
        xs_high, xs_ready, h_done, relu_ready, hid_ready, z_done, y_ready = (
            k.sem(n) for n in ("xs_high", "xs_ready", "h_done", "relu_ready", "hid_ready", "z_done", "y_ready"))
        block = stack.enter_context(k.block())

        def run(eng, step):
            sweep(eng, 2, -1, 2, UNITS // 2 - 1, UNITS // 2 + 1, step)

        @block.tensor
        def _(pe):
            def step(i, s):
                n, b = 2 * i + s, s % 2
                if live(n - 1, UNITS):
                    hold(pe, y_ready, n - 2)
                    for m in range(M):
                        hold(pe, hid_ready, M * (n - 1) + m + 1)
                        last = nc.tensor.matmul(b_z[1 - b][:, :], w2[:, m, :], hid[:, m, :], start=m == 0, stop=m == M - 1)
                    last.then_inc(z_done, 1)
                if live(n, UNITS):
                    hold(pe, xs_ready, n + 1)
                    for m in range(M):
                        hold(pe, hid_ready, M * (n - 1) + m + 1)
                        for q, (wi, xi) in enumerate(((0, 0), (0, 1), (1, 0))):
                            last = nc.tensor.matmul(b_h[m][:, :], w1[wi][:, m * P:(m + 1) * P], xs[b][xi][:, :],
                                                    start=q == 0, stop=q == 2)
                        last.then_inc(h_done, 1)
            run(pe, step)

        @block.scalar
        def _(act):
            def step(i, s):
                n, b = 2 * i + s, s % 2
                if live(n, UNITS):
                    for m in range(M):
                        hold(act, h_done, M * n + m + 1)
                        if kind == "silu":
                            hold(act, z_done, n)
                            nc.scalar.activation(hid[:, m, :], b_h[m][:, :], ACT.Silu, bias=b1[:, m:m + 1])\
                                .then_inc(hid_ready, 1)
                        else:
                            hold(act, hid_ready, M * n + m - 1)
                            nc.scalar.activation(relu[:, m % 2, :], b_h[m][:, :], ACT.Relu).then_inc(relu_ready, 1)
            run(act, step)

        @block.vector
        def _(dve):
            def step(i, s):
                n, b = 2 * i + s, s % 2
                if live(n + 1, UNITS):
                    hold(dve, h_done, M * n)
                    xb = src[:, bass.ds((n + 1) * UNIT, UNIT)]
                    nc.vector.tensor_scalar(xs[1 - b][0][:, :], xb, 1.0, None, ALU.mult).then_inc(xs_high, 1)
                    hold(dve, xs_high, n + 2)
                    nc.vector.tensor_tensor(xs[1 - b][1][:, :], xb, xs[1 - b][0][:, :].bitcast(FP32),
                                            ALU.subtract).then_inc(xs_ready, 1)
                if live(n - 1, UNITS):
                    hold(dve, z_done, n)
                    xb = x[:, bass.ds((n - 1) * UNIT, UNIT)]
                    if out_bias is None:
                        nc.vector.scalar_tensor_tensor(xb, b_z[1 - b][:, :], out_scale[:, 0:1], xb, ALU.mult, ALU.add)\
                            .then_inc(y_ready, 1)
                    else:
                        nc.vector.scalar_tensor_tensor(xb, b_z[1 - b][:, :], out_bias[:, 0:1], xb, ALU.add, ALU.add)\
                            .then_inc(y_ready, 1)
                if live(n, UNITS) and kind == "relu2":
                    for m in range(M):
                        hold(dve, relu_ready, M * n + m + 1)
                        hold(dve, z_done, n)
                        nc.vector.tensor_tensor(hid[:, m, :], b_h[m][:, :], relu[:, m % 2, :], ALU.mult)\
                            .then_inc(hid_ready, 1)
            run(dve, step)


def quantised_mlp(nc, c, x, w):
    layer = "l1f"
    with ExitStack() as stack:
        k = Scope(nc, stack, layer)
        w1 = [k.sb(f"w1{p}", [P, 4 * P], F32R) for p in range(2)]
        w2 = k.sb("w2", [P, 4, P])
        b1, b2 = k.sb("b1", [P, 4]), k.sb("b2", [P, 1])
        with ExitStack() as staging:
            ks = Scope(nc, staging, layer + "_s")
            q1, q2 = ks.sb("q1", [P, 4 * P], I32), ks.sb("q2", [P, 4, P], I32)
            s1, s2 = ks.sb("s1", [P, 4 * P]), ks.sb("s2", [P, 4, P])
            b1_raw, gamma, beta, b2_raw = ks.sb("b1r", [P, 4]), ks.sb("gamma", [P, 1]), ks.sb("beta", [P, 1]), ks.sb("b2r", [P, 1])
            d1, d2, full = ks.sb("d1", [P, 4 * P]), ks.sb("d2", [P, 4, P]), ks.sb("full", [P, 4 * P])
            pb = ks.bank("pb")
            loaded, chain, beta_done = ks.sem("loaded"), ks.sem("dequantised"), ks.sem("beta_done")
            pairs = ((q1[:, :], "fc1_q"), (q2[:, :, :], "fc2_q"), (s1[:, :], "fc1_s"), (s2[:, :, :], "fc2_s"),
                     (b1_raw[:, :], "b1"), (gamma[:, :], "gamma"), (beta[:, :], "beta"), (b2_raw[:, :], "b2"))
            with ks.block() as block:
                @block.sync
                def _(sp):
                    for dst, name in pairs:
                        sp.dma_start(dst, w[name]).then_inc(loaded, 16)

                @block.vector
                def _(dve):
                    dve.wait_ge(loaded, 16 * len(pairs))
                    nc.vector.tensor_scalar(d1[:, :], q1[:, :], -128.0, None, ALU.add).then_inc(chain, 1)
                    nc.vector.tensor_scalar(d2[:, :, :], q2[:, :, :], -128.0, 0.25, ALU.add, ALU.mult).then_inc(chain, 1)
                    nc.vector.tensor_scalar(b2[:, :], b2_raw[:, :], 0.25, None, ALU.mult)
                    dve.wait_ge(chain, 2)
                    nc.vector.tensor_tensor(full[:, :], d1[:, :], s1[:, :], ALU.mult).then_inc(chain, 1)
                    nc.vector.tensor_tensor(w2[:, :, :], d2[:, :, :], s2[:, :, :], ALU.mult)
                    dve.wait_ge(chain, 3)
                    nc.vector.tensor_scalar(s1[:, :], full[:, :], gamma[:, 0:1], None, ALU.mult).then_inc(chain, 1)
                    dve.wait_ge(chain, 4)
                    nc.vector.tensor_copy(w1[0][:, :], s1[:, :]).then_inc(chain, 1)
                    dve.wait_ge(chain, 5)
                    nc.vector.tensor_tensor(w1[1][:, :], s1[:, :], w1[0][:, :].bitcast(FP32), ALU.subtract)
                    dve.wait_ge(beta_done, 1)
                    nc.vector.tensor_tensor(b1[:, :], pb[:, 0:4], b1_raw[:, :], ALU.add)

                @block.tensor
                def _(pe):
                    pe.wait_ge(chain, 3)
                    for m in range(4):
                        last = nc.tensor.matmul(pb[:, m:m + 1], full[:, m * P:(m + 1) * P], beta[:, 0:1], start=m == 0,
                                                stop=True, skip_group_check=True)
                    last.then_inc(beta_done, 1)
        h = k.sb("h", [P, TOKENS])
        layer_norm(nc, layer + "n", c, x, h)
        mlp(nc, layer, c, h, x, w1, w2, "silu", b1, None, b2)


ROUND = 1.5 * 2.0 ** 23


def ternary_mlp(nc, c, x, w):
    layer = "l3f"
    with ExitStack() as stack:
        k = Scope(nc, stack, layer)
        w1 = [k.sb(f"w1{p}", [P, 4 * P], F32R) for p in range(2)]
        w2 = k.sb("w2", [P, 4, P])
        scale2 = k.sb("scale2", [P, 1])
        with ExitStack() as staging:
            ks = Scope(nc, staging, layer + "_s")
            fc, proj = ks.sb("fc", [P, 4 * P]), ks.sb("proj", [P, 4 * P])
            size_fc, size_proj = ks.sb("size_fc", [P, 4 * P]), ks.sb("size_proj", [P, 4 * P])
            scale, inverse = ks.sb("scale", [P, 5 * P]), ks.sb("inverse", [P, 5 * P])
            r1, r2, low_rank = ks.sb("r1", [P, 4 * P]), ks.sb("r2", [P, 4 * P]), ks.sb("low_rank", [P, 4 * P])
            bt, v, ut, bv = ks.sb("bt", [16, 16]), ks.sb("v", [16, P]), ks.sb("ut", [16, 4 * P]), ks.sb("bv", [16, P])
            gate = ks.sb("gate", [P, 1])
            b_fc, b_proj, b_col, b_bv, b_low = (ks.bank("b_" + n) for n in ("fc", "proj", "col", "bv", "low"))
            loaded, sizes, means, bv_done, bv_ready, low_done, chain = (
                ks.sem("s_" + n) for n in ("loaded", "sizes", "means", "bv_done", "bv_ready", "low_done", "rounded"))
            pairs = ((fc[:, :], "w_fc"), (proj[:, :], "w_proj"), (bt[:, :], "bt"), (v[:, :], "v"), (ut[:, :], "ut"),
                     (gate[:, :], "gate"))
            with ks.block() as block:
                @block.sync
                def _(sp):
                    for dst, name in pairs:
                        sp.dma_start(dst, w[name]).then_inc(loaded, 16)

                @block.scalar
                def _(act):
                    act.wait_ge(loaded, 16 * len(pairs))
                    nc.scalar.activation(size_fc[:, :], fc[:, :], ACT.Abs).then_inc(sizes, 1)
                    nc.scalar.activation(size_proj[:, :], proj[:, :], ACT.Abs).then_inc(sizes, 1)

                @block.tensor
                def _(pe):
                    pe.wait_ge(loaded, 16 * len(pairs))
                    nc.tensor.matmul(b_bv[0:16, 0:P], bt[:, :], v[:, :], start=True, stop=True).then_inc(bv_done, 1)
                    pe.wait_ge(sizes, 2)
                    nc.tensor.matmul(b_fc[:, :], c.mean[:, :], size_fc[:, :], start=True, stop=True).then_inc(means, 1)
                    for m in range(4):
                        last = nc.tensor.matmul(b_proj[:, 0:P], c.mean[:, :], size_proj[:, m * P:(m + 1) * P],
                                                start=m == 0, stop=m == 3)
                    last.then_inc(means, 1)
                    for m in range(4):
                        last = nc.tensor.matmul(b_col[:, 0:1], size_proj[:, m * P:(m + 1) * P], c.mean[:, 0:1],
                                                start=m == 0, stop=m == 3)
                    last.then_inc(means, 1)
                    pe.wait_ge(bv_ready, 1)
                    nc.tensor.matmul(b_low[:, :], bv[:, :], ut[:, :], start=True, stop=True).then_inc(low_done, 1)

                @block.vector
                def _(dve):
                    dve.wait_ge(bv_done, 1)
                    nc.vector.tensor_copy(bv[:, :], b_bv[0:16, 0:P]).then_inc(bv_ready, 1)
                    dve.wait_ge(means, 3)
                    nc.vector.tensor_scalar(scale[:, 0:4 * P], b_fc[:, :], 1e-5, None, ALU.max).then_inc(chain, 1)
                    nc.vector.tensor_scalar(scale[:, 4 * P:5 * P], b_proj[:, 0:P], 0.25, 1e-5, ALU.mult, ALU.max).then_inc(chain, 1)
                    nc.vector.tensor_scalar(scale2[:, :], b_col[:, 0:1], 0.25, 1e-5, ALU.mult, ALU.max)
                    dve.wait_ge(chain, 2)
                    nc.vector.reciprocal(inverse[:, :], scale[:, :]).then_inc(chain, 1)
                    dve.wait_ge(chain, 3)
                    nc.vector.tensor_tensor(r1[:, :], fc[:, :], inverse[:, 0:4 * P], ALU.mult).then_inc(chain, 1)
                    for m in range(4):
                        nc.vector.tensor_tensor(r2[:, m * P:(m + 1) * P], proj[:, m * P:(m + 1) * P],
                                                inverse[:, 4 * P:5 * P], ALU.mult).then_inc(chain, 1)
                    dve.wait_ge(chain, 8)
                    for n, (r, t) in enumerate(((r1, size_fc), (r2, size_proj))):
                        nc.vector.tensor_scalar(t[:, :], r[:, :], -1.0, 1.0, ALU.max, ALU.min).then_inc(chain, 1)
                        dve.wait_ge(chain, 9 + 2 * n)
                        nc.vector.tensor_scalar(r[:, :], t[:, :], ROUND, None, ALU.add).then_inc(chain, 1)
                        dve.wait_ge(chain, 10 + 2 * n)
                    nc.vector.tensor_scalar(size_fc[:, :], r1[:, :], -ROUND, None, ALU.add).then_inc(chain, 1)
                    nc.vector.tensor_scalar(w2[:, :, :], r2[:, :].rearrange("p (m o) -> p m o", m=4), -ROUND, None, ALU.add)
                    dve.wait_ge(low_done, 1)
                    nc.vector.tensor_scalar(low_rank[:, :], b_low[:, :], gate[:, 0:1], None, ALU.mult).then_inc(chain, 1)
                    dve.wait_ge(chain, 14)
                    nc.vector.tensor_tensor(r1[:, :], size_fc[:, :], scale[:, 0:4 * P], ALU.mult).then_inc(chain, 1)
                    dve.wait_ge(chain, 15)
                    nc.vector.tensor_tensor(fc[:, :], r1[:, :], low_rank[:, :], ALU.add).then_inc(chain, 1)
                    dve.wait_ge(chain, 16)
                    nc.vector.tensor_copy(w1[0][:, :], fc[:, :]).then_inc(chain, 1)
                    dve.wait_ge(chain, 17)
                    nc.vector.tensor_tensor(w1[1][:, :], fc[:, :], w1[0][:, :].bitcast(FP32), ALU.subtract)
        mlp(nc, layer, c, x, x, w1, w2, "relu2", None, scale2, None)


def gated_mlp(nc, c, x, w):
    layer = "l2f"
    M = 4
    with ExitStack() as stack:
        k = Scope(nc, stack, layer)
        w12 = [k.sb(f"w12{p}", [P, 8 * P], F32R) for p in range(2)]
        wh = [[k.sb(f"wh{n}{p}", [P, 16 * P], F32R) for p in range(2)] for n in range(2)]
        w3 = [k.sb(f"w3{p}", [P, 4 * P], F32R) for p in range(2)]
        scales = k.sb("scales", [P, 17])
        half_s1, half_s12 = k.sb("half_s1", [P, 4]), k.sb("half_s12", [P, 4])
        with ExitStack() as staging:
            ks = Scope(nc, staging, layer + "_s")
            s12 = ks.sb("w12", [P, 8 * P])
            sh = [ks.sb(f"wh{n}", [P, 16 * P]) for n in range(2)]
            s3 = ks.sb("w3", [P, 4 * P])
            load_and_split(nc, ks, "load", [
                (w["w12"], s12[:, :], w12[0][:, :], w12[1][:, :]),
                (w["h1"], sh[0][:, :], wh[0][0][:, :], wh[0][1][:, :]),
                (w["h2"], sh[1][:, :], wh[1][0][:, :], wh[1][1][:, :]),
                (w["w3"], s3[:, :], w3[0][:, :], w3[1][:, :]),
                (w["scales"], scales[:, :], None, None)])
            halved = ks.sem("halved")
            with ks.block() as block:
                @block.vector
                def _(dve):
                    nc.vector.tensor_scalar(half_s1[:, :], scales[:, 0:4], 0.5, None, ALU.mult).then_inc(halved, 1)
                    dve.wait_ge(halved, 1)
                    nc.vector.tensor_tensor(half_s12[:, :], half_s1[:, :], scales[:, 4:8], ALU.mult)

        xs = [[k.sb(f"xs{b}{p}", [P, UNIT], F32R) for p in range(2)] for b in range(2)]
        act_out = [[k.sb(f"act{n}{p}", [P, M, UNIT], F32R) for p in range(2)] for n in range(3)]
        tanh = k.sb("tanh", [P, 2, UNIT])
        half = k.sb("half", [P, 2, UNIT])
        prod = k.sb("prod", [P, 2, UNIT])
        gelu = k.sb("gelu", [P, 2, UNIT])
        b_h = [k.bank(f"b_h{m}") for m in range(2)]
        b_a = [[k.bank(f"b_a{m}{q}") for q in range(2)] for m in range(2)]
        b_z = k.bank("b_z")
        (xs_high, xs_ready, a_done, tanh_ready, half_ready, prod_ready, a_high, a_ready, h_done, gelu_ready, h_high,
         h_ready, z_done, y_ready) = (
            k.sem(n) for n in ("xs_high", "xs_ready", "a_done", "tanh_ready", "half_ready", "prod_ready", "a_high",
                               "a_ready", "h_done", "gelu_ready", "h_high", "h_ready", "z_done", "y_ready"))
        block = stack.enter_context(k.block())
        PASSES = ((0, 0), (0, 1), (1, 0))

        def run(eng, step):
            sweep(eng, 2, -1, 2, UNITS // 2 - 1, UNITS // 2 + 2, step)

        def h1_tiles(n):
            if isinstance(n, int):
                return M * min(max(n - 2, 0), UNITS) + M * min(max(n - 1, 0), UNITS)
            return 2 * M * n - 3 * M

        @block.tensor
        def _(pe):
            def step(i, s):
                n, b = 2 * i + s, s % 2
                if live(n - 3, UNITS):
                    hold(pe, h_ready, h1_tiles(n - 1) + (M if live(n - 3, UNITS) else 0))
                    hold(pe, y_ready, n - 3)
                    q = 0
                    for m in range(M):
                        for wi, xi in PASSES:
                            last = nc.tensor.matmul(b_z[:, :], w3[wi][:, m * P:(m + 1) * P], act_out[2][xi][:, m, :],
                                                    start=q == 0, stop=q == 3 * M - 1)
                            q += 1
                    last.then_inc(z_done, 1)
                done = h1_tiles(n)
                for layer_n, unit in ((1, n - 2), (0, n - 1)):
                    if not live(unit, UNITS):
                        continue
                    if layer_n == 1:
                        hold(pe, h_ready, h1_tiles(n))
                    else:
                        hold(pe, a_ready, M * n)
                    for m in range(M):
                        hold(pe, h_ready, done - 1)
                        q = 0
                        for kt in range(M):
                            for wi, xi in PASSES:
                                last = nc.tensor.matmul(b_h[m % 2][:, :], wh[layer_n][wi][:, (m * M + kt) * P:(m * M + kt + 1) * P],
                                                        act_out[layer_n][xi][:, kt, :], start=q == 0, stop=q == 3 * M - 1)
                                q += 1
                        last.then_inc(h_done, 1)
                        done = done + 1
                if live(n, UNITS):
                    hold(pe, xs_ready, n + 1)
                    for m in range(M):
                        hold(pe, prod_ready, M * n + m - 1)
                        for side in range(2):
                            for q, (wi, xi) in enumerate(PASSES):
                                tile = slice((side * M + m) * P, (side * M + m + 1) * P)
                                last = nc.tensor.matmul(b_a[m % 2][side][:, :], w12[wi][:, tile], xs[b][xi][:, :],
                                                        start=q == 0, stop=q == 2)
                        last.then_inc(a_done, 1)
            run(pe, step)

        @block.scalar
        def _(act):
            def step(i, s):
                n = 2 * i + s
                done = h1_tiles(n)
                for layer_n, unit in ((1, n - 2), (0, n - 1)):
                    if not live(unit, UNITS):
                        continue
                    for m in range(M):
                        hold(act, h_done, done + 1)
                        hold(act, h_ready, done - 1)
                        nc.scalar.activation(gelu[:, m % 2, :], b_h[m % 2][:, :], ACT.Gelu,
                                             scale=scales[:, 8 + 4 * layer_n + m:9 + 4 * layer_n + m]).then_inc(gelu_ready, 1)
                        done = done + 1
                        hold(act, gelu_ready, done)
                        if layer_n == 1:
                            hold(act, z_done, n - 2)
                        else:
                            hold(act, h_done, h1_tiles(n) + (M if live(n - 2, UNITS) else 0))
                        nc.scalar.activation(act_out[layer_n + 1][0][:, m, :], gelu[:, m % 2, :], ACT.Copy)\
                            .then_inc(h_high, 1)
                if live(n, UNITS):
                    for m in range(M):
                        hold(act, a_done, M * n + m + 1)
                        hold(act, half_ready, M * n + m - 1)
                        nc.scalar.activation(tanh[:, m % 2, :], b_a[m % 2][0][:, :], ACT.Tanh,
                                             scale=half_s1[:, m:m + 1]).then_inc(tanh_ready, 1)
                        hold(act, prod_ready, M * n + m + 1)
                        hold(act, h_done, h1_tiles(n + 1))
                        nc.scalar.activation(act_out[0][0][:, m, :], prod[:, m % 2, :], ACT.Copy).then_inc(a_high, 1)
            run(act, step)

        @block.vector
        def _(dve):
            def step(i, s):
                n, b = 2 * i + s, s % 2
                if live(n + 1, UNITS):
                    hold(dve, a_done, M * n)
                    xb = x[:, bass.ds((n + 1) * UNIT, UNIT)]
                    nc.vector.tensor_scalar(xs[1 - b][0][:, :], xb, 1.0, None, ALU.mult).then_inc(xs_high, 1)
                    hold(dve, xs_high, n + 2)
                    nc.vector.tensor_tensor(xs[1 - b][1][:, :], xb, xs[1 - b][0][:, :].bitcast(FP32),
                                            ALU.subtract).then_inc(xs_ready, 1)
                if live(n - 3, UNITS):
                    hold(dve, z_done, n - 2)
                    xb = x[:, bass.ds((n - 3) * UNIT, UNIT)]
                    nc.vector.scalar_tensor_tensor(xb, b_z[:, :], scales[:, 16:17], xb, ALU.mult, ALU.add)\
                        .then_inc(y_ready, 1)
                done = h1_tiles(n)
                for layer_n, unit in ((1, n - 2), (0, n - 1)):
                    if not live(unit, UNITS):
                        continue
                    for m in range(M):
                        hold(dve, h_high, done + 1)
                        nc.vector.tensor_tensor(act_out[layer_n + 1][1][:, m, :], gelu[:, m % 2, :],
                                                act_out[layer_n + 1][0][:, m, :].bitcast(FP32), ALU.subtract)\
                            .then_inc(h_ready, 1)
                        done = done + 1
                if live(n, UNITS):
                    for m in range(M):
                        hold(dve, tanh_ready, M * n + m + 1)
                        nc.vector.scalar_tensor_tensor(half[:, m % 2, :], tanh[:, m % 2, :], 1.0, b_a[m % 2][0][:, :],
                                                       ALU.add, ALU.mult).then_inc(half_ready, 1)
                        hold(dve, half_ready, M * n + m + 1)
                        hold(dve, a_high, M * n + m - 1)
                        nc.vector.scalar_tensor_tensor(prod[:, m % 2, :], b_a[m % 2][1][:, :], half_s12[:, m:m + 1],
                                                       half[:, m % 2, :], ALU.mult, ALU.mult).then_inc(prod_ready, 1)
                        hold(dve, a_high, M * n + m + 1)
                        nc.vector.tensor_tensor(act_out[0][1][:, m, :], prod[:, m % 2, :],
                                                act_out[0][0][:, m, :].bitcast(FP32), ALU.subtract).then_inc(a_ready, 1)
            run(dve, step)


def chunked_attention(nc, c, x, w):
    layer = "l3a"
    H, CHUNK = 8, 64
    WIDTH = H * P
    PAIRS = H // 2
    with ExitStack() as stack:
        k = Scope(nc, stack, layer)
        wqkv = [[k.sb(f"w{n}{p}", [P, WIDTH], F32R) for p in range(2)] for n in ("q", "k", "v")]
        wg = [k.sb(f"wg{p}", [P, H], F32R) for p in range(2)]
        wo = k.sb("wo", [P, H, P])
        bg, gain = k.sb("bg", [P, H]), k.sb("gain", [P, 1])
        between = k.sb("between", [P, 3, P])
        first_half = k.sb("first_half", [P, 1])
        mask = k.sb("mask", [P, H, CHUNK], BF16)
        with ExitStack() as staging:
            ks = Scope(nc, staging, layer + "_s")
            raw = [ks.sb(f"raw{n}", [P, WIDTH]) for n in range(3)]
            rawg, rawm = ks.sb("rawg", [P, H]), ks.sb("rawm", [P, CHUNK])
            load_and_split(nc, ks, "load",
                           [(w[name], raw[n][:, :], wqkv[n][0][:, :], wqkv[n][1][:, :]) for n, name in enumerate(("wq", "wk", "wv"))]
                           + [(w["wg"], rawg[:, :], wg[0][:, :], wg[1][:, :]), (w["wo"], wo[:, :, :], None, None),
                              (w["bg"], bg[:, :], None, None), (w["gain"], gain[:, :], None, None),
                              (w["between"], between[:, :, :], None, None), (w["first_half"], first_half[:, :], None, None),
                              (w["mask"], rawm[:, :], None, None)])
            with ks.block() as block:
                @block.vector
                def _(dve):
                    for h in range(H):
                        nc.vector.tensor_copy(mask[:, h, :], rawm[:, :])

        xs = [k.sb(f"xs{p}", [P, SEQ], F32R) for p in range(2)]
        sq = k.sb("sq", [P, WIDTH])
        ss, ln_ss, rms = k.sb("ss", [P, H]), k.sb("ln_ss", [P, H]), k.sb("rms", [P, H])
        rms_gain = k.sb("rms_gain", [P, H])
        qkn = [k.sb(f"qkn{n}", [P, WIDTH]) for n in range(4)]
        vt = k.sb("vt", [P, 2, WIDTH])
        qt, kt = k.sb("qt", [P, H, SEQ]), k.sb("kt", [P, H, SEQ])
        z, ze, lg = k.sb("z", [P, 2, H]), k.sb("ze", [P, 2, H]), k.sb("lg", [P, 2, H])
        decay = k.sb("decay", [P, 3, H])
        centred, probs = k.sb("centred", [P, H, CHUNK]), k.sb("probs", [P, H, CHUNK])
        top, total, inv = k.sb("top", [P, H]), k.sb("total", [P, H]), k.sb("inv", [P, H])
        pn = [k.sb(f"pn{tb}", [P, H, P]) for tb in range(2)]
        ptt = k.sb("ptt", [P, H, 3 * HALF])
        yt = k.sb("yt", [P, H, SEQ])
        ring = [k.bank(f"ring{n}", 2) for n in range(2)]
        b_d = [k.bank(f"b_d{n}") for n in range(2)]
        b_x = [k.bank(f"b_x{n}") for n in range(2)]
        (presets, xs_high, xs_ready, g_done, z_ready, z_low, ze_ready, lg_ready, l_done, decay_ready, qk_done, sq_ready,
         ss_ready, ln_ready, rms_ready, rg_ready, qk_ready, d_done, top_ready, c_ready, probs_ready, total_ready,
         inv_ready, pn_ready, x_done, x_ready, pt_done, pt_ready, y_done, y_ready, f_done, f_ready, v_done, v_ready,
         tr_done, tr_ready) = (k.sem(n) for n in (
             "presets", "xs_high", "xs_ready", "g_done", "z_ready", "z_low", "ze_ready", "lg_ready", "l_done", "decay_ready",
             "qk_done", "sq_ready", "ss_ready", "ln_ready", "rms_ready", "rg_ready", "qk_ready", "d_done", "top_ready",
             "c_ready", "probs_ready", "total_ready", "inv_ready", "pn_ready", "x_done", "x_ready", "pt_done",
             "pt_ready", "y_done", "y_ready", "f_done", "f_ready", "v_done", "v_ready", "tr_done", "tr_ready"))
        block = stack.enter_context(k.block())
        B = BATCHES

        def run(eng, step):
            sweep(eng, 1, -1, 2, B - 1, B + 1, lambda i, s: step(i))

        def at(i, count_now, count_before):
            return count_now if live(i, B) else count_before

        @block.gpsimd
        def _(pool):
            for tb in range(2):
                nc.gpsimd.memset(pn[tb][:, :, :], 0.0).then_inc(presets, 1)

        @block.tensor
        def _(pe):
            pe.wait_ge(presets, 2)

            def project(bank, weights, tb):
                for half in range(2):
                    for q, (xi, wi) in enumerate(((0, 0), (1, 0), (0, 1))):
                        last = nc.tensor.matmul(bank[:, half * BANK:(half + 1) * BANK], xs[xi][:, tb * P:(tb + 1) * P],
                                                weights[wi][:, half * BANK:(half + 1) * BANK], start=q == 0, stop=q == 2)
                return last

            def step(i):
                j = i - 1
                if live(i, B):
                    hold(pe, xs_ready, i + 1)
                    hold(pe, decay_ready, i)
                    hold(pe, x_ready, 4 * (i - 1))
                    for tb in range(2):
                        for q, (xi, wi) in enumerate(((0, 0), (1, 0), (0, 1))):
                            last = nc.tensor.matmul(b_x[1][:, tb * H:(tb + 1) * H], xs[xi][:, tb * P:(tb + 1) * P], wg[wi][:, :],
                                                    start=q == 0 and tb == 0, stop=q == 2, skip_group_check=True)
                    last.then_inc(g_done, 1)
                    for n in range(4):
                        if n < 2:
                            hold(pe, tr_ready, 4 * i)
                        else:
                            hold(pe, qk_ready, 4 * i + n - 1)
                        project(ring[n % 2], wqkv[n % 2], n // 2).then_inc(qk_done, 1)
                if live(j, B):
                    hold(pe, tr_ready, 4 * i)
                    hold(pe, y_ready, PAIRS * j)
                    for tb in range(2):
                        nc.tensor.matmul(b_d[tb][:, :], c.ident_b[:, :], mask[:, :, :], start=True, stop=True,
                                         skip_group_check=True)
                        for h in range(H):
                            for half in range(2):
                                t = slice(tb * P + half * CHUNK, tb * P + (half + 1) * CHUNK)
                                last = nc.tensor.matmul(b_d[tb][half * CHUNK:(half + 1) * CHUNK, h * CHUNK:(h + 1) * CHUNK],
                                                        qt[:, h, t], kt[:, h, t], start=False, stop=True,
                                                        skip_group_check=True)
                        last.then_inc(d_done, 1)
                    hold(pe, z_ready, at(i, i + 1, i))
                    hold(pe, f_ready, j)
                    for p in range(PAIRS):
                        hold(pe, x_ready, PAIRS * j + p - 1)
                        bank = b_x[p % 2]
                        for hh in range(2):
                            h = 2 * p + hh
                            nc.tensor.matmul(bank[:, hh * SEQ:hh * SEQ + 192], kt[:, h, 0:HALF], qt[:, h, CHUNK:SEQ],
                                             start=hh == 0, stop=True, skip_group_check=True)
                            last = nc.tensor.matmul(bank[:, hh * SEQ + 192:(hh + 1) * SEQ], kt[:, h, HALF:SEQ],
                                                    qt[:, h, 192:SEQ], start=False, stop=True, skip_group_check=True)
                        last.then_inc(x_done, 1)
                    for tb in range(2):
                        hold(pe, pn_ready, 4 * j + 2 * tb + 2)
                        hold(pe, qk_ready, at(i, 4 * i + 3 + tb, 4 * i))
                        for h in range(H):
                            last = nc.tensor.transpose(ring[tb][:, h * P:(h + 1) * P], pn[tb][:, h, :], c.ident[:, :])
                        last.then_inc(pt_done, 1)
                    hold(pe, pt_ready, 2 * i)
                    hold(pe, c_ready, 2 * i)
                    for p in range(PAIRS):
                        hold(pe, y_ready, PAIRS * j + p - 1)
                        for hh in range(2):
                            h = 2 * p + hh
                            nc.tensor.matmul(b_d[p % 2][:, hh * SEQ:(hh + 1) * SEQ], vt[:, 0, h * P:(h + 1) * P], ptt[:, h, 0:SEQ],
                                             start=hh == 0, stop=True, skip_group_check=True)
                            last = nc.tensor.matmul(b_d[p % 2][:, hh * SEQ + HALF:(hh + 1) * SEQ], vt[:, 1, h * P:(h + 1) * P],
                                                    ptt[:, h, SEQ:3 * HALF], start=False, stop=True, skip_group_check=True)
                        last.then_inc(y_done, 1)
                    hold(pe, x_ready, PAIRS * i)
                    hold(pe, y_ready, PAIRS * i)
                    for h in range(H):
                        last = nc.tensor.matmul(b_x[0][:, 0:SEQ], wo[:, h, :], yt[:, h, :], start=h == 0, stop=h == H - 1)
                    last.then_inc(f_done, 1)
                if live(i, B):
                    for tb in range(2):
                        hold(pe, pt_ready, 2 * i - 1 + tb if not isinstance(i, int) or i > 0 else 0)
                        hold(pe, qk_ready, 4 * i + 3 + tb)
                        project(ring[tb], wqkv[2], tb).then_inc(v_done, 1)
                    hold(pe, lg_ready, i + 1)
                    hold(pe, x_ready, PAIRS * i)
                    for q, (n, tb, col) in enumerate(((0, 0, 0), (1, 0, 1), (2, 1, 1))):
                        last = nc.tensor.matmul(b_x[1][:, BANK // 2 + col * H:BANK // 2 + (col + 1) * H], between[:, n, :],
                                                lg[:, tb, :], start=q == 0, stop=q != 1, skip_group_check=True)
                    last.then_inc(l_done, 1)
                    for n in range(4):
                        hold(pe, qk_ready, 4 * i + n + 1)
                        if n < 2:
                            hold(pe, v_ready, 2 * i + n + 1)
                        else:
                            hold(pe, tr_ready, 4 * i + n - 1)
                        for h in range(H):
                            last = nc.tensor.transpose(ring[n % 2][:, h * P:(h + 1) * P], qkn[n][:, h * P:(h + 1) * P], c.ident[:, :])
                        last.then_inc(tr_done, 1)
            run(pe, step)

        @block.scalar
        def _(act):
            act.wait_ge(presets, 2)

            def step(i):
                j = i - 1
                if live(i, B):
                    hold(act, z_low, i + 1)
                    nc.scalar.activation(ze[:, :, :], z[:, :, :], ACT.Exp, scale=-1.0).then_inc(ze_ready, 1)
                    hold(act, ze_ready, i + 1)
                    hold(act, l_done, i)
                    nc.scalar.activation(lg[:, :, :], ze[:, :, :], ACT.Ln, bias=1.0).then_inc(lg_ready, 1)
                    for n in range(4):
                        hold(act, qk_done, 4 * i + n + 1)
                        hold(act, ss_ready, 4 * i + n)
                        nc.scalar.activation(sq[:, :], ring[n % 2][:, :], ACT.Square).then_inc(sq_ready, 1)
                        hold(act, ss_ready, 4 * i + n + 1)
                        hold(act, rms_ready, 4 * i + n)
                        nc.scalar.activation(ln_ss[:, :], ss[:, :], ACT.Ln, scale=1.0 / P, bias=c.eps[:, 1:2]).then_inc(ln_ready, 1)
                        hold(act, ln_ready, 4 * i + n + 1)
                        hold(act, qk_ready, 4 * i + n)
                        nc.scalar.activation(rms[:, :], ln_ss[:, :], ACT.Exp, scale=-0.5).then_inc(rms_ready, 1)
                if live(j, B):
                    for tb in range(2):
                        hold(act, c_ready, 2 * j + tb + 1)
                        hold(act, pn_ready, 4 * j + 2 * tb)
                        nc.scalar.activation(probs[:, :, :], centred[:, :, :], ACT.Exp, scale=P ** -0.5).then_inc(probs_ready, 1)
                    hold(act, f_done, j)
                    for p in range(PAIRS):
                        hold(act, y_done, PAIRS * j + p + 1)
                        nc.scalar.activation(yt[:, 2 * p:2 * p + 2, :], b_d[p % 2][:, :].rearrange("p (h t) -> p h t", t=SEQ),
                                             ACT.Copy).then_inc(y_ready, 1)
                if live(i, B):
                    for tb in range(2):
                        hold(act, v_done, 2 * i + tb + 1)
                        nc.scalar.activation(vt[:, tb, :], ring[tb][:, :], ACT.Copy).then_inc(v_ready, 1)
                    hold(act, l_done, i + 1)
                    hold(act, x_ready, PAIRS * i)
                    nc.scalar.activation(decay[:, 1:3, :], b_x[1][:, BANK // 2:BANK // 2 + 2 * H].rearrange("p (c h) -> p c h", h=H),
                                         ACT.Exp, scale=-1.0).then_inc(decay_ready, 1)
                    for n in range(4):
                        hold(act, tr_done, 4 * i + n + 1)
                        hold(act, x_done, PAIRS * i)
                        nc.scalar.activation((qt, kt)[n % 2][:, :, (n // 2) * P:(n // 2 + 1) * P],
                                             ring[n % 2][:, :].rearrange("p (h t) -> p h t", t=P), ACT.Copy).then_inc(tr_ready, 1)
            run(act, step)

        @block.vector
        def _(dve):
            nc.vector.tensor_scalar(decay[:, 0, :], bg[:, :], 0.0, first_half[:, 0:1], ALU.mult, ALU.add).then_inc(rg_ready, 1)
            dve.wait_ge(presets, 2)

            def step(i):
                j = i - 1
                if live(i, B):
                    hold(dve, g_done, i + 1)
                    hold(dve, ze_ready, i)
                    nc.vector.tensor_tensor(z[:, :, :], b_x[1][:, 0:2 * H].rearrange("p (b h) -> p b h", h=H),
                                            bg[:, :].unsqueeze(1).to_broadcast([P, 2, H]), ALU.add).then_inc(z_ready, 1)
                    hold(dve, z_ready, i + 1)
                    nc.vector.tensor_scalar(z[:, :, :], z[:, :, :], -85.0, None, ALU.max).then_inc(z_low, 1)
                    for n in range(4):
                        hold(dve, sq_ready, 4 * i + n + 1)
                        hold(dve, ln_ready, 4 * i + n)
                        nc.vector.tensor_reduce(ss[:, :], sq[:, :].rearrange("p (h d) -> p h d", d=P), AX.X, ALU.add).then_inc(ss_ready, 1)
                        hold(dve, rms_ready, 4 * i + n + 1)
                        scale = rms
                        if n % 2 == 0:
                            nc.vector.tensor_scalar(rms_gain[:, :], rms[:, :], gain[:, 0:1], None, ALU.mult).then_inc(rg_ready, 1)
                            hold(dve, rg_ready, 2 * i + n // 2 + 2)
                            scale = rms_gain
                        hold(dve, tr_done, 4 * (i - 1) + n + 1)
                        nc.vector.tensor_tensor(qkn[n][:, :].rearrange("p (h d) -> p h d", d=P),
                                                ring[n % 2][:, :].rearrange("p (h d) -> p h d", d=P),
                                                scale[:, :].unsqueeze(2).to_broadcast([P, H, P]), ALU.mult).then_inc(qk_ready, 1)
                if live(j, B):
                    for tb in range(2):
                        u = 2 * j + tb
                        hold(dve, d_done, u + 1)
                        scores = b_d[tb][:, :].rearrange("p (h s) -> p h s", s=CHUNK)
                        hold(dve, c_ready, u)
                        nc.vector.tensor_reduce(top[:, :], scores, AX.X, ALU.max).then_inc(top_ready, 1)
                        hold(dve, top_ready, u + 1)
                        hold(dve, probs_ready, u)
                        nc.vector.tensor_tensor(centred[:, :, :], scores, top[:, :].unsqueeze(2).to_broadcast([P, H, CHUNK]),
                                                ALU.subtract).then_inc(c_ready, 1)
                        hold(dve, probs_ready, u + 1)
                        hold(dve, inv_ready, u)
                        nc.vector.tensor_reduce(total[:, :], probs[:, :, :], AX.X, ALU.add).then_inc(total_ready, 1)
                        hold(dve, total_ready, u + 1)
                        hold(dve, pn_ready, 2 * u)
                        nc.vector.reciprocal(inv[:, :], total[:, :]).then_inc(inv_ready, 1)
                        hold(dve, inv_ready, u + 1)
                        hold(dve, pt_done, u - 1)
                        for half in range(2):
                            rows = slice(half * CHUNK, (half + 1) * CHUNK)
                            nc.vector.tensor_tensor(pn[tb][rows, :, half * CHUNK:(half + 1) * CHUNK], probs[rows, :, :],
                                                    inv[rows, :].unsqueeze(2).to_broadcast([CHUNK, H, CHUNK]),
                                                    ALU.mult).then_inc(pn_ready, 1)
                    hold(dve, decay_ready, i)
                    hold(dve, y_done, PAIRS * j)
                    for p in range(PAIRS):
                        hold(dve, x_done, PAIRS * j + p + 1)
                        bank = b_x[p % 2][:, :].rearrange("p (h c t) -> p h c t", h=2, t=CHUNK)
                        for hh in range(2):
                            h = 2 * p + hh
                            nc.vector.tensor_tensor(ptt[:, h, CHUNK:SEQ].rearrange("p (c t) -> p c t", t=CHUNK), bank[:, hh, 0:3, :],
                                                    decay[:, :, h:h + 1].to_broadcast([P, 3, CHUNK]), ALU.mult)
                        nc.vector.tensor_scalar(ptt[:, 2 * p:2 * p + 2, SEQ + CHUNK:3 * HALF], bank[:, :, 3, :],
                                                first_half[:, 0:1], None, ALU.mult).then_inc(x_ready, 1)
                    hold(dve, x_ready, PAIRS * i)
                    for tb in range(2):
                        hold(dve, pt_done, 2 * j + tb + 1)
                        bank = ring[tb][:, :].rearrange("p (h t) -> p h t", t=P)
                        nc.vector.tensor_copy(ptt[:, :, tb * SEQ:tb * SEQ + CHUNK], bank[:, :, 0:CHUNK])
                        own = ptt[:, :, tb * SEQ + CHUNK:tb * SEQ + P]
                        nc.vector.tensor_tensor(own, bank[:, :, CHUNK:P], own, ALU.add).then_inc(pt_ready, 1)
                    hold(dve, f_done, i)
                    xb = x[:, bass.ds(j * SEQ, SEQ)]
                    nc.vector.tensor_tensor(xb, b_x[0][:, 0:SEQ], xb, ALU.add).then_inc(f_ready, 1)
                if live(i + 1, B):
                    hold(dve, v_done, 2 * (i + 1))
                    xb = x[:, bass.ds((i + 1) * SEQ, SEQ)]
                    nc.vector.tensor_scalar(xs[0][:, :], xb, 1.0, None, ALU.mult).then_inc(xs_high, 1)
                    hold(dve, xs_high, i + 2)
                    nc.vector.tensor_tensor(xs[1][:, :], xb, xs[0][:, :].bitcast(FP32), ALU.subtract).then_inc(xs_ready, 1)
            run(dve, step)


class Constants:

    def __init__(self, nc, stack, dram):
        k = Scope(nc, stack, "const")
        self.centre = k.sb("centre", [P, P])
        self.mean = k.sb("mean", [P, P])
        self.ones = k.sb("ones", [P, 64])
        self.eps = k.sb("eps", [P, 3])
        self.low_rows = k.sb("low_rows", [P, 4])
        self.aug_low = k.sb("aug_low", [3, 1])
        self.ident_r = k.sb("ident_r", [P, P], F32R)
        self.ident = k.sb("ident", [P, P])
        self.ident_b = k.sb("ident_b", [P, P], BF16)
        self.mask_q = k.sb("mask_q", [P, 2, P], BF16)
        self.mask_k = k.sb("mask_k", [P, 2, P], BF16)
        self.aug_x = k.sb("aug_x", [3, SEQ], F32R)
        with ExitStack() as staging:
            ks = Scope(nc, staging, "const_s")
            mq, mk, ax = ks.sb("mq", [P, P]), ks.sb("mk", [P, P]), ks.sb("ax", [3, SEQ])
            loaded = ks.sem("loaded")
            pairs = [(self.centre, "centre"), (self.ident, "ident"), (mq, "mask_q"), (mk, "mask_k"),
                     (ax, "aug_x"), (self.low_rows, "low_rows"), (self.aug_low, "aug_low")]
            with ks.block() as block:
                @block.sync
                def _(sp):
                    for dst, name in pairs:
                        sp.dma_start(dst[:, :], dram[name]).then_inc(loaded, 16)
                    sp.wait_ge(loaded, 16 * len(pairs))

                @block.vector
                def _(dve):
                    nc.vector.memset(self.mean[:, :], 1.0 / P)
                    nc.vector.memset(self.ones[:, :], 1.0)
                    nc.vector.memset(self.eps[:, 0:1], EPS)
                    nc.vector.memset(self.eps[:, 1:2], 1e-6)
                    nc.vector.memset(self.eps[:, 2:3], EPS / 4)
                    dve.wait_ge(loaded, 16 * len(pairs))
                    nc.vector.tensor_copy(self.ident_r[:, :], self.ident[:, :])
                    nc.vector.tensor_copy(self.ident_b[:, :], self.ident[:, :])
                    nc.vector.tensor_copy(self.aug_x[:, :], ax[:, :])
                    for b in range(2):
                        nc.vector.tensor_copy(self.mask_q[:, b, :], mq[:, :])
                        nc.vector.tensor_copy(self.mask_k[:, b, :], mk[:, :])


L0_SHAPE = AttentionShape(dim=8, rows=32, tiles=1, events=4, split=True, v_width=32, scale=8 ** -0.5, q_aug=True,
                          v_slots=(0, 3), o_tiles=4, low_col=0)
L1_SHAPE = AttentionShape(dim=64, rows=128, tiles=2, events=8, split=False, v_width=64, scale=0.125, q_aug=False,
                          v_slots=(0, 1, 3, 4), o_tiles=8)
L2_SHAPE = AttentionShape(dim=16, rows=64, tiles=1, events=8, split=True, v_width=32, scale=8 ** -0.5, q_aug=False,
                          v_slots=(0, 3), o_tiles=4, low_col=2)


def program(nc, d, out):
    with ExitStack() as stack:
        k = Scope(nc, stack, "model")
        x = k.sb("x", [P, TOKENS])
        x_loaded, stored = k.sem("x_loaded"), k.sem("stored")
        c = Constants(nc, stack, d)
        with nc.Block() as block:
            @block.sync
            def _(sp):
                sp.dma_start(x[:, :], d["x"]).then_inc(x_loaded, 16)
                sp.wait_ge(x_loaded, 16)
        for run in STAGES:
            run(nc, c, x, d)
        with nc.Block() as block:
            @block.sync
            def _(sp):
                sp.dma_start(out, x[:, :]).then_inc(stored, 16)
                sp.wait_ge(stored, 16)


def group(d, prefix):
    return {name[len(prefix):]: ap for name, ap in d.items() if name.startswith(prefix)}


STAGES = [
    lambda nc, c, x, d: attention(nc, "l0a", c, x, group(d, "l0a_"), L0_SHAPE),
    lambda nc, c, x, d: layer_norm(nc, "ln0", c, x, x),
    lambda nc, c, x, d: reglu(nc, "l0f", c, x, group(d, "l0f_")),
    lambda nc, c, x, d: layer_norm(nc, "ln1", c, x, x),
    lambda nc, c, x, d: attention(nc, "l1a", c, x, group(d, "l1a_"), L1_SHAPE),
    lambda nc, c, x, d: layer_norm(nc, "ln2", c, x, x),
    lambda nc, c, x, d: quantised_mlp(nc, c, x, group(d, "l1f_")),
    lambda nc, c, x, d: layer_norm(nc, "ln3", c, x, x, eps=2),
    lambda nc, c, x, d: attention(nc, "l2a", c, x, group(d, "l2a_"), L2_SHAPE),
    lambda nc, c, x, d: layer_norm(nc, "ln4", c, x, x),
    lambda nc, c, x, d: gated_mlp(nc, c, x, group(d, "l2f_")),
    lambda nc, c, x, d: layer_norm(nc, "ln5", c, x, x),
    lambda nc, c, x, d: chunked_attention(nc, c, x, group(d, "l3a_")),
    lambda nc, c, x, d: layer_norm(nc, "ln6", c, x, x),
    lambda nc, c, x, d: ternary_mlp(nc, c, x, group(d, "l3f_")),
    lambda nc, c, x, d: layer_norm(nc, "ln7", c, x, x),
]


def head_tiles(np, w, rows, copies):
    dim = w.shape[2]
    tiles = np.zeros((w.shape[0], 16, rows), w.dtype)
    for n in range(copies):
        tiles[:, :, n * dim:(n + 1) * dim] = w
    return tiles.reshape(w.shape[0], 16 * rows)


def n_rows(np):
    return np.arange(P)


def layout(np, a):
    h = {}
    n = np.arange(P)
    h["x"] = a["L0_attn_x"].transpose(2, 0, 1).reshape(P, TOKENS)
    h["centre"] = (np.eye(P) - 1.0 / P).astype(np.float32)
    h["ident"] = np.eye(P, dtype=np.float32)
    h["mask_q"] = np.where(n[None, :] > n[:, None], MASKED, 0.0).astype(np.float32)
    h["mask_k"] = np.ascontiguousarray(h["mask_q"].T)
    h["aug_x"] = np.stack([np.ones(SEQ), np.ones(SEQ), np.arange(SEQ)]).astype(np.float32)
    h["aug_low"] = np.array([[0], [1], [0]], np.float32)
    low = np.zeros((P, 4), np.float32)
    low[:, 0] = ((n % 32 >= 16) & (n % 32 < 24)) | (n % 32 == 27)
    low[:, 1] = (n % 32 >= 8) & (n % 32 < 16)
    low[:, 2] = (n % 64 >= 32) & (n % 64 < 48)
    low[:, 3] = (n % 64 >= 16) & (n % 64 < 32)
    h["low_rows"] = low

    def wo_tiles(w, width):
        padded = np.zeros((16, width, P), np.float32)
        padded[:, :w.shape[1]] = w
        return padded.reshape(-1, P, P).transpose(1, 0, 2)

    def ones_rows(rows, at):
        aug = np.zeros((3, 16, rows), np.float32)
        aug[0:2, :, at:at + 2] = 1.0
        return aug

    for p in ("q", "k"):
        h["l0a_w" + p] = head_tiles(np, a["L0_attn_W" + p].T.reshape(P, 16, 8), 32, 3)
    h["l0a_wv"] = a["L0_attn_Wv"].T
    h["l0a_wo"] = wo_tiles(a["L0_attn_Wo"].T.reshape(16, 8, P), 32)
    bv = np.zeros((16, 32), np.float32)
    bv[:, :8] = a["L0_attn_bv"].reshape(16, 8)
    h["l0a_bv"] = bv.reshape(4, P).T
    h["l0a_bo"] = a["L0_attn_bo"].reshape(P, 1)
    slopes = np.power(np.float32(2.0), -8.0 * np.arange(1, 17, dtype=np.float32) / 16).astype(np.float32)
    aug = np.zeros((3, 16, 32), np.float32)
    for n3 in range(3):
        aug[0:2, :, n3 * 8:n3 * 8 + 8] = a["L0_attn_bq"].reshape(1, 16, 8)
    aug[0:2, :, 26:28] = (slopes * np.float32(8 ** 0.5))[None, :, None]
    h["l0a_aug_q"] = aug.reshape(3, 512)
    aug = ones_rows(32, 24)
    for n3 in range(3):
        aug[0:2, :, n3 * 8:n3 * 8 + 8] = a["L0_attn_bk"].reshape(1, 16, 8)
    aug[2, :, 26:28] = 1.0
    h["l0a_aug_k"] = aug.reshape(3, 512)

    for p in ("q", "k"):
        h["l1a_w" + p] = head_tiles(np, a["L1_attn_w_" + p].transpose(2, 0, 1), 128, 1)
    h["l1a_wv"] = a["L1_attn_w_v"].transpose(2, 0, 1).reshape(P, 1024)
    h["l1a_wo"] = a["L1_attn_w_o"].reshape(8, P, P).transpose(1, 0, 2)
    h["l1a_aug_k"] = ones_rows(128, 64).reshape(3, 2048)

    for p in ("q", "k"):
        h["l2a_w" + p] = head_tiles(np, a["L2_attn_W" + p].reshape(P, 16, 16), 64, 3)
    h["l2a_wv"] = a["L2_attn_Wv"]
    h["l2a_wo"] = wo_tiles(a["L2_attn_Wo"].reshape(16, 16, P), 32)
    h["l2a_aug_k"] = ones_rows(64, 48).reshape(3, 1024)

    h["l0f_w"] = np.stack([a["L0_ffn_W_r"].T, a["L0_ffn_W_k"].T], axis=1)
    h["l0f_mu"] = np.stack([a["L0_ffn_mu_r"], a["L0_ffn_mu_k"]], axis=1)
    h["l0f_wv"] = a["L0_ffn_W_v"].T

    def columns(v):
        return v.reshape(-1, P).T

    def k_tiles(w):
        return w.reshape(-1, P, w.shape[1]).transpose(1, 0, 2)

    h["l1f_fc1_q"] = a["L1_ffn_fc1_q"]
    h["l1f_fc2_q"] = k_tiles(a["L1_ffn_fc2_q"])
    h["l1f_fc1_s"] = np.broadcast_to(a["L1_ffn_fc1_scales"], (P, 512))
    h["l1f_fc2_s"] = np.broadcast_to(a["L1_ffn_fc2_scales"][None], (P, 4, P))
    h["l1f_b1"] = columns(a["L1_ffn_fc1_bias"])
    h["l1f_b2"] = columns(a["L1_ffn_fc2_bias"])
    h["l1f_gamma"] = columns(a["L1_ffn_ln_gamma"])
    h["l1f_beta"] = columns(a["L1_ffn_ln_beta"])

    h["l2f_w12"] = np.concatenate([a["L2_ffn_w1_w"].T, a["L2_ffn_w2_w"].T], axis=1)
    for n in ("1", "2"):
        h["l2f_h" + n] = a["L2_ffn_h" + n + "_w"].reshape(4, P, 4, P).transpose(3, 0, 2, 1).reshape(P, 16 * P)
    h["l2f_w3"] = k_tiles(a["L2_ffn_w3_w"].T).reshape(P, 4 * P)
    h["l2f_scales"] = np.concatenate([columns(a["L2_ffn_" + n]) for n in ("w1_s", "w2_s", "h1_s", "h2_s", "w3_s")], axis=1)

    for n in ("q", "k", "v", "g"):
        h["l3a_w" + n] = a["L3_attn_W" + n].T
    h["l3a_wo"] = k_tiles(a["L3_attn_Wo"].T)
    h["l3a_bg"] = np.broadcast_to(a["L3_attn_bg"], (P, 8))
    h["l3a_gain"] = np.broadcast_to(a["L3_attn_qk_gain"].reshape(1, 1), (P, 1))
    chunk = np.arange(P) // 64
    between = np.zeros((P, 3, P), np.float32)
    between[:, 0] = between[:, 1] = (chunk[:, None] == 1) & (chunk[None, :] == 0)
    between[:, 2] = chunk[:, None] == 0
    h["l3a_between"] = between
    h["l3a_first_half"] = (chunk == 0).astype(np.float32).reshape(P, 1)
    h["l3a_mask"] = np.where(np.arange(64)[None, :] > (n_rows(np) % 64)[:, None], MASKED, 0.0).astype(np.float32)

    h["l3f_w_fc"] = a["L3_ffn_w_fc"].T
    h["l3f_w_proj"] = k_tiles(a["L3_ffn_w_proj"].T).reshape(P, 4 * P)
    h["l3f_bt"] = a["L3_ffn_fast_b"].T
    h["l3f_v"] = a["L3_ffn_v"]
    h["l3f_ut"] = a["L3_ffn_u"].T
    h["l3f_gate"] = np.broadcast_to(a["L3_ffn_gate"].reshape(1, 1), (P, 1))
    return h


def kernel(**inputs):
    import numpy as _np
    import concourse.bacc as _bacc
    from concourse import mybir as _mybir
    from concourse.bass_utils import run_bass_kernel_spmd as _run

    nc = _bacc.Bacc("TRN2", target_bir_lowering=False, num_devices=1)
    arrays, d = {}, {}
    for name, value in layout(_np, {n: _np.asarray(v) for n, v in inputs.items()}).items():
        value = _np.ascontiguousarray(value)
        arrays["in_" + name] = value
        d[name] = nc.dram_tensor("in_" + name, value.shape, _mybir.dt.from_np(value.dtype), kind="ExternalInput").ap()
    out = nc.dram_tensor("out", (P, TOKENS), _mybir.dt.float32, kind="ExternalOutput").ap()
    program(nc, d, out)
    r = _run(nc, [arrays], core_ids=[0])
    return _np.ascontiguousarray(r.results[0]["out"].reshape(P, BATCHES, SEQ).transpose(1, 2, 0))
```

```python
import concourse.bass as bass
from concourse import mybir
from contextlib import ExitStack, contextmanager

FP32 = mybir.dt.float32
F32R = mybir.dt.float32r
BF16 = mybir.dt.bfloat16
I32 = mybir.dt.int32
ACT = mybir.ActivationFunctionType
ALU = mybir.AluOpType
AX = mybir.AxisListType

P = 128
BATCHES, SEQ = 32, 256
TOKENS = BATCHES * SEQ
BANK = 512
UNIT = BANK
UNITS = TOKENS // UNIT
HALF = SEQ // 2
EPS = 1e-5
MASKED = -1e30


def live(unit, total):
    return not isinstance(unit, int) or 0 <= unit < total


def hold(eng, sem, count):
    if not isinstance(count, int) or count > 0:
        eng.wait_ge(sem, count)


def sweep(eng, slots, first, loop_from, loop_to, last, step):
    for i in range(first, loop_from):
        for s in range(slots):
            step(i, s)
    with eng.Fori(loop_from, loop_to) as i:
        for s in range(slots):
            step(i, s)
    for i in range(loop_to, last):
        for s in range(slots):
            step(i, s)


class Scope:

    def __init__(self, nc, stack, layer):
        self.nc, self.stack, self.layer = nc, stack, layer
        self.sems = []

    def sb(self, name, shape, dt=FP32):
        return self.stack.enter_context(self.nc.sbuf_tensor(f"{self.layer}_{name}", shape, dt))

    def bank(self, name, banks=1):
        return self.stack.enter_context(self.nc.psum_tensor(f"{self.layer}_{name}", [P, banks * BANK], FP32))

    def sem(self, name):
        handle = self.stack.enter_context(self.nc.semaphore(f"{self.layer}_{name}"))
        self.sems.append(handle)
        return handle

    @contextmanager
    def block(self):
        with self.nc.Block() as block:
            yield block
        numbers = sorted(s.num for s in self.sems)
        with self.nc.Block() as block:
            @block.gpsimd
            def _(pool):
                first = 0
                for n in range(1, len(numbers) + 1):
                    if n == len(numbers) or numbers[n] != numbers[n - 1] + 1:
                        nc_range = range(numbers[first], numbers[n - 1] + 1)
                        pool.sem_clear(nc_range)
                        first = n


def load_and_split(nc, k, block_name, parts):
    loaded, high_ready = k.sem("w_loaded"), k.sem("w_high")
    with k.block() as block:
        @block.sync
        def _(sp):
            for dram, stage, _, _ in parts:
                sp.dma_start(stage, dram).then_inc(loaded, 16)
            sp.wait_ge(loaded, 16 * len(parts))

        @block.vector
        def _(dve):
            dve.wait_ge(loaded, 16 * len(parts))
            n = 0
            for _, stage, high, low in parts:
                if high is None:
                    continue
                nc.vector.tensor_copy(high, stage).then_inc(high_ready, 1)
                n += 1
                if low is not None:
                    dve.wait_ge(high_ready, n)
                    nc.vector.tensor_tensor(low, stage, high.bitcast(FP32), ALU.subtract)


def layer_norm(nc, layer, c, src, dst, eps=0):
    with ExitStack() as stack:
        k = Scope(nc, stack, layer)
        centred = [k.bank(f"centred{i}") for i in range(2)]
        var = [k.bank(f"var{i}") for i in range(2)]
        sq = k.sb("sq", [P, 2, UNIT])
        lnv = k.sb("lnv", [P, UNIT])
        rstd = k.sb("rstd", [P, 2, UNIT])
        centred_done, sq_ready, var_done, ln_ready, rstd_ready, x_ready = (
            k.sem(n) for n in ("centred_done", "sq_ready", "var_done", "ln_ready", "rstd_ready", "x_ready"))
        block = stack.enter_context(k.block())

        def tokens(buf, n):
            return buf[:, bass.ds(n * UNIT, UNIT)]

        @block.tensor
        def _(pe):
            def step(i, s):
                n, b = 2 * i + s, s % 2
                if live(n, UNITS):
                    hold(pe, x_ready, n - 1)
                    nc.tensor.matmul(centred[b][:, :], c.centre[:, :], tokens(src, n),
                                     start=True, stop=True).then_inc(centred_done, 1)
                if live(n - 1, UNITS):
                    hold(pe, sq_ready, n)
                    hold(pe, ln_ready, n - 2)
                    nc.tensor.matmul(var[1 - b][:, :], c.mean[:, :], sq[:, 1 - b, :],
                                     start=True, stop=True).then_inc(var_done, 1)
            sweep(pe, 2, 0, 2, UNITS // 2, UNITS // 2 + 1, step)

        @block.scalar
        def _(act):
            def step(i, s):
                n, b = 2 * i + s, s % 2
                if live(n, UNITS):
                    hold(act, var_done, n - 1)
                    act.wait_ge(centred_done, n + 1)
                    nc.scalar.activation(sq[:, b, :], centred[b][:, :], ACT.Square).then_inc(sq_ready, 1)
                if live(n - 1, UNITS):
                    hold(act, rstd_ready, n - 1)
                    act.wait_ge(var_done, n)
                    nc.scalar.activation(lnv[:, :], var[1 - b][:, :], ACT.Ln, bias=c.eps[:, eps:eps + 1]).then_inc(ln_ready, 1)
                    hold(act, x_ready, n - 2)
                    act.wait_ge(ln_ready, n)
                    nc.scalar.activation(rstd[:, 1 - b, :], lnv[:, :], ACT.Exp, scale=-0.5).then_inc(rstd_ready, 1)
            sweep(act, 2, 0, 2, UNITS // 2, UNITS // 2 + 1, step)

        @block.vector
        def _(dve):
            def step(i, s):
                n, b = 2 * i + s, s % 2
                if live(n - 1, UNITS):
                    dve.wait_ge(rstd_ready, n)
                    nc.vector.tensor_tensor(tokens(dst, n - 1), centred[1 - b][:, :], rstd[:, 1 - b, :],
                                            ALU.mult).then_inc(x_ready, 1)
            sweep(dve, 2, 0, 1, UNITS // 2, UNITS // 2 + 1, step)


class AttentionShape:

    def __init__(self, dim, rows, v_width, scale, biased, v_slots, o_tiles, low_cols):
        self.dim, self.rows, self.v_width, self.scale, self.biased = dim, rows, v_width, scale, biased
        self.v_slots, self.o_tiles, self.low_cols = v_slots, o_tiles, low_cols
        self.n_tiles = 16 * rows // P
        self.heads_per_tile = P // rows
        self.buffers = 4 if rows == P else 2
        self.pv_every = 2 if v_width == 32 else 1


HEADS, STEPS = 16, 8


def attention(nc, layer, c, x, w, a):
    E, R, VW = a.n_tiles, a.rows, a.v_width
    VD = HEADS * a.dim
    KEPT = 4
    with ExitStack() as stack:
        k = Scope(nc, stack, layer)
        wq = [k.sb(f"wq{p}", [P, E * P], F32R) for p in range(2)]
        wk = [k.sb(f"wk{p}", [P, E * P], F32R) for p in range(2)]
        wv = [k.sb(f"wv{p}", [P, VD], F32R) for p in range(2)]
        wo = k.sb("wo", [P, a.o_tiles, P])
        fbias = k.sb("fbias", [P, 1])
        if a.biased:
            aug = [k.sb(f"aug_{n}", [3, E * P], F32R) for n in "qk"]
        with ExitStack() as staging:
            ks = Scope(nc, staging, layer + "_s")
            sq_, sk_, sv_ = ks.sb("q", [P, E * P]), ks.sb("k", [P, E * P]), ks.sb("v", [P, VD])
            parts = [(w["wq"], sq_[:, :], wq[0][:, :], wq[1][:, :]), (w["wk"], sk_[:, :], wk[0][:, :], wk[1][:, :]),
                     (w["wv"], sv_[:, :], wv[0][:, :], wv[1][:, :]), (w["wo"], wo[:, :, :], None, None)]
            if a.biased:
                raw_aug = [ks.sb(f"a{n}", [3, E * P]) for n in "qk"]
                t_aug = ks.sb("t_aug", [3, E * P], F32R)
                bvp, bo = ks.sb("bvp", [P, 4]), ks.sb("bo", [P, 1])
                parts += [(w["aug_q"], raw_aug[0][:, :], None, None), (w["aug_k"], raw_aug[1][:, :], None, None),
                          (w["bv"], bvp[:, :], None, None), (w["bo"], bo[:, :], None, None)]
            load_and_split(nc, ks, "load", parts)
            if a.biased:
                high, low, summed = ks.sem("aug_high"), ks.sem("aug_low"), ks.sem("bias_summed")
                pb = ks.bank("pb")
                with ks.block() as block:
                    @block.vector
                    def _(dve):
                        for n in range(2):
                            if n > 0:
                                dve.wait_ge(low, n)
                            nc.vector.tensor_scalar(t_aug[:, :], raw_aug[n][:, :], c.aug_low[0:3, 0:1], None,
                                                    ALU.mult).then_inc(high, 1)
                            dve.wait_ge(high, n + 1)
                            nc.vector.tensor_tensor(aug[n][:, :], raw_aug[n][:, :], t_aug[:, :].bitcast(FP32),
                                                    ALU.subtract).then_inc(low, 1)
                        dve.wait_ge(summed, 1)
                        nc.vector.tensor_tensor(fbias[:, :], pb[:, 0:1], bo[:, :], ALU.add)

                    @block.tensor
                    def _(pe):
                        for g in range(4):
                            last = nc.tensor.matmul(pb[:, 0:1], wo[:, g, :], bvp[:, g:g + 1], start=g == 0, stop=g == 3)
                        last.then_inc(summed, 1)

        xs = [k.sb(f"xs{p}", [P, SEQ], F32R) for p in range(2)]
        ops = [k.sb(f"ops{i}", [P, 4, SEQ], F32R) for i in range(a.buffers)]
        top = [k.sb(f"top{i}", [P, 2, 2]) for i in range(2)]
        top_scaled = [k.sb(f"top_scaled{i}", [P, 2, 2]) for i in range(2)]
        total, inv = [k.sb(f"total{i}", [P, 2, 2]) for i in range(2)], [k.sb(f"inv{i}", [P, 2, 2]) for i in range(2)]
        probs = k.sb("probs", [P, KEPT, 2, 3 * HALF])
        probs_t = k.sb("probs_t", [P, KEPT, 2, 3 * HALF])
        vb = k.sb("vb", [P, 2, HEADS, VW])
        ot = k.sb("ot", [P, a.o_tiles, SEQ])

        scores = [k.bank(f"scores{i}", 2) for i in range(2)]
        b_t, b_o = k.bank("b_t"), k.bank("b_o")
        proj = [k.bank(f"proj{i}") for i in range(2)]

        (presets, xs_high, xs_ready, proj_done, t_ready, ops_ready, s_done, top_ready, scaled_ready, exp_ready,
         inv_ready, probs_ready, t_done, pt0_ready, pt1_ready, pv_done, o_ready, v_done, v_ready, f_done, y_ready) = (
            k.sem(n) for n in (
                "presets", "xs_high", "xs_ready", "proj_done", "t_ready", "ops_ready", "s_done", "top_ready",
                "scaled_ready", "exp_ready", "inv_ready", "probs_ready", "t_done", "pt0_ready", "pt1_ready", "pv_done",
                "o_ready", "v_done", "v_ready", "f_done", "y_ready"))
        block = stack.enter_context(k.block())
        F = STEPS // a.pv_every
        NV = len(a.v_slots)
        STEPS_ALL = BATCHES * STEPS
        LAG = a.pv_every + 2

        def events(i, s):
            i, s = i + s // STEPS, s % STEPS
            if E < STEPS:
                return [(E * i + s // 2, s // 2)] if s % 2 == 0 else []
            per = E // STEPS
            return [(E * i + per * s + d, per * s + d) for d in range(per)]

        def events_until(i, s):
            return E * i + (s * E // STEPS if E >= STEPS else s // 2) + max(1, E // STEPS)

        def head(s, hh):
            h = 2 * s + hh
            return ops[h // a.heads_per_tile % a.buffers], slice(h * R % P, h * R % P + R)

        def pv_event(i, s):
            if (s - 3) % a.pv_every != a.pv_every - 1:
                return None
            return F * i + (s - 3 - (a.pv_every - 1)) // a.pv_every

        def pv_until(i, s):
            return F * i + (s - 3 - (a.pv_every - 1)) // a.pv_every + 1

        def pv_of(i, s, n):
            return F * i + s // a.pv_every + 1 if not isinstance(n, int) or n - 2 - KEPT >= 0 else 0

        def run(eng, step):
            sweep(eng, STEPS, -1, 2, BATCHES - 1, BATCHES + 1, step)

        def tri(bank):
            return bank.rearrange("p (b t) -> p b t", t=HALF)[:, 0:4:2, :]

        @block.tensor
        def _(pe):
            pe.wait_ge(presets, 1)

            def transpose(i, s, hh):
                n = STEPS * i + s
                if live(n - 2, STEPS_ALL):
                    if hh == 0:
                        hold(pe, probs_ready, n - 1)
                        hold(pe, pt1_ready, n - 2)
                    else:
                        hold(pe, pt0_ready, n - 1)
                    for b in range(3):
                        last = nc.tensor.transpose(b_t[:, b * P:(b + 1) * P],
                                                   probs[:, (s - 2) % KEPT, hh, b * P:(b + 1) * P], c.ident[:, :])
                    last.then_inc(t_done, 1)

            def step(i, s):
                n = STEPS * i + s
                if s == 3 and live(i - 1, BATCHES):
                    hold(pe, o_ready, F * i)
                    hold(pe, v_ready, NV * i + sum(v < 3 for v in a.v_slots) * live(i, BATCHES))
                    for g in range(a.o_tiles):
                        last = nc.tensor.matmul(b_o[:, 0:SEQ], wo[:, g, :], ot[:, g, :], start=g == 0,
                                                stop=g == a.o_tiles - 1)
                    last.then_inc(f_done, 1)
                if live(n, STEPS_ALL):
                    hold(pe, exp_ready, n - 1)
                    hold(pe, ops_ready, events_until(i, s))
                    for hh in range(2):
                        nc.tensor.matmul(tri(scores[s % 2][:, hh * BANK:(hh + 1) * BANK]), c.ident_b[:, :],
                                         c.mask_q[:, :, :], start=True, stop=True, skip_group_check=True)
                    for hh in range(2):
                        op, rows = head(s, hh)
                        bank = scores[s % 2][:, hh * BANK:(hh + 1) * BANK]
                        for qb in range(2):
                            for key in ((1, 3) if R == P else (3,)):
                                last = nc.tensor.matmul(bank[:, qb * HALF:HALF + qb * SEQ], op[rows, 2, qb * HALF:(qb + 1) * HALF],
                                                        op[rows, key, 0:(qb + 1) * HALF], start=False, stop=True,
                                                        skip_group_check=True)
                    last.then_inc(s_done, 1)
                transpose(i, s, 0)
                if live(n + 1, STEPS_ALL):
                    for e, tile in events(i, s + 1):
                        hold(pe, xs_ready, i + (2 if s == STEPS - 1 else 1))
                        hold(pe, ops_ready, e - 1)
                        bank = proj[tile % 2]
                        cols = slice(tile * P, (tile + 1) * P)
                        for q, wt in enumerate((wq, wk)):
                            out = bank[:, q * SEQ:(q + 1) * SEQ]
                            for m, (wi, xi) in enumerate(((0, 0), (0, 1), (1, 0))):
                                last = nc.tensor.matmul(out, wt[wi][:, cols], xs[xi][:, :], start=m == 0 and q == 0,
                                                        stop=m == 2, skip_group_check=True)
                            if a.biased:
                                last = nc.tensor.matmul(out, aug[q][0:3, cols], c.aug_x[0:3, :], start=False, stop=True,
                                                        skip_group_check=True)
                        last.then_inc(proj_done, 1)
                transpose(i, s, 1)
                f = pv_event(i, s)
                if f is not None and live(n - LAG, STEPS_ALL):
                    hold(pe, pt0_ready, n - 2)
                    hold(pe, pt1_ready, n - 2)
                    hold(pe, v_ready, NV * i + sum(v < s for v in a.v_slots) * live(i, BATCHES))
                    hold(pe, o_ready, f)
                    if s >= 3:
                        hold(pe, y_ready, i)
                    heads = [(2 * ((s - 3 - d) % STEPS) + hh, (s - 3 - d) % KEPT, hh)
                             for d in range(a.pv_every - 1, -1, -1) for hh in range(2)]
                    for kb in range(2):
                        for g, (h, kept, hh) in enumerate(heads):
                            last = nc.tensor.matmul(b_o[g * VW:(g + 1) * VW, kb * HALF:SEQ], vb[:, kb, h, :],
                                                    probs_t[:, kept, hh, kb * SEQ:kb * SEQ + SEQ - kb * HALF],
                                                    start=kb == 0, stop=kb == 1, skip_group_check=True)
                    last.then_inc(pv_done, 1)
                if s in a.v_slots and live(i, BATCHES):
                    j = a.v_slots.index(s)
                    hold(pe, xs_ready, i + 1)
                    hold(pe, v_ready, NV * i + j)
                    hold(pe, o_ready, pv_until(i, s))
                    hold(pe, y_ready, i if s >= 3 else i - 1)
                    first, width, tbs = v_chunk(a, j)
                    for q, tb in enumerate(tbs):
                        out = b_o[:, q * width:(q + 1) * width]
                        for m, (xi, wi) in enumerate(((0, 0), (1, 0), (0, 1))):
                            last = nc.tensor.matmul(out, xs[xi][:, tb * HALF:(tb + 1) * HALF],
                                                    wv[wi][:, first * a.dim:first * a.dim + width],
                                                    start=m == 0 and q == 0, stop=m == 2, skip_group_check=True)
                    last.then_inc(v_done, 1)
            run(pe, step)

        @block.gpsimd
        def _(pool):
            nc.gpsimd.memset(vb[:, :, :, :], 0.0).then_inc(presets, 1)

            def step(i, s):
                n = STEPS * i + s
                if live(n - 1, STEPS_ALL):
                    hold(pool, inv_ready, n)
                    kept, scale = (s - 1) % KEPT, inv[(s - 1) % 2]
                    nc.gpsimd.tensor_tensor(probs[:, kept, :, 0:HALF], probs[:, kept, :, 0:HALF],
                                            scale[:, 0, :].unsqueeze(2).to_broadcast([P, 2, HALF]), ALU.mult)
                    nc.gpsimd.tensor_tensor(probs[:, kept, :, HALF:3 * HALF], probs[:, kept, :, HALF:3 * HALF],
                                            scale[:, 1, :].unsqueeze(2).to_broadcast([P, 2, SEQ]),
                                            ALU.mult).then_inc(probs_ready, 1)
            run(pool, step)

        @block.scalar
        def _(act):
            act.wait_ge(presets, 1)

            def step(i, s):
                n = STEPS * i + s
                if live(n - 1, STEPS_ALL):
                    hold(act, scaled_ready, n)
                    hold(act, t_done, 2 * (n - 1 - KEPT + 1))
                    hold(act, inv_ready, n - 2)
                    for hh in range(2):
                        for qb in range(2):
                            cols = slice(qb * HALF, HALF + qb * SEQ)
                            last = nc.scalar.activation(probs[:, (s - 1) % KEPT, hh, cols],
                                                        scores[(s - 1) % 2][:, hh * BANK + cols.start:hh * BANK + cols.stop],
                                                        ACT.Exp, bias=top_scaled[(s - 1) % 2][:, qb, hh:hh + 1], scale=a.scale,
                                                        accum_out=total[(s - 1) % 2][:, qb, hh:hh + 1])
                    last.then_inc(exp_ready, 1)
                if live(n - 2, STEPS_ALL):
                    hold(act, t_done, 2 * (n - 2) + 1)
                    hold(act, pv_done, pv_of(i, s - 2 - KEPT, n))
                    nc.scalar.activation(probs_t[:, (s - 2) % KEPT, 0, :], b_t[:, 0:3 * HALF], ACT.Copy).then_inc(pt0_ready, 1)
                if live(n + 1, STEPS_ALL):
                    for e, tile in events(i, s + 1):
                        hold(act, proj_done, e + 1)
                        hold(act, s_done, n - 1 if E < STEPS else n)
                        op, bank = ops[tile % a.buffers], proj[tile % 2]
                        for q in range(2):
                            last = nc.scalar.activation(op[:, q, :], bank[:, q * SEQ:(q + 1) * SEQ], ACT.Copy,
                                                        scale=c.low_rows[:, a.low_cols[q]:a.low_cols[q] + 1])
                        last.then_inc(t_ready, 1)
                if s in a.v_slots and live(i, BATCHES):
                    j = a.v_slots.index(s)
                    first, width, tbs = v_chunk(a, j)
                    act.wait_ge(v_done, NV * i + j + 1)
                    hold(act, pv_done, F * i - (F // 2 if NV == 4 and j < 2 else 0))
                    nc.scalar.activation(vb[:, tbs[0]:tbs[-1] + 1, first:first + width // a.dim, 0:a.dim],
                                         b_o[:, 0:len(tbs) * width].rearrange("p (b h d) -> p b h d", b=len(tbs), d=a.dim),
                                         ACT.Copy).then_inc(v_ready, 1)
            run(act, step)

        @block.vector
        def _(dve):
            def step(i, s):
                n = STEPS * i + s
                if s == 3 and live(i - 1, BATCHES):
                    hold(dve, f_done, i)
                    xb = x[:, bass.ds((i - 1) * SEQ, SEQ)]
                    if a.biased:
                        last = nc.vector.scalar_tensor_tensor(xb, b_o[:, 0:SEQ], fbias[:, 0:1], xb, ALU.add, ALU.add)
                    else:
                        last = nc.vector.tensor_tensor(xb, b_o[:, 0:SEQ], xb, ALU.add)
                    last.then_inc(y_ready, 1)
                if live(n, STEPS_ALL):
                    mine = top[s % 2]
                    banks = scores[s % 2][:, :].rearrange("p (h t) -> p h t", t=BANK)
                    dve.wait_ge(s_done, n + 1)
                    hold(dve, exp_ready, n - 1)
                    hold(dve, scaled_ready, n - 1)
                    nc.vector.tensor_reduce(mine[:, 0, :], banks[:, :, 0:HALF], AX.X, ALU.max, negate=True)
                    nc.vector.tensor_reduce(mine[:, 1, :], banks[:, :, HALF:3 * HALF], AX.X, ALU.max,
                                            negate=True).then_inc(top_ready, 1)
                    dve.wait_ge(top_ready, n + 1)
                    nc.vector.tensor_scalar(top_scaled[s % 2][:, :, :], mine[:, :, :], a.scale, None,
                                            ALU.mult).then_inc(scaled_ready, 1)
                if s == STEPS - 1 and live(i + 1, BATCHES):
                    hold(dve, proj_done, E * (i + 1))
                    hold(dve, v_done, NV * (i + 1))
                    xb = x[:, bass.ds((i + 1) * SEQ, SEQ)]
                    nc.vector.tensor_scalar(xs[0][:, :], xb, 1.0, None, ALU.mult).then_inc(xs_high, 1)
                    hold(dve, xs_high, i + 2)
                    nc.vector.tensor_tensor(xs[1][:, :], xb, xs[0][:, :].bitcast(FP32), ALU.subtract).then_inc(xs_ready, 1)
                if live(n - 1, STEPS_ALL):
                    hold(dve, exp_ready, n)
                    hold(dve, probs_ready, n - 2)
                    nc.vector.reciprocal(inv[(s - 1) % 2][:, :, :], total[(s - 1) % 2][:, :, :]).then_inc(inv_ready, 1)
                if live(n + 1, STEPS_ALL):
                    for e, tile in events(i, s + 1):
                        op = ops[tile % a.buffers]
                        dve.wait_ge(t_ready, e + 1)
                        nc.vector.tensor_tensor(op[:, 2:4, :], proj[tile % 2][:, :].rearrange("p (q t) -> p q t", t=SEQ),
                                                op[:, 0:2, :].bitcast(FP32), ALU.subtract).then_inc(ops_ready, 1)
                if live(n - 2, STEPS_ALL):
                    hold(dve, t_done, 2 * (n - 1))
                    hold(dve, pv_done, pv_of(i, s - 2 - KEPT, n))
                    nc.vector.tensor_copy(probs_t[:, (s - 2) % KEPT, 1, :], b_t[:, 0:3 * HALF]).then_inc(pt1_ready, 1)
                f = pv_event(i, s)
                if f is not None and live(n - LAG, STEPS_ALL):
                    g = ((s - LAG) % STEPS) // a.pv_every
                    hold(dve, pv_done, f + 1)
                    hold(dve, f_done, i if s >= LAG else i - 1)
                    nc.vector.tensor_copy(ot[:, g, :], b_o[:, 0:SEQ]).then_inc(o_ready, 1)
            run(dve, step)


def v_chunk(a, j):
    if len(a.v_slots) == 1:
        return 0, HEADS * a.dim, (0, 1)
    return j // 2 * 8, HEADS * a.dim // 2, (j % 2,)


def reglu(nc, layer, c, x, w):
    with ExitStack() as stack:
        k = Scope(nc, stack, layer)
        wm = k.sb("wm", [P, 2, 2, 2, P], F32R)
        wv = k.sb("wv", [P, P])
        with ExitStack() as staging:
            ks = Scope(nc, staging, layer + "_s")
            raw, mu = ks.sb("raw", [P, 2, P]), ks.sb("mu", [P, 2])
            rest, mixed = ks.sb("rest", [P, 2]), ks.sb("mixed", [P, 2, 2, P])
            loaded, rest_ready, mixed_ready, high_ready = (
                ks.sem(n) for n in ("loaded", "rest_ready", "mixed_ready", "high_ready"))
            with ks.block() as block:
                @block.sync
                def _(sp):
                    for dst, src in ((raw[:, :, :], w["w"]), (mu[:, :], w["mu"]), (wv[:, :], w["wv"])):
                        sp.dma_start(dst, src).then_inc(loaded, 16)

                @block.vector
                def _(dve):
                    dve.wait_ge(loaded, 48)
                    nc.vector.tensor_scalar(rest[:, :], mu[:, :], -1.0, 1.0, ALU.mult, ALU.add).then_inc(rest_ready, 1)
                    dve.wait_ge(rest_ready, 1)
                    for m in range(2):
                        for t, share in enumerate((mu, rest)):
                            nc.vector.tensor_scalar(mixed[:, m, t, :], raw[:, m, :], share[:, m:m + 1], None,
                                                    ALU.mult).then_inc(mixed_ready, 1)
                    dve.wait_ge(mixed_ready, 4)
                    nc.vector.tensor_copy(wm[:, :, :, 0, :], mixed[:, :, :, :]).then_inc(high_ready, 1)
                    dve.wait_ge(high_ready, 1)
                    nc.vector.tensor_tensor(wm[:, :, :, 1, :], mixed[:, :, :, :], wm[:, :, :, 0, :].bitcast(FP32), ALU.subtract)

        xs = [[k.sb(f"xs{b}{p}", [P, 2, SEQ + 1], F32R) for p in range(2)] for b in range(2)]
        kr = k.sb("kr", [P, UNIT])
        kk = [k.sb(f"kk{b}", [P, UNIT]) for b in range(2)]
        sg = [k.sb(f"sg{b}", [P, UNIT]) for b in range(2)]
        gated = k.sb("gated", [P, UNIT])
        b_k, b_r, b_v = k.bank("b_k"), k.bank("b_r"), k.bank("b_v")
        presets, xs_high, xs_ready, k_done, r_done, kr_ready, kk_ready, sg_ready, v_done, gated_ready, y_ready = (
            k.sem(n) for n in ("presets", "xs_high", "xs_ready", "k_done", "r_done", "kr_ready", "kk_ready", "sg_ready",
                               "v_done", "gated_ready", "y_ready"))
        block = stack.enter_context(k.block())

        def run(eng, step):
            sweep(eng, 2, -1, 2, UNITS // 2 - 1, UNITS // 2 + 1, step)

        @block.gpsimd
        def _(pool):
            for b in range(2):
                for p in range(2):
                    nc.gpsimd.memset(xs[b][p][:, :, 0:1].bitcast(FP32), 0.0).then_inc(presets, 1)

        @block.tensor
        def _(pe):
            pe.wait_ge(presets, 4)

            def step(i, s):
                n, b = 2 * i + s, s % 2
                if live(n, UNITS):
                    hold(pe, xs_ready, n + 1)
                    for m, bank, done in ((1, b_k, k_done), (0, b_r, r_done)):
                        hold(pe, kk_ready if m else sg_ready, n)
                        q = 0
                        for t, off in ((0, 1), (1, 0)):
                            for wi, xi in ((0, 0), (0, 1), (1, 0)):
                                last = nc.tensor.matmul(bank[:, :], wm[:, m, t, wi, :], xs[b][xi][:, :, off:off + SEQ],
                                                        start=q == 0, stop=q == 5)
                                q += 1
                        last.then_inc(done, 1)
                if live(n - 1, UNITS):
                    hold(pe, kk_ready, n)
                    hold(pe, gated_ready, n - 1)
                    nc.tensor.matmul(b_v[:, :], wv[:, :], kk[1 - b][:, :], start=True, stop=True).then_inc(v_done, 1)
            run(pe, step)

        @block.scalar
        def _(act):
            def step(i, s):
                n, b = 2 * i + s, s % 2
                if live(n, UNITS):
                    hold(act, k_done, n + 1)
                    hold(act, kk_ready, n)
                    nc.scalar.activation(kr[:, :], b_k[:, :], ACT.Relu).then_inc(kr_ready, 1)
                    hold(act, r_done, n + 1)
                    hold(act, gated_ready, n - 1)
                    nc.scalar.activation(sg[b][:, :], b_r[:, :], ACT.Sigmoid).then_inc(sg_ready, 1)
            run(act, step)

        @block.vector
        def _(dve):
            def step(i, s):
                n, b = 2 * i + s, s % 2
                if live(n + 1, UNITS):
                    hold(dve, r_done, n)
                    xb = x[:, bass.ds((n + 1) * UNIT, UNIT)].rearrange("p (b t) -> p b t", t=SEQ)
                    high, low = xs[1 - b][0][:, :, 1:SEQ + 1], xs[1 - b][1][:, :, 1:SEQ + 1]
                    nc.vector.tensor_scalar(high, xb, 1.0, None, ALU.mult).then_inc(xs_high, 1)
                    hold(dve, xs_high, n + 2)
                    nc.vector.tensor_tensor(low, xb, high.bitcast(FP32), ALU.subtract).then_inc(xs_ready, 1)
                if live(n, UNITS):
                    hold(dve, kr_ready, n + 1)
                    hold(dve, v_done, n - 1)
                    nc.vector.tensor_tensor(kk[b][:, :], b_k[:, :], kr[:, :], ALU.mult).then_inc(kk_ready, 1)
                if live(n - 1, UNITS):
                    hold(dve, sg_ready, n)
                    hold(dve, v_done, n)
                    hold(dve, y_ready, n - 1)
                    nc.vector.tensor_tensor(gated[:, :], b_v[:, :], sg[1 - b][:, :], ALU.mult).then_inc(gated_ready, 1)
                    hold(dve, gated_ready, n)
                    xb = x[:, bass.ds((n - 1) * UNIT, UNIT)]
                    nc.vector.tensor_tensor(xb, gated[:, :], xb, ALU.add).then_inc(y_ready, 1)
            run(dve, step)


def mlp(nc, layer, c, src, x, w1, w2, kind, b1, out_scale, out_bias):
    M = 4
    with ExitStack() as stack:
        k = Scope(nc, stack, layer)
        xs = [[k.sb(f"xs{b}{p}", [P, UNIT], F32R) for p in range(2)] for b in range(2)]
        hid = k.sb("hid", [P, M, UNIT])
        relu = k.sb("relu", [P, 2, UNIT])
        b_h = [k.bank(f"b_h{m}") for m in range(M)]
        b_z = [k.bank(f"b_z{m}") for m in range(2)]
        xs_high, xs_ready, h_done, relu_ready, hid_ready, z_done, y_ready = (
            k.sem(n) for n in ("xs_high", "xs_ready", "h_done", "relu_ready", "hid_ready", "z_done", "y_ready"))
        block = stack.enter_context(k.block())

        def run(eng, step):
            sweep(eng, 2, -1, 2, UNITS // 2 - 1, UNITS // 2 + 1, step)

        @block.tensor
        def _(pe):
            def step(i, s):
                n, b = 2 * i + s, s % 2
                if live(n - 1, UNITS):
                    hold(pe, y_ready, n - 2)
                    for m in range(M):
                        hold(pe, hid_ready, M * (n - 1) + m + 1)
                        last = nc.tensor.matmul(b_z[1 - b][:, :], w2[:, m, :], hid[:, m, :], start=m == 0, stop=m == M - 1)
                    last.then_inc(z_done, 1)
                if live(n, UNITS):
                    hold(pe, xs_ready, n + 1)
                    for m in range(M):
                        hold(pe, hid_ready, M * (n - 1) + m + 1)
                        for q, (wi, xi) in enumerate(((0, 0), (0, 1), (1, 0))):
                            last = nc.tensor.matmul(b_h[m][:, :], w1[wi][:, m * P:(m + 1) * P], xs[b][xi][:, :],
                                                    start=q == 0, stop=q == 2)
                        last.then_inc(h_done, 1)
            run(pe, step)

        @block.scalar
        def _(act):
            def step(i, s):
                n, b = 2 * i + s, s % 2
                if live(n, UNITS):
                    for m in range(M):
                        hold(act, h_done, M * n + m + 1)
                        if kind == "silu":
                            hold(act, z_done, n)
                            nc.scalar.activation(hid[:, m, :], b_h[m][:, :], ACT.Silu, bias=b1[:, m:m + 1])\
                                .then_inc(hid_ready, 1)
                        else:
                            hold(act, hid_ready, M * n + m - 1)
                            nc.scalar.activation(relu[:, m % 2, :], b_h[m][:, :], ACT.Relu).then_inc(relu_ready, 1)
            run(act, step)

        @block.vector
        def _(dve):
            def step(i, s):
                n, b = 2 * i + s, s % 2
                if live(n + 1, UNITS):
                    hold(dve, h_done, M * n)
                    xb = src[:, bass.ds((n + 1) * UNIT, UNIT)]
                    nc.vector.tensor_scalar(xs[1 - b][0][:, :], xb, 1.0, None, ALU.mult).then_inc(xs_high, 1)
                    hold(dve, xs_high, n + 2)
                    nc.vector.tensor_tensor(xs[1 - b][1][:, :], xb, xs[1 - b][0][:, :].bitcast(FP32),
                                            ALU.subtract).then_inc(xs_ready, 1)
                if live(n - 1, UNITS):
                    hold(dve, z_done, n)
                    xb = x[:, bass.ds((n - 1) * UNIT, UNIT)]
                    if out_bias is None:
                        nc.vector.scalar_tensor_tensor(xb, b_z[1 - b][:, :], out_scale[:, 0:1], xb, ALU.mult, ALU.add)\
                            .then_inc(y_ready, 1)
                    else:
                        nc.vector.scalar_tensor_tensor(xb, b_z[1 - b][:, :], out_bias[:, 0:1], xb, ALU.add, ALU.add)\
                            .then_inc(y_ready, 1)
                if live(n, UNITS) and kind == "relu2":
                    for m in range(M):
                        hold(dve, relu_ready, M * n + m + 1)
                        hold(dve, z_done, n)
                        nc.vector.tensor_tensor(hid[:, m, :], b_h[m][:, :], relu[:, m % 2, :], ALU.mult)\
                            .then_inc(hid_ready, 1)
            run(dve, step)


def quantised_mlp(nc, c, x, w):
    layer = "l1f"
    with ExitStack() as stack:
        k = Scope(nc, stack, layer)
        w1 = [k.sb(f"w1{p}", [P, 4 * P], F32R) for p in range(2)]
        w2 = k.sb("w2", [P, 4, P])
        b1, b2 = k.sb("b1", [P, 4]), k.sb("b2", [P, 1])
        with ExitStack() as staging:
            ks = Scope(nc, staging, layer + "_s")
            q1, q2 = ks.sb("q1", [P, 4 * P], I32), ks.sb("q2", [P, 4, P], I32)
            s1, s2 = ks.sb("s1", [P, 4 * P]), ks.sb("s2", [P, 4, P])
            b1_raw, gamma, beta, b2_raw = ks.sb("b1r", [P, 4]), ks.sb("gamma", [P, 1]), ks.sb("beta", [P, 1]), ks.sb("b2r", [P, 1])
            d1, d2, full = ks.sb("d1", [P, 4 * P]), ks.sb("d2", [P, 4, P]), ks.sb("full", [P, 4 * P])
            pb = ks.bank("pb")
            loaded, chain, beta_done = ks.sem("loaded"), ks.sem("dequantised"), ks.sem("beta_done")
            pairs = ((q1[:, :], "fc1_q"), (q2[:, :, :], "fc2_q"), (s1[:, :], "fc1_s"), (s2[:, :, :], "fc2_s"),
                     (b1_raw[:, :], "b1"), (gamma[:, :], "gamma"), (beta[:, :], "beta"), (b2_raw[:, :], "b2"))
            with ks.block() as block:
                @block.sync
                def _(sp):
                    for dst, name in pairs:
                        sp.dma_start(dst, w[name]).then_inc(loaded, 16)

                @block.vector
                def _(dve):
                    dve.wait_ge(loaded, 16 * len(pairs))
                    nc.vector.tensor_scalar(d1[:, :], q1[:, :], -128.0, None, ALU.add).then_inc(chain, 1)
                    nc.vector.tensor_scalar(d2[:, :, :], q2[:, :, :], -128.0, 0.25, ALU.add, ALU.mult).then_inc(chain, 1)
                    nc.vector.tensor_scalar(b2[:, :], b2_raw[:, :], 0.25, None, ALU.mult)
                    dve.wait_ge(chain, 2)
                    nc.vector.tensor_tensor(full[:, :], d1[:, :], s1[:, :], ALU.mult).then_inc(chain, 1)
                    nc.vector.tensor_tensor(w2[:, :, :], d2[:, :, :], s2[:, :, :], ALU.mult)
                    dve.wait_ge(chain, 3)
                    nc.vector.tensor_scalar(s1[:, :], full[:, :], gamma[:, 0:1], None, ALU.mult).then_inc(chain, 1)
                    dve.wait_ge(chain, 4)
                    nc.vector.tensor_copy(w1[0][:, :], s1[:, :]).then_inc(chain, 1)
                    dve.wait_ge(chain, 5)
                    nc.vector.tensor_tensor(w1[1][:, :], s1[:, :], w1[0][:, :].bitcast(FP32), ALU.subtract)
                    dve.wait_ge(beta_done, 1)
                    nc.vector.tensor_tensor(b1[:, :], pb[:, 0:4], b1_raw[:, :], ALU.add)

                @block.tensor
                def _(pe):
                    pe.wait_ge(chain, 3)
                    for m in range(4):
                        last = nc.tensor.matmul(pb[:, m:m + 1], full[:, m * P:(m + 1) * P], beta[:, 0:1], start=m == 0,
                                                stop=True, skip_group_check=True)
                    last.then_inc(beta_done, 1)
        h = k.sb("h", [P, TOKENS])
        layer_norm(nc, layer + "n", c, x, h)
        mlp(nc, layer, c, h, x, w1, w2, "silu", b1, None, b2)


ROUND = 1.5 * 2.0 ** 23


def ternary_mlp(nc, c, x, w):
    layer = "l3f"
    with ExitStack() as stack:
        k = Scope(nc, stack, layer)
        w1 = [k.sb(f"w1{p}", [P, 4 * P], F32R) for p in range(2)]
        w2 = k.sb("w2", [P, 4, P])
        scale2 = k.sb("scale2", [P, 1])
        with ExitStack() as staging:
            ks = Scope(nc, staging, layer + "_s")
            fc, proj = ks.sb("fc", [P, 4 * P]), ks.sb("proj", [P, 4 * P])
            size_fc, size_proj = ks.sb("size_fc", [P, 4 * P]), ks.sb("size_proj", [P, 4 * P])
            scale, inverse = ks.sb("scale", [P, 5 * P]), ks.sb("inverse", [P, 5 * P])
            r1, r2, low_rank = ks.sb("r1", [P, 4 * P]), ks.sb("r2", [P, 4 * P]), ks.sb("low_rank", [P, 4 * P])
            bt, v, ut, bv = ks.sb("bt", [16, 16]), ks.sb("v", [16, P]), ks.sb("ut", [16, 4 * P]), ks.sb("bv", [16, P])
            gate = ks.sb("gate", [P, 1])
            b_fc, b_proj, b_col, b_bv, b_low = (ks.bank("b_" + n) for n in ("fc", "proj", "col", "bv", "low"))
            loaded, sizes, means, bv_done, bv_ready, low_done, chain = (
                ks.sem("s_" + n) for n in ("loaded", "sizes", "means", "bv_done", "bv_ready", "low_done", "rounded"))
            pairs = ((fc[:, :], "w_fc"), (proj[:, :], "w_proj"), (bt[:, :], "bt"), (v[:, :], "v"), (ut[:, :], "ut"),
                     (gate[:, :], "gate"))
            with ks.block() as block:
                @block.sync
                def _(sp):
                    for dst, name in pairs:
                        sp.dma_start(dst, w[name]).then_inc(loaded, 16)

                @block.scalar
                def _(act):
                    act.wait_ge(loaded, 16 * len(pairs))
                    nc.scalar.activation(size_fc[:, :], fc[:, :], ACT.Abs).then_inc(sizes, 1)
                    nc.scalar.activation(size_proj[:, :], proj[:, :], ACT.Abs).then_inc(sizes, 1)

                @block.tensor
                def _(pe):
                    pe.wait_ge(loaded, 16 * len(pairs))
                    nc.tensor.matmul(b_bv[0:16, 0:P], bt[:, :], v[:, :], start=True, stop=True).then_inc(bv_done, 1)
                    pe.wait_ge(sizes, 2)
                    nc.tensor.matmul(b_fc[:, :], c.mean[:, :], size_fc[:, :], start=True, stop=True).then_inc(means, 1)
                    for m in range(4):
                        last = nc.tensor.matmul(b_proj[:, 0:P], c.mean[:, :], size_proj[:, m * P:(m + 1) * P],
                                                start=m == 0, stop=m == 3)
                    last.then_inc(means, 1)
                    for m in range(4):
                        last = nc.tensor.matmul(b_col[:, 0:1], size_proj[:, m * P:(m + 1) * P], c.mean[:, 0:1],
                                                start=m == 0, stop=m == 3)
                    last.then_inc(means, 1)
                    pe.wait_ge(bv_ready, 1)
                    nc.tensor.matmul(b_low[:, :], bv[:, :], ut[:, :], start=True, stop=True).then_inc(low_done, 1)

                @block.vector
                def _(dve):
                    dve.wait_ge(bv_done, 1)
                    nc.vector.tensor_copy(bv[:, :], b_bv[0:16, 0:P]).then_inc(bv_ready, 1)
                    dve.wait_ge(means, 3)
                    nc.vector.tensor_scalar(scale[:, 0:4 * P], b_fc[:, :], 1e-5, None, ALU.max).then_inc(chain, 1)
                    nc.vector.tensor_scalar(scale[:, 4 * P:5 * P], b_proj[:, 0:P], 0.25, 1e-5, ALU.mult, ALU.max).then_inc(chain, 1)
                    nc.vector.tensor_scalar(scale2[:, :], b_col[:, 0:1], 0.25, 1e-5, ALU.mult, ALU.max)
                    dve.wait_ge(chain, 2)
                    nc.vector.reciprocal(inverse[:, :], scale[:, :]).then_inc(chain, 1)
                    dve.wait_ge(chain, 3)
                    nc.vector.tensor_tensor(r1[:, :], fc[:, :], inverse[:, 0:4 * P], ALU.mult).then_inc(chain, 1)
                    for m in range(4):
                        nc.vector.tensor_tensor(r2[:, m * P:(m + 1) * P], proj[:, m * P:(m + 1) * P],
                                                inverse[:, 4 * P:5 * P], ALU.mult).then_inc(chain, 1)
                    dve.wait_ge(chain, 8)
                    for n, (r, t) in enumerate(((r1, size_fc), (r2, size_proj))):
                        nc.vector.tensor_scalar(t[:, :], r[:, :], -1.0, 1.0, ALU.max, ALU.min).then_inc(chain, 1)
                        dve.wait_ge(chain, 9 + 2 * n)
                        nc.vector.tensor_scalar(r[:, :], t[:, :], ROUND, None, ALU.add).then_inc(chain, 1)
                        dve.wait_ge(chain, 10 + 2 * n)
                    nc.vector.tensor_scalar(size_fc[:, :], r1[:, :], -ROUND, None, ALU.add).then_inc(chain, 1)
                    nc.vector.tensor_scalar(w2[:, :, :], r2[:, :].rearrange("p (m o) -> p m o", m=4), -ROUND, None, ALU.add)
                    dve.wait_ge(low_done, 1)
                    nc.vector.tensor_scalar(low_rank[:, :], b_low[:, :], gate[:, 0:1], None, ALU.mult).then_inc(chain, 1)
                    dve.wait_ge(chain, 14)
                    nc.vector.tensor_tensor(r1[:, :], size_fc[:, :], scale[:, 0:4 * P], ALU.mult).then_inc(chain, 1)
                    dve.wait_ge(chain, 15)
                    nc.vector.tensor_tensor(fc[:, :], r1[:, :], low_rank[:, :], ALU.add).then_inc(chain, 1)
                    dve.wait_ge(chain, 16)
                    nc.vector.tensor_copy(w1[0][:, :], fc[:, :]).then_inc(chain, 1)
                    dve.wait_ge(chain, 17)
                    nc.vector.tensor_tensor(w1[1][:, :], fc[:, :], w1[0][:, :].bitcast(FP32), ALU.subtract)
        mlp(nc, layer, c, x, x, w1, w2, "relu2", None, scale2, None)


def gated_mlp(nc, c, x, w):
    layer = "l2f"
    M = 4
    with ExitStack() as stack:
        k = Scope(nc, stack, layer)
        w12 = [k.sb(f"w12{p}", [P, 8 * P], F32R) for p in range(2)]
        wh = [[k.sb(f"wh{n}{p}", [P, 16 * P], F32R) for p in range(2)] for n in range(2)]
        w3 = [k.sb(f"w3{p}", [P, 4 * P], F32R) for p in range(2)]
        scales = k.sb("scales", [P, 17])
        half_s1, half_s12 = k.sb("half_s1", [P, 4]), k.sb("half_s12", [P, 4])
        with ExitStack() as staging:
            ks = Scope(nc, staging, layer + "_s")
            s12 = ks.sb("w12", [P, 8 * P])
            sh = [ks.sb(f"wh{n}", [P, 16 * P]) for n in range(2)]
            s3 = ks.sb("w3", [P, 4 * P])
            load_and_split(nc, ks, "load", [
                (w["w12"], s12[:, :], w12[0][:, :], w12[1][:, :]),
                (w["h1"], sh[0][:, :], wh[0][0][:, :], wh[0][1][:, :]),
                (w["h2"], sh[1][:, :], wh[1][0][:, :], wh[1][1][:, :]),
                (w["w3"], s3[:, :], w3[0][:, :], w3[1][:, :]),
                (w["scales"], scales[:, :], None, None)])
            halved = ks.sem("halved")
            with ks.block() as block:
                @block.vector
                def _(dve):
                    nc.vector.tensor_scalar(half_s1[:, :], scales[:, 0:4], 0.5, None, ALU.mult).then_inc(halved, 1)
                    dve.wait_ge(halved, 1)
                    nc.vector.tensor_tensor(half_s12[:, :], half_s1[:, :], scales[:, 4:8], ALU.mult)

        xs = [[k.sb(f"xs{b}{p}", [P, UNIT], F32R) for p in range(2)] for b in range(2)]
        act_out = [[k.sb(f"act{n}{p}", [P, M, UNIT], F32R) for p in range(2)] for n in range(3)]
        tanh = k.sb("tanh", [P, 2, UNIT])
        half = k.sb("half", [P, 2, UNIT])
        prod = k.sb("prod", [P, 2, UNIT])
        gelu = k.sb("gelu", [P, 2, UNIT])
        b_h = [k.bank(f"b_h{m}") for m in range(2)]
        b_a = [[k.bank(f"b_a{m}{q}") for q in range(2)] for m in range(2)]
        b_z = k.bank("b_z")
        (xs_high, xs_ready, a_done, tanh_ready, half_ready, prod_ready, a_high, a_ready, h_done, gelu_ready, h_high,
         h_ready, z_done, y_ready) = (
            k.sem(n) for n in ("xs_high", "xs_ready", "a_done", "tanh_ready", "half_ready", "prod_ready", "a_high",
                               "a_ready", "h_done", "gelu_ready", "h_high", "h_ready", "z_done", "y_ready"))
        block = stack.enter_context(k.block())
        PASSES = ((0, 0), (0, 1), (1, 0))

        def run(eng, step):
            sweep(eng, 2, -1, 2, UNITS // 2 - 1, UNITS // 2 + 2, step)

        def h1_tiles(n):
            if isinstance(n, int):
                return M * min(max(n - 2, 0), UNITS) + M * min(max(n - 1, 0), UNITS)
            return 2 * M * n - 3 * M

        @block.tensor
        def _(pe):
            def step(i, s):
                n, b = 2 * i + s, s % 2
                if live(n - 3, UNITS):
                    hold(pe, h_ready, h1_tiles(n - 1) + (M if live(n - 3, UNITS) else 0))
                    hold(pe, y_ready, n - 3)
                    q = 0
                    for m in range(M):
                        for wi, xi in PASSES:
                            last = nc.tensor.matmul(b_z[:, :], w3[wi][:, m * P:(m + 1) * P], act_out[2][xi][:, m, :],
                                                    start=q == 0, stop=q == 3 * M - 1)
                            q += 1
                    last.then_inc(z_done, 1)
                done = h1_tiles(n)
                for layer_n, unit in ((1, n - 2), (0, n - 1)):
                    if not live(unit, UNITS):
                        continue
                    if layer_n == 1:
                        hold(pe, h_ready, h1_tiles(n))
                    else:
                        hold(pe, a_ready, M * n)
                    for m in range(M):
                        hold(pe, h_ready, done - 1)
                        q = 0
                        for kt in range(M):
                            for wi, xi in PASSES:
                                last = nc.tensor.matmul(b_h[m % 2][:, :], wh[layer_n][wi][:, (m * M + kt) * P:(m * M + kt + 1) * P],
                                                        act_out[layer_n][xi][:, kt, :], start=q == 0, stop=q == 3 * M - 1)
                                q += 1
                        last.then_inc(h_done, 1)
                        done = done + 1
                if live(n, UNITS):
                    hold(pe, xs_ready, n + 1)
                    for m in range(M):
                        hold(pe, prod_ready, M * n + m - 1)
                        for side in range(2):
                            for q, (wi, xi) in enumerate(PASSES):
                                tile = slice((side * M + m) * P, (side * M + m + 1) * P)
                                last = nc.tensor.matmul(b_a[m % 2][side][:, :], w12[wi][:, tile], xs[b][xi][:, :],
                                                        start=q == 0, stop=q == 2)
                        last.then_inc(a_done, 1)
            run(pe, step)

        @block.scalar
        def _(act):
            def step(i, s):
                n = 2 * i + s
                done = h1_tiles(n)
                for layer_n, unit in ((1, n - 2), (0, n - 1)):
                    if not live(unit, UNITS):
                        continue
                    for m in range(M):
                        hold(act, h_done, done + 1)
                        hold(act, h_ready, done - 1)
                        nc.scalar.activation(gelu[:, m % 2, :], b_h[m % 2][:, :], ACT.Gelu,
                                             scale=scales[:, 8 + 4 * layer_n + m:9 + 4 * layer_n + m]).then_inc(gelu_ready, 1)
                        done = done + 1
                        hold(act, gelu_ready, done)
                        if layer_n == 1:
                            hold(act, z_done, n - 2)
                        else:
                            hold(act, h_done, h1_tiles(n) + (M if live(n - 2, UNITS) else 0))
                        nc.scalar.activation(act_out[layer_n + 1][0][:, m, :], gelu[:, m % 2, :], ACT.Copy)\
                            .then_inc(h_high, 1)
                if live(n, UNITS):
                    for m in range(M):
                        hold(act, a_done, M * n + m + 1)
                        hold(act, half_ready, M * n + m - 1)
                        nc.scalar.activation(tanh[:, m % 2, :], b_a[m % 2][0][:, :], ACT.Tanh,
                                             scale=half_s1[:, m:m + 1]).then_inc(tanh_ready, 1)
                        hold(act, prod_ready, M * n + m + 1)
                        hold(act, h_done, h1_tiles(n + 1))
                        nc.scalar.activation(act_out[0][0][:, m, :], prod[:, m % 2, :], ACT.Copy).then_inc(a_high, 1)
            run(act, step)

        @block.vector
        def _(dve):
            def step(i, s):
                n, b = 2 * i + s, s % 2
                if live(n + 1, UNITS):
                    hold(dve, a_done, M * n)
                    xb = x[:, bass.ds((n + 1) * UNIT, UNIT)]
                    nc.vector.tensor_scalar(xs[1 - b][0][:, :], xb, 1.0, None, ALU.mult).then_inc(xs_high, 1)
                    hold(dve, xs_high, n + 2)
                    nc.vector.tensor_tensor(xs[1 - b][1][:, :], xb, xs[1 - b][0][:, :].bitcast(FP32),
                                            ALU.subtract).then_inc(xs_ready, 1)
                if live(n - 3, UNITS):
                    hold(dve, z_done, n - 2)
                    xb = x[:, bass.ds((n - 3) * UNIT, UNIT)]
                    nc.vector.scalar_tensor_tensor(xb, b_z[:, :], scales[:, 16:17], xb, ALU.mult, ALU.add)\
                        .then_inc(y_ready, 1)
                done = h1_tiles(n)
                for layer_n, unit in ((1, n - 2), (0, n - 1)):
                    if not live(unit, UNITS):
                        continue
                    for m in range(M):
                        hold(dve, h_high, done + 1)
                        nc.vector.tensor_tensor(act_out[layer_n + 1][1][:, m, :], gelu[:, m % 2, :],
                                                act_out[layer_n + 1][0][:, m, :].bitcast(FP32), ALU.subtract)\
                            .then_inc(h_ready, 1)
                        done = done + 1
                if live(n, UNITS):
                    for m in range(M):
                        hold(dve, tanh_ready, M * n + m + 1)
                        nc.vector.scalar_tensor_tensor(half[:, m % 2, :], tanh[:, m % 2, :], 1.0, b_a[m % 2][0][:, :],
                                                       ALU.add, ALU.mult).then_inc(half_ready, 1)
                        hold(dve, half_ready, M * n + m + 1)
                        hold(dve, a_high, M * n + m - 1)
                        nc.vector.scalar_tensor_tensor(prod[:, m % 2, :], b_a[m % 2][1][:, :], half_s12[:, m:m + 1],
                                                       half[:, m % 2, :], ALU.mult, ALU.mult).then_inc(prod_ready, 1)
                        hold(dve, a_high, M * n + m + 1)
                        nc.vector.tensor_tensor(act_out[0][1][:, m, :], prod[:, m % 2, :],
                                                act_out[0][0][:, m, :].bitcast(FP32), ALU.subtract).then_inc(a_ready, 1)
            run(dve, step)


def chunked_attention(nc, c, x, w):
    layer = "l3a"
    H, CHUNK = 8, 64
    WIDTH = H * P
    PAIRS = H // 2
    with ExitStack() as stack:
        k = Scope(nc, stack, layer)
        wqkv = [[k.sb(f"w{n}{p}", [P, WIDTH], F32R) for p in range(2)] for n in ("q", "k", "v")]
        wg = [k.sb(f"wg{p}", [P, H], F32R) for p in range(2)]
        wo = k.sb("wo", [P, H, P])
        bg, gain = k.sb("bg", [P, H]), k.sb("gain", [P, 1])
        between = k.sb("between", [P, 3, P])
        first_half = k.sb("first_half", [P, 1])
        mask = k.sb("mask", [P, H, CHUNK], BF16)
        with ExitStack() as staging:
            ks = Scope(nc, staging, layer + "_s")
            raw = [ks.sb(f"raw{n}", [P, WIDTH]) for n in range(3)]
            rawg, rawm = ks.sb("rawg", [P, H]), ks.sb("rawm", [P, CHUNK])
            load_and_split(nc, ks, "load",
                           [(w[name], raw[n][:, :], wqkv[n][0][:, :], wqkv[n][1][:, :]) for n, name in enumerate(("wq", "wk", "wv"))]
                           + [(w["wg"], rawg[:, :], wg[0][:, :], wg[1][:, :]), (w["wo"], wo[:, :, :], None, None),
                              (w["bg"], bg[:, :], None, None), (w["gain"], gain[:, :], None, None),
                              (w["between"], between[:, :, :], None, None), (w["first_half"], first_half[:, :], None, None),
                              (w["mask"], rawm[:, :], None, None)])
            with ks.block() as block:
                @block.vector
                def _(dve):
                    for h in range(H):
                        nc.vector.tensor_copy(mask[:, h, :], rawm[:, :])

        xs = [k.sb(f"xs{p}", [P, SEQ], F32R) for p in range(2)]
        sq = k.sb("sq", [P, WIDTH])
        ss, ln_ss, rms = k.sb("ss", [P, H]), k.sb("ln_ss", [P, H]), k.sb("rms", [P, H])
        rms_gain = k.sb("rms_gain", [P, H])
        qkn = [k.sb(f"qkn{n}", [P, WIDTH]) for n in range(4)]
        vt = k.sb("vt", [P, 2, WIDTH])
        qt, kt = k.sb("qt", [P, H, SEQ]), k.sb("kt", [P, H, SEQ])
        z, ze, lg = k.sb("z", [P, 2, H]), k.sb("ze", [P, 2, H]), k.sb("lg", [P, 2, H])
        decay = k.sb("decay", [P, 3, H])
        centred, probs = k.sb("centred", [P, H, CHUNK]), k.sb("probs", [P, H, CHUNK])
        top, total, inv = k.sb("top", [P, H]), k.sb("total", [P, H]), k.sb("inv", [P, H])
        pn = [k.sb(f"pn{tb}", [P, H, P]) for tb in range(2)]
        ptt = k.sb("ptt", [P, H, 3 * HALF])
        yt = k.sb("yt", [P, H, SEQ])
        ring = [k.bank(f"ring{n}", 2) for n in range(2)]
        b_d = [k.bank(f"b_d{n}") for n in range(2)]
        b_x = [k.bank(f"b_x{n}") for n in range(2)]
        (presets, xs_high, xs_ready, g_done, z_ready, z_low, ze_ready, lg_ready, l_done, decay_ready, qk_done, sq_ready,
         ss_ready, ln_ready, rms_ready, rg_ready, qk_ready, d_done, top_ready, c_ready, probs_ready, total_ready,
         inv_ready, pn_ready, x_done, x_ready, pt_done, pt_ready, y_done, y_ready, f_done, f_ready, v_done, v_ready,
         tr_done, tr_ready) = (k.sem(n) for n in (
             "presets", "xs_high", "xs_ready", "g_done", "z_ready", "z_low", "ze_ready", "lg_ready", "l_done", "decay_ready",
             "qk_done", "sq_ready", "ss_ready", "ln_ready", "rms_ready", "rg_ready", "qk_ready", "d_done", "top_ready",
             "c_ready", "probs_ready", "total_ready", "inv_ready", "pn_ready", "x_done", "x_ready", "pt_done",
             "pt_ready", "y_done", "y_ready", "f_done", "f_ready", "v_done", "v_ready", "tr_done", "tr_ready"))
        block = stack.enter_context(k.block())
        B = BATCHES

        def run(eng, step):
            sweep(eng, 1, -1, 2, B - 1, B + 1, lambda i, s: step(i))

        def at(i, count_now, count_before):
            return count_now if live(i, B) else count_before

        @block.gpsimd
        def _(pool):
            for tb in range(2):
                nc.gpsimd.memset(pn[tb][:, :, :], 0.0).then_inc(presets, 1)

        @block.tensor
        def _(pe):
            pe.wait_ge(presets, 2)

            def project(bank, weights, tb):
                for half in range(2):
                    for q, (xi, wi) in enumerate(((0, 0), (1, 0), (0, 1))):
                        last = nc.tensor.matmul(bank[:, half * BANK:(half + 1) * BANK], xs[xi][:, tb * P:(tb + 1) * P],
                                                weights[wi][:, half * BANK:(half + 1) * BANK], start=q == 0, stop=q == 2)
                return last

            def step(i):
                j = i - 1
                if live(i, B):
                    hold(pe, xs_ready, i + 1)
                    hold(pe, decay_ready, i)
                    hold(pe, x_ready, 4 * (i - 1))
                    for tb in range(2):
                        for q, (xi, wi) in enumerate(((0, 0), (1, 0), (0, 1))):
                            last = nc.tensor.matmul(b_x[1][:, tb * H:(tb + 1) * H], xs[xi][:, tb * P:(tb + 1) * P], wg[wi][:, :],
                                                    start=q == 0 and tb == 0, stop=q == 2, skip_group_check=True)
                    last.then_inc(g_done, 1)
                    for n in range(4):
                        if n < 2:
                            hold(pe, tr_ready, 4 * i)
                        else:
                            hold(pe, qk_ready, 4 * i + n - 1)
                        project(ring[n % 2], wqkv[n % 2], n // 2).then_inc(qk_done, 1)
                if live(j, B):
                    hold(pe, tr_ready, 4 * i)
                    hold(pe, y_ready, PAIRS * j)
                    for tb in range(2):
                        nc.tensor.matmul(b_d[tb][:, :], c.ident_b[:, :], mask[:, :, :], start=True, stop=True,
                                         skip_group_check=True)
                        for h in range(H):
                            for half in range(2):
                                t = slice(tb * P + half * CHUNK, tb * P + (half + 1) * CHUNK)
                                last = nc.tensor.matmul(b_d[tb][half * CHUNK:(half + 1) * CHUNK, h * CHUNK:(h + 1) * CHUNK],
                                                        qt[:, h, t], kt[:, h, t], start=False, stop=True,
                                                        skip_group_check=True)
                        last.then_inc(d_done, 1)
                    hold(pe, z_ready, at(i, i + 1, i))
                    hold(pe, f_ready, j)
                    for p in range(PAIRS):
                        hold(pe, x_ready, PAIRS * j + p - 1)
                        bank = b_x[p % 2]
                        for hh in range(2):
                            h = 2 * p + hh
                            nc.tensor.matmul(bank[:, hh * SEQ:hh * SEQ + 192], kt[:, h, 0:HALF], qt[:, h, CHUNK:SEQ],
                                             start=hh == 0, stop=True, skip_group_check=True)
                            last = nc.tensor.matmul(bank[:, hh * SEQ + 192:(hh + 1) * SEQ], kt[:, h, HALF:SEQ],
                                                    qt[:, h, 192:SEQ], start=False, stop=True, skip_group_check=True)
                        last.then_inc(x_done, 1)
                    for tb in range(2):
                        hold(pe, pn_ready, 4 * j + 2 * tb + 2)
                        hold(pe, qk_ready, at(i, 4 * i + 3 + tb, 4 * i))
                        for h in range(H):
                            last = nc.tensor.transpose(ring[tb][:, h * P:(h + 1) * P], pn[tb][:, h, :], c.ident[:, :])
                        last.then_inc(pt_done, 1)
                    hold(pe, pt_ready, 2 * i)
                    hold(pe, c_ready, 2 * i)
                    for p in range(PAIRS):
                        hold(pe, y_ready, PAIRS * j + p - 1)
                        for hh in range(2):
                            h = 2 * p + hh
                            nc.tensor.matmul(b_d[p % 2][:, hh * SEQ:(hh + 1) * SEQ], vt[:, 0, h * P:(h + 1) * P], ptt[:, h, 0:SEQ],
                                             start=hh == 0, stop=True, skip_group_check=True)
                            last = nc.tensor.matmul(b_d[p % 2][:, hh * SEQ + HALF:(hh + 1) * SEQ], vt[:, 1, h * P:(h + 1) * P],
                                                    ptt[:, h, SEQ:3 * HALF], start=False, stop=True, skip_group_check=True)
                        last.then_inc(y_done, 1)
                    hold(pe, x_ready, PAIRS * i)
                    hold(pe, y_ready, PAIRS * i)
                    for h in range(H):
                        last = nc.tensor.matmul(b_x[0][:, 0:SEQ], wo[:, h, :], yt[:, h, :], start=h == 0, stop=h == H - 1)
                    last.then_inc(f_done, 1)
                if live(i, B):
                    for tb in range(2):
                        hold(pe, pt_ready, 2 * i - 1 + tb if not isinstance(i, int) or i > 0 else 0)
                        hold(pe, qk_ready, 4 * i + 3 + tb)
                        project(ring[tb], wqkv[2], tb).then_inc(v_done, 1)
                    hold(pe, lg_ready, i + 1)
                    hold(pe, x_ready, PAIRS * i)
                    for q, (n, tb, col) in enumerate(((0, 0, 0), (1, 0, 1), (2, 1, 1))):
                        last = nc.tensor.matmul(b_x[1][:, BANK // 2 + col * H:BANK // 2 + (col + 1) * H], between[:, n, :],
                                                lg[:, tb, :], start=q == 0, stop=q != 1, skip_group_check=True)
                    last.then_inc(l_done, 1)
                    for n in range(4):
                        hold(pe, qk_ready, 4 * i + n + 1)
                        if n < 2:
                            hold(pe, v_ready, 2 * i + n + 1)
                        else:
                            hold(pe, tr_ready, 4 * i + n - 1)
                        for h in range(H):
                            last = nc.tensor.transpose(ring[n % 2][:, h * P:(h + 1) * P], qkn[n][:, h * P:(h + 1) * P], c.ident[:, :])
                        last.then_inc(tr_done, 1)
            run(pe, step)

        @block.scalar
        def _(act):
            act.wait_ge(presets, 2)

            def step(i):
                j = i - 1
                if live(i, B):
                    hold(act, z_low, i + 1)
                    nc.scalar.activation(ze[:, :, :], z[:, :, :], ACT.Exp, scale=-1.0).then_inc(ze_ready, 1)
                    hold(act, ze_ready, i + 1)
                    hold(act, l_done, i)
                    nc.scalar.activation(lg[:, :, :], ze[:, :, :], ACT.Ln, bias=1.0).then_inc(lg_ready, 1)
                    for n in range(4):
                        hold(act, qk_done, 4 * i + n + 1)
                        hold(act, ss_ready, 4 * i + n)
                        nc.scalar.activation(sq[:, :], ring[n % 2][:, :], ACT.Square).then_inc(sq_ready, 1)
                        hold(act, ss_ready, 4 * i + n + 1)
                        hold(act, rms_ready, 4 * i + n)
                        nc.scalar.activation(ln_ss[:, :], ss[:, :], ACT.Ln, scale=1.0 / P, bias=c.eps[:, 1:2]).then_inc(ln_ready, 1)
                        hold(act, ln_ready, 4 * i + n + 1)
                        hold(act, qk_ready, 4 * i + n)
                        nc.scalar.activation(rms[:, :], ln_ss[:, :], ACT.Exp, scale=-0.5).then_inc(rms_ready, 1)
                if live(j, B):
                    for tb in range(2):
                        hold(act, c_ready, 2 * j + tb + 1)
                        hold(act, pn_ready, 4 * j + 2 * tb)
                        nc.scalar.activation(probs[:, :, :], centred[:, :, :], ACT.Exp, scale=P ** -0.5).then_inc(probs_ready, 1)
                    hold(act, f_done, j)
                    for p in range(PAIRS):
                        hold(act, y_done, PAIRS * j + p + 1)
                        nc.scalar.activation(yt[:, 2 * p:2 * p + 2, :], b_d[p % 2][:, :].rearrange("p (h t) -> p h t", t=SEQ),
                                             ACT.Copy).then_inc(y_ready, 1)
                if live(i, B):
                    for tb in range(2):
                        hold(act, v_done, 2 * i + tb + 1)
                        nc.scalar.activation(vt[:, tb, :], ring[tb][:, :], ACT.Copy).then_inc(v_ready, 1)
                    hold(act, l_done, i + 1)
                    hold(act, x_ready, PAIRS * i)
                    nc.scalar.activation(decay[:, 1:3, :], b_x[1][:, BANK // 2:BANK // 2 + 2 * H].rearrange("p (c h) -> p c h", h=H),
                                         ACT.Exp, scale=-1.0).then_inc(decay_ready, 1)
                    for n in range(4):
                        hold(act, tr_done, 4 * i + n + 1)
                        hold(act, x_done, PAIRS * i)
                        nc.scalar.activation((qt, kt)[n % 2][:, :, (n // 2) * P:(n // 2 + 1) * P],
                                             ring[n % 2][:, :].rearrange("p (h t) -> p h t", t=P), ACT.Copy).then_inc(tr_ready, 1)
            run(act, step)

        @block.vector
        def _(dve):
            nc.vector.tensor_scalar(decay[:, 0, :], bg[:, :], 0.0, first_half[:, 0:1], ALU.mult, ALU.add).then_inc(rg_ready, 1)
            dve.wait_ge(presets, 2)

            def step(i):
                j = i - 1
                if live(i, B):
                    hold(dve, g_done, i + 1)
                    hold(dve, ze_ready, i)
                    nc.vector.tensor_tensor(z[:, :, :], b_x[1][:, 0:2 * H].rearrange("p (b h) -> p b h", h=H),
                                            bg[:, :].unsqueeze(1).to_broadcast([P, 2, H]), ALU.add).then_inc(z_ready, 1)
                    hold(dve, z_ready, i + 1)
                    nc.vector.tensor_scalar(z[:, :, :], z[:, :, :], -85.0, None, ALU.max).then_inc(z_low, 1)
                    for n in range(4):
                        hold(dve, sq_ready, 4 * i + n + 1)
                        hold(dve, ln_ready, 4 * i + n)
                        nc.vector.tensor_reduce(ss[:, :], sq[:, :].rearrange("p (h d) -> p h d", d=P), AX.X, ALU.add).then_inc(ss_ready, 1)
                        hold(dve, rms_ready, 4 * i + n + 1)
                        scale = rms
                        if n % 2 == 0:
                            nc.vector.tensor_scalar(rms_gain[:, :], rms[:, :], gain[:, 0:1], None, ALU.mult).then_inc(rg_ready, 1)
                            hold(dve, rg_ready, 2 * i + n // 2 + 2)
                            scale = rms_gain
                        hold(dve, tr_done, 4 * (i - 1) + n + 1)
                        nc.vector.tensor_tensor(qkn[n][:, :].rearrange("p (h d) -> p h d", d=P),
                                                ring[n % 2][:, :].rearrange("p (h d) -> p h d", d=P),
                                                scale[:, :].unsqueeze(2).to_broadcast([P, H, P]), ALU.mult).then_inc(qk_ready, 1)
                if live(j, B):
                    for tb in range(2):
                        u = 2 * j + tb
                        hold(dve, d_done, u + 1)
                        scores = b_d[tb][:, :].rearrange("p (h s) -> p h s", s=CHUNK)
                        hold(dve, c_ready, u)
                        nc.vector.tensor_reduce(top[:, :], scores, AX.X, ALU.max).then_inc(top_ready, 1)
                        hold(dve, top_ready, u + 1)
                        hold(dve, probs_ready, u)
                        nc.vector.tensor_tensor(centred[:, :, :], scores, top[:, :].unsqueeze(2).to_broadcast([P, H, CHUNK]),
                                                ALU.subtract).then_inc(c_ready, 1)
                        hold(dve, probs_ready, u + 1)
                        hold(dve, inv_ready, u)
                        nc.vector.tensor_reduce(total[:, :], probs[:, :, :], AX.X, ALU.add).then_inc(total_ready, 1)
                        hold(dve, total_ready, u + 1)
                        hold(dve, pn_ready, 2 * u)
                        nc.vector.reciprocal(inv[:, :], total[:, :]).then_inc(inv_ready, 1)
                        hold(dve, inv_ready, u + 1)
                        hold(dve, pt_done, u - 1)
                        for half in range(2):
                            rows = slice(half * CHUNK, (half + 1) * CHUNK)
                            nc.vector.tensor_tensor(pn[tb][rows, :, half * CHUNK:(half + 1) * CHUNK], probs[rows, :, :],
                                                    inv[rows, :].unsqueeze(2).to_broadcast([CHUNK, H, CHUNK]),
                                                    ALU.mult).then_inc(pn_ready, 1)
                    hold(dve, decay_ready, i)
                    hold(dve, y_done, PAIRS * j)
                    for p in range(PAIRS):
                        hold(dve, x_done, PAIRS * j + p + 1)
                        bank = b_x[p % 2][:, :].rearrange("p (h c t) -> p h c t", h=2, t=CHUNK)
                        for hh in range(2):
                            h = 2 * p + hh
                            nc.vector.tensor_tensor(ptt[:, h, CHUNK:SEQ].rearrange("p (c t) -> p c t", t=CHUNK), bank[:, hh, 0:3, :],
                                                    decay[:, :, h:h + 1].to_broadcast([P, 3, CHUNK]), ALU.mult)
                        nc.vector.tensor_scalar(ptt[:, 2 * p:2 * p + 2, SEQ + CHUNK:3 * HALF], bank[:, :, 3, :],
                                                first_half[:, 0:1], None, ALU.mult).then_inc(x_ready, 1)
                    hold(dve, x_ready, PAIRS * i)
                    for tb in range(2):
                        hold(dve, pt_done, 2 * j + tb + 1)
                        bank = ring[tb][:, :].rearrange("p (h t) -> p h t", t=P)
                        nc.vector.tensor_copy(ptt[:, :, tb * SEQ:tb * SEQ + CHUNK], bank[:, :, 0:CHUNK])
                        own = ptt[:, :, tb * SEQ + CHUNK:tb * SEQ + P]
                        nc.vector.tensor_tensor(own, bank[:, :, CHUNK:P], own, ALU.add).then_inc(pt_ready, 1)
                    hold(dve, f_done, i)
                    xb = x[:, bass.ds(j * SEQ, SEQ)]
                    nc.vector.tensor_tensor(xb, b_x[0][:, 0:SEQ], xb, ALU.add).then_inc(f_ready, 1)
                if live(i + 1, B):
                    hold(dve, v_done, 2 * (i + 1))
                    xb = x[:, bass.ds((i + 1) * SEQ, SEQ)]
                    nc.vector.tensor_scalar(xs[0][:, :], xb, 1.0, None, ALU.mult).then_inc(xs_high, 1)
                    hold(dve, xs_high, i + 2)
                    nc.vector.tensor_tensor(xs[1][:, :], xb, xs[0][:, :].bitcast(FP32), ALU.subtract).then_inc(xs_ready, 1)
            run(dve, step)


class Constants:

    def __init__(self, nc, stack, dram):
        k = Scope(nc, stack, "const")
        self.centre = k.sb("centre", [P, P])
        self.mean = k.sb("mean", [P, P])
        self.ones = k.sb("ones", [P, 64])
        self.eps = k.sb("eps", [P, 3])
        self.low_rows = k.sb("low_rows", [P, 6])
        self.aug_low = k.sb("aug_low", [3, 1])
        self.ident_r = k.sb("ident_r", [P, P], F32R)
        self.ident = k.sb("ident", [P, P])
        self.ident_b = k.sb("ident_b", [P, P], BF16)
        self.mask_q = k.sb("mask_q", [P, 2, P], BF16)
        self.mask_k = k.sb("mask_k", [P, 2, P], BF16)
        self.aug_x = k.sb("aug_x", [3, SEQ], F32R)
        with ExitStack() as staging:
            ks = Scope(nc, staging, "const_s")
            mq, mk, ax = ks.sb("mq", [P, P]), ks.sb("mk", [P, P]), ks.sb("ax", [3, SEQ])
            loaded = ks.sem("loaded")
            pairs = [(self.centre, "centre"), (self.ident, "ident"), (mq, "mask_q"), (mk, "mask_k"),
                     (ax, "aug_x"), (self.low_rows, "low_rows"), (self.aug_low, "aug_low")]
            with ks.block() as block:
                @block.sync
                def _(sp):
                    for dst, name in pairs:
                        sp.dma_start(dst[:, :], dram[name]).then_inc(loaded, 16)
                    sp.wait_ge(loaded, 16 * len(pairs))

                @block.vector
                def _(dve):
                    nc.vector.memset(self.mean[:, :], 1.0 / P)
                    nc.vector.memset(self.ones[:, :], 1.0)
                    nc.vector.memset(self.eps[:, 0:1], EPS)
                    nc.vector.memset(self.eps[:, 1:2], 1e-6)
                    nc.vector.memset(self.eps[:, 2:3], EPS / 4)
                    dve.wait_ge(loaded, 16 * len(pairs))
                    nc.vector.tensor_copy(self.ident_r[:, :], self.ident[:, :])
                    nc.vector.tensor_copy(self.ident_b[:, :], self.ident[:, :])
                    nc.vector.tensor_copy(self.aug_x[:, :], ax[:, :])
                    for b in range(2):
                        nc.vector.tensor_copy(self.mask_q[:, b, :], mq[:, :])
                        nc.vector.tensor_copy(self.mask_k[:, b, :], mk[:, :])


L0_SHAPE = AttentionShape(dim=8, rows=32, v_width=32, scale=8 ** -0.5, biased=True, v_slots=(3,), o_tiles=4,
                          low_cols=(0, 1))
L1_SHAPE = AttentionShape(dim=64, rows=128, v_width=64, scale=0.125, biased=False, v_slots=(0, 1, 3, 4), o_tiles=8,
                          low_cols=(4, 5))
L2_SHAPE = AttentionShape(dim=16, rows=64, v_width=32, scale=8 ** -0.5, biased=False, v_slots=(3,), o_tiles=4,
                          low_cols=(2, 3))


def program(nc, d, out):
    with ExitStack() as stack:
        k = Scope(nc, stack, "model")
        x = k.sb("x", [P, TOKENS])
        x_loaded, stored = k.sem("x_loaded"), k.sem("stored")
        c = Constants(nc, stack, d)
        with nc.Block() as block:
            @block.sync
            def _(sp):
                sp.dma_start(x[:, :], d["x"]).then_inc(x_loaded, 16)
                sp.wait_ge(x_loaded, 16)
        for run in STAGES:
            run(nc, c, x, d)
        with nc.Block() as block:
            @block.sync
            def _(sp):
                sp.dma_start(out, x[:, :]).then_inc(stored, 16)
                sp.wait_ge(stored, 16)


def group(d, prefix):
    return {name[len(prefix):]: ap for name, ap in d.items() if name.startswith(prefix)}


STAGES = [
    lambda nc, c, x, d: attention(nc, "l0a", c, x, group(d, "l0a_"), L0_SHAPE),
    lambda nc, c, x, d: layer_norm(nc, "ln0", c, x, x),
    lambda nc, c, x, d: reglu(nc, "l0f", c, x, group(d, "l0f_")),
    lambda nc, c, x, d: layer_norm(nc, "ln1", c, x, x),
    lambda nc, c, x, d: attention(nc, "l1a", c, x, group(d, "l1a_"), L1_SHAPE),
    lambda nc, c, x, d: layer_norm(nc, "ln2", c, x, x),
    lambda nc, c, x, d: quantised_mlp(nc, c, x, group(d, "l1f_")),
    lambda nc, c, x, d: layer_norm(nc, "ln3", c, x, x, eps=2),
    lambda nc, c, x, d: attention(nc, "l2a", c, x, group(d, "l2a_"), L2_SHAPE),
    lambda nc, c, x, d: layer_norm(nc, "ln4", c, x, x),
    lambda nc, c, x, d: gated_mlp(nc, c, x, group(d, "l2f_")),
    lambda nc, c, x, d: layer_norm(nc, "ln5", c, x, x),
    lambda nc, c, x, d: chunked_attention(nc, c, x, group(d, "l3a_")),
    lambda nc, c, x, d: layer_norm(nc, "ln6", c, x, x),
    lambda nc, c, x, d: ternary_mlp(nc, c, x, group(d, "l3f_")),
    lambda nc, c, x, d: layer_norm(nc, "ln7", c, x, x),
]


def head_tiles(np, w, rows, copies):
    dim = w.shape[2]
    tiles = np.zeros((w.shape[0], 16, rows), w.dtype)
    for n in range(copies):
        tiles[:, :, n * dim:(n + 1) * dim] = w
    return tiles.reshape(w.shape[0], 16 * rows)


def n_rows(np):
    return np.arange(P)


def layout(np, a):
    h = {}
    n = np.arange(P)
    h["x"] = a["L0_attn_x"].transpose(2, 0, 1).reshape(P, TOKENS)
    h["centre"] = (np.eye(P) - 1.0 / P).astype(np.float32)
    h["ident"] = np.eye(P, dtype=np.float32)
    h["mask_q"] = np.where(n[None, :] > n[:, None], MASKED, 0.0).astype(np.float32)
    h["mask_k"] = np.ascontiguousarray(h["mask_q"].T)
    h["aug_x"] = np.stack([np.ones(SEQ), np.ones(SEQ), np.arange(SEQ)]).astype(np.float32)
    h["aug_low"] = np.array([[0], [1], [0]], np.float32)
    low = np.zeros((P, 6), np.float32)
    low[:, 0] = ((n % 32 >= 16) & (n % 32 < 24)) | (n % 32 == 27)
    low[:, 1] = (n % 32 >= 8) & (n % 32 < 16)
    low[:, 2] = (n % 64 >= 32) & (n % 64 < 48)
    low[:, 3] = (n % 64 >= 16) & (n % 64 < 32)
    low[:, 4] = n >= 64
    low[:, 5] = 1
    h["low_rows"] = low

    def wo_tiles(w, width):
        padded = np.zeros((16, width, P), np.float32)
        padded[:, :w.shape[1]] = w
        return padded.reshape(-1, P, P).transpose(1, 0, 2)

    for p in ("q", "k"):
        h["l0a_w" + p] = head_tiles(np, a["L0_attn_W" + p].T.reshape(P, 16, 8), 32, 3)
    h["l0a_wv"] = a["L0_attn_Wv"].T
    h["l0a_wo"] = wo_tiles(a["L0_attn_Wo"].T.reshape(16, 8, P), 32)
    bv = np.zeros((16, 32), np.float32)
    bv[:, :8] = a["L0_attn_bv"].reshape(16, 8)
    h["l0a_bv"] = bv.reshape(4, P).T
    h["l0a_bo"] = a["L0_attn_bo"].reshape(P, 1)
    slopes = np.power(np.float32(2.0), -8.0 * np.arange(1, 17, dtype=np.float32) / 16).astype(np.float32)
    aug = np.zeros((3, 16, 32), np.float32)
    for n3 in range(3):
        aug[0:2, :, n3 * 8:n3 * 8 + 8] = a["L0_attn_bq"].reshape(1, 16, 8)
    aug[0:2, :, 26:28] = (slopes * np.float32(8 ** 0.5))[None, :, None]
    h["l0a_aug_q"] = aug.reshape(3, 512)
    aug = np.zeros((3, 16, 32), np.float32)
    for n3 in range(3):
        aug[0:2, :, n3 * 8:n3 * 8 + 8] = a["L0_attn_bk"].reshape(1, 16, 8)
    aug[2, :, 26:28] = 1.0
    h["l0a_aug_k"] = aug.reshape(3, 512)

    for p in ("q", "k"):
        h["l1a_w" + p] = head_tiles(np, a["L1_attn_w_" + p].transpose(2, 0, 1), 128, 2)
    h["l1a_wv"] = a["L1_attn_w_v"].transpose(2, 0, 1).reshape(P, 1024)
    h["l1a_wo"] = a["L1_attn_w_o"].reshape(8, P, P).transpose(1, 0, 2)

    for p in ("q", "k"):
        h["l2a_w" + p] = head_tiles(np, a["L2_attn_W" + p].reshape(P, 16, 16), 64, 3)
    h["l2a_wv"] = a["L2_attn_Wv"]
    h["l2a_wo"] = wo_tiles(a["L2_attn_Wo"].reshape(16, 16, P), 32)

    h["l0f_w"] = np.stack([a["L0_ffn_W_r"].T, a["L0_ffn_W_k"].T], axis=1)
    h["l0f_mu"] = np.stack([a["L0_ffn_mu_r"], a["L0_ffn_mu_k"]], axis=1)
    h["l0f_wv"] = a["L0_ffn_W_v"].T

    def columns(v):
        return v.reshape(-1, P).T

    def k_tiles(w):
        return w.reshape(-1, P, w.shape[1]).transpose(1, 0, 2)

    h["l1f_fc1_q"] = a["L1_ffn_fc1_q"]
    h["l1f_fc2_q"] = k_tiles(a["L1_ffn_fc2_q"])
    h["l1f_fc1_s"] = np.broadcast_to(a["L1_ffn_fc1_scales"], (P, 512))
    h["l1f_fc2_s"] = np.broadcast_to(a["L1_ffn_fc2_scales"][None], (P, 4, P))
    h["l1f_b1"] = columns(a["L1_ffn_fc1_bias"])
    h["l1f_b2"] = columns(a["L1_ffn_fc2_bias"])
    h["l1f_gamma"] = columns(a["L1_ffn_ln_gamma"])
    h["l1f_beta"] = columns(a["L1_ffn_ln_beta"])

    h["l2f_w12"] = np.concatenate([a["L2_ffn_w1_w"].T, a["L2_ffn_w2_w"].T], axis=1)
    for n in ("1", "2"):
        h["l2f_h" + n] = a["L2_ffn_h" + n + "_w"].reshape(4, P, 4, P).transpose(3, 0, 2, 1).reshape(P, 16 * P)
    h["l2f_w3"] = k_tiles(a["L2_ffn_w3_w"].T).reshape(P, 4 * P)
    h["l2f_scales"] = np.concatenate([columns(a["L2_ffn_" + n]) for n in ("w1_s", "w2_s", "h1_s", "h2_s", "w3_s")], axis=1)

    for n in ("q", "k", "v", "g"):
        h["l3a_w" + n] = a["L3_attn_W" + n].T
    h["l3a_wo"] = k_tiles(a["L3_attn_Wo"].T)
    h["l3a_bg"] = np.broadcast_to(a["L3_attn_bg"], (P, 8))
    h["l3a_gain"] = np.broadcast_to(a["L3_attn_qk_gain"].reshape(1, 1), (P, 1))
    chunk = np.arange(P) // 64
    between = np.zeros((P, 3, P), np.float32)
    between[:, 0] = between[:, 1] = (chunk[:, None] == 1) & (chunk[None, :] == 0)
    between[:, 2] = chunk[:, None] == 0
    h["l3a_between"] = between
    h["l3a_first_half"] = (chunk == 0).astype(np.float32).reshape(P, 1)
    h["l3a_mask"] = np.where(np.arange(64)[None, :] > (n_rows(np) % 64)[:, None], MASKED, 0.0).astype(np.float32)

    h["l3f_w_fc"] = a["L3_ffn_w_fc"].T
    h["l3f_w_proj"] = k_tiles(a["L3_ffn_w_proj"].T).reshape(P, 4 * P)
    h["l3f_bt"] = a["L3_ffn_fast_b"].T
    h["l3f_v"] = a["L3_ffn_v"]
    h["l3f_ut"] = a["L3_ffn_u"].T
    h["l3f_gate"] = np.broadcast_to(a["L3_ffn_gate"].reshape(1, 1), (P, 1))
    return h


def kernel(**inputs):
    import numpy as _np
    import concourse.bacc as _bacc
    from concourse import mybir as _mybir
    from concourse.bass_utils import run_bass_kernel_spmd as _run

    nc = _bacc.Bacc("TRN2", target_bir_lowering=False, num_devices=1)
    arrays, d = {}, {}
    for name, value in layout(_np, {n: _np.asarray(v) for n, v in inputs.items()}).items():
        value = _np.ascontiguousarray(value)
        arrays["in_" + name] = value
        d[name] = nc.dram_tensor("in_" + name, value.shape, _mybir.dt.from_np(value.dtype), kind="ExternalInput").ap()
    out = nc.dram_tensor("out", (P, TOKENS), _mybir.dt.float32, kind="ExternalOutput").ap()
    program(nc, d, out)
    r = _run(nc, [arrays], core_ids=[0])
    return _np.ascontiguousarray(r.results[0]["out"].reshape(P, BATCHES, SEQ).transpose(1, 2, 0))
```

```python
import concourse.bass as bass
from concourse import mybir
from contextlib import ExitStack, contextmanager

FP32 = mybir.dt.float32
F32R = mybir.dt.float32r
BF16 = mybir.dt.bfloat16
I32 = mybir.dt.int32
ACT = mybir.ActivationFunctionType
ALU = mybir.AluOpType
AX = mybir.AxisListType

P = 128
BATCHES, SEQ = 32, 256
TOKENS = BATCHES * SEQ
BANK = 512
UNIT = BANK
UNITS = TOKENS // UNIT
HALF = SEQ // 2
EPS = 1e-5
MASKED = -1e30


def live(unit, total):
    return not isinstance(unit, int) or 0 <= unit < total


def hold(eng, sem, count):
    if not isinstance(count, int) or count > 0:
        eng.wait_ge(sem, count)


def sweep(eng, slots, first, loop_from, loop_to, last, step):
    for i in range(first, loop_from):
        for s in range(slots):
            step(i, s)
    with eng.Fori(loop_from, loop_to) as i:
        for s in range(slots):
            step(i, s)
    for i in range(loop_to, last):
        for s in range(slots):
            step(i, s)


class Scope:

    def __init__(self, nc, stack, layer):
        self.nc, self.stack, self.layer = nc, stack, layer
        self.sems = []

    def sb(self, name, shape, dt=FP32):
        return self.stack.enter_context(self.nc.sbuf_tensor(f"{self.layer}_{name}", shape, dt))

    def bank(self, name, banks=1):
        return self.stack.enter_context(self.nc.psum_tensor(f"{self.layer}_{name}", [P, banks * BANK], FP32))

    def sem(self, name):
        handle = self.stack.enter_context(self.nc.semaphore(f"{self.layer}_{name}"))
        self.sems.append(handle)
        return handle

    @contextmanager
    def block(self):
        with self.nc.Block() as block:
            yield block
        numbers = sorted(s.num for s in self.sems)
        with self.nc.Block() as block:
            @block.gpsimd
            def _(pool):
                first = 0
                for n in range(1, len(numbers) + 1):
                    if n == len(numbers) or numbers[n] != numbers[n - 1] + 1:
                        nc_range = range(numbers[first], numbers[n - 1] + 1)
                        pool.sem_clear(nc_range)
                        first = n


def load_and_split(nc, k, block_name, parts):
    loaded, high_ready = k.sem("w_loaded"), k.sem("w_high")
    with k.block() as block:
        @block.sync
        def _(sp):
            for dram, stage, _, _ in parts:
                sp.dma_start(stage, dram).then_inc(loaded, 16)
            sp.wait_ge(loaded, 16 * len(parts))

        @block.vector
        def _(dve):
            dve.wait_ge(loaded, 16 * len(parts))
            n = 0
            for _, stage, high, low in parts:
                if high is None:
                    continue
                nc.vector.tensor_copy(high, stage).then_inc(high_ready, 1)
                n += 1
                if low is not None:
                    dve.wait_ge(high_ready, n)
                    nc.vector.tensor_tensor(low, stage, high.bitcast(FP32), ALU.subtract)


def layer_norm(nc, layer, c, src, dst, eps=0):
    SLOTS, CHUNKS = 4, 8
    with ExitStack() as stack:
        k = Scope(nc, stack, layer)
        centred = [k.bank(f"centred{i}") for i in range(SLOTS)]
        var = [k.bank(f"var{i}") for i in range(SLOTS)]
        sq = k.sb("sq", [P, SLOTS, UNIT])
        rstd = k.sb("rstd", [P, TOKENS])
        centred_done, sq_ready, var_done, ln_ready, copied, rstd_ready = (
            k.sem(n) for n in ("centred_done", "sq_ready", "var_done", "ln_ready", "copied", "rstd_ready"))
        block = stack.enter_context(k.block())

        def tokens(buf, n):
            return buf[:, bass.ds(n * UNIT, UNIT)]

        def chunk(buf, n):
            return buf[:, n * TOKENS // CHUNKS:(n + 1) * TOKENS // CHUNKS]

        @block.tensor
        def _(pe):
            def step(i, s):
                n, p = SLOTS * i + s, (s - 1) % SLOTS
                if live(n, UNITS):
                    hold(pe, copied, n - SLOTS + 1)
                    nc.tensor.matmul(centred[s][:, :], c.centre[:, :], tokens(src, n),
                                     start=True, stop=True).then_inc(centred_done, 1)
                if live(n - 1, UNITS):
                    hold(pe, sq_ready, n)
                    hold(pe, ln_ready, n - SLOTS)
                    nc.tensor.matmul(var[p][:, :], c.mean[:, :], sq[:, p, :],
                                     start=True, stop=True).then_inc(var_done, 1)
            sweep(pe, SLOTS, 0, 1, UNITS // SLOTS, UNITS // SLOTS + 1, step)

        @block.scalar
        def _(act):
            for n in range(UNITS + 1):
                p = (n - 1) % SLOTS
                if n < UNITS:
                    hold(act, var_done, n - SLOTS + 1)
                    act.wait_ge(centred_done, n + 1)
                    nc.scalar.activation(sq[:, n % SLOTS, :], centred[n % SLOTS][:, :], ACT.Square).then_inc(sq_ready, 1)
                if n > 0:
                    act.wait_ge(var_done, n)
                    nc.scalar.activation(tokens(rstd, n - 1), var[p][:, :], ACT.Ln,
                                         bias=c.eps[:, eps:eps + 1]).then_inc(ln_ready, 1)
            for n in range(CHUNKS):
                act.wait_ge(ln_ready, (n + 1) * UNITS // CHUNKS)
                nc.scalar.activation(chunk(rstd, n), chunk(rstd, n), ACT.Exp, scale=-0.5).then_inc(rstd_ready, 1)

        @block.vector
        def _(dve):
            def step(i, s):
                n = SLOTS * i + s
                dve.wait_ge(centred_done, n + 1)
                hold(dve, sq_ready, n + 1)
                nc.vector.tensor_scalar(tokens(dst, n), centred[s][:, :], 1.0, None, ALU.mult).then_inc(copied, 1)
            sweep(dve, SLOTS, 0, 1, UNITS // SLOTS, UNITS // SLOTS, step)
            for n in range(CHUNKS):
                dve.wait_ge(copied, (n + 1) * UNITS // CHUNKS)
                dve.wait_ge(rstd_ready, n + 1)
                nc.vector.tensor_tensor(chunk(dst, n), chunk(dst, n), chunk(rstd, n), ALU.mult)


class AttentionShape:

    def __init__(self, dim, rows, v_width, scale, biased, v_slots, o_tiles, low_cols, lag=2):
        self.lag = lag
        self.dim, self.rows, self.v_width, self.scale, self.biased = dim, rows, v_width, scale, biased
        self.v_slots, self.o_tiles, self.low_cols = v_slots, o_tiles, low_cols
        self.n_tiles = 16 * rows // P
        self.heads_per_tile = P // rows
        self.buffers = {32: 2, 64: 4, 128: 8}[rows]
        self.pv_every = 2 if v_width == 32 else 1


HEADS, STEPS = 16, 8


def attention(nc, layer, c, x, w, a):
    E, R, VW = a.n_tiles, a.rows, a.v_width
    VD = HEADS * a.dim
    KEPT = 4
    AHEAD = 2
    T_LAG, PV_LAG = a.lag, a.lag + 1
    with ExitStack() as stack:
        k = Scope(nc, stack, layer)
        wq = [k.sb(f"wq{p}", [P, E * P], F32R) for p in range(2)]
        wk = [k.sb(f"wk{p}", [P, E * P], F32R) for p in range(2)]
        wv = [k.sb(f"wv{p}", [P, VD], F32R) for p in range(2)]
        wo = k.sb("wo", [P, a.o_tiles, P])
        fbias = k.sb("fbias", [P, 1])
        if a.biased:
            aug = [k.sb(f"aug_{n}", [3, E * P], F32R) for n in "qk"]
        with ExitStack() as staging:
            ks = Scope(nc, staging, layer + "_s")
            sq_, sk_, sv_ = ks.sb("q", [P, E * P]), ks.sb("k", [P, E * P]), ks.sb("v", [P, VD])
            parts = [(w["wq"], sq_[:, :], wq[0][:, :], wq[1][:, :]), (w["wk"], sk_[:, :], wk[0][:, :], wk[1][:, :]),
                     (w["wv"], sv_[:, :], wv[0][:, :], wv[1][:, :]), (w["wo"], wo[:, :, :], None, None)]
            if a.biased:
                raw_aug = [ks.sb(f"a{n}", [3, E * P]) for n in "qk"]
                t_aug = ks.sb("t_aug", [3, E * P], F32R)
                bvp, bo = ks.sb("bvp", [P, 4]), ks.sb("bo", [P, 1])
                parts += [(w["aug_q"], raw_aug[0][:, :], None, None), (w["aug_k"], raw_aug[1][:, :], None, None),
                          (w["bv"], bvp[:, :], None, None), (w["bo"], bo[:, :], None, None)]
            load_and_split(nc, ks, "load", parts)
            if a.biased:
                high, low, summed = ks.sem("aug_high"), ks.sem("aug_low"), ks.sem("bias_summed")
                pb = ks.bank("pb")
                with ks.block() as block:
                    @block.vector
                    def _(dve):
                        for n in range(2):
                            if n > 0:
                                dve.wait_ge(low, n)
                            nc.vector.tensor_scalar(t_aug[:, :], raw_aug[n][:, :], c.aug_low[0:3, 0:1], None,
                                                    ALU.mult).then_inc(high, 1)
                            dve.wait_ge(high, n + 1)
                            nc.vector.tensor_tensor(aug[n][:, :], raw_aug[n][:, :], t_aug[:, :].bitcast(FP32),
                                                    ALU.subtract).then_inc(low, 1)
                        dve.wait_ge(summed, 1)
                        nc.vector.tensor_tensor(fbias[:, :], pb[:, 0:1], bo[:, :], ALU.add)

                    @block.tensor
                    def _(pe):
                        for g in range(4):
                            last = nc.tensor.matmul(pb[:, 0:1], wo[:, g, :], bvp[:, g:g + 1], start=g == 0, stop=g == 3)
                        last.then_inc(summed, 1)

        xs = [k.sb(f"xs{p}", [P, SEQ], F32R) for p in range(2)]
        ops = [k.sb(f"ops{i}", [P, 4, SEQ], F32R) for i in range(a.buffers)]
        top = [k.sb(f"top{i}", [P, 2, 2]) for i in range(2)]
        top_scaled = [k.sb(f"top_scaled{i}", [P, 2, 2]) for i in range(2)]
        total, inv = [k.sb(f"total{i}", [P, 2, 2]) for i in range(2)], [k.sb(f"inv{i}", [P, 2, 2]) for i in range(2)]
        probs = k.sb("probs", [P, KEPT, 2, 3 * HALF])
        probs_t = k.sb("probs_t", [P, KEPT, 2, 3 * HALF])
        vb = k.sb("vb", [P, 2, HEADS, VW])
        ot = k.sb("ot", [P, a.o_tiles, SEQ])

        scores = [k.bank(f"scores{i}", 2) for i in range(2)]
        EARLY = a.n_tiles > STEPS
        b_t = [k.bank(f"b_t{i}") for i in range(1 if EARLY else 2)]
        projs = [k.bank(f"proj{i}") for i in range(2 if EARLY else 1)]
        b_o = k.bank("b_o")

        (presets, xs_high, xs_ready, proj_done, t_ready, ops_ready, s_done, top_ready, scaled_ready, exp_ready,
         inv_ready, probs_ready, t_done, pt0_ready, pt1_ready, pv_done, o_ready, v_done, v_ready, f_done, y_ready) = (
            k.sem(n) for n in (
                "presets", "xs_high", "xs_ready", "proj_done", "t_ready", "ops_ready", "s_done", "top_ready",
                "scaled_ready", "exp_ready", "inv_ready", "probs_ready", "t_done", "pt0_ready", "pt1_ready", "pv_done",
                "o_ready", "v_done", "v_ready", "f_done", "y_ready"))
        block = stack.enter_context(k.block())
        F = STEPS // a.pv_every
        NV = len(a.v_slots)
        STEPS_ALL = BATCHES * STEPS
        LAG = PV_LAG + a.pv_every - 1

        def events(i, s):
            i, s = i + s // STEPS, s % STEPS
            if E < STEPS:
                return [(E * i + s // 2, s // 2)] if s % 2 == 0 else []
            per = E // STEPS
            return [(E * i + per * s + d, per * s + d) for d in range(per)]

        def events_until(i, s):
            return E * i + (s * E // STEPS if E >= STEPS else s // 2) + max(1, E // STEPS)

        def head(s, hh):
            h = 2 * s + hh
            return ops[h // a.heads_per_tile % a.buffers], slice(h * R % P, h * R % P + R)

        def pv_event(i, s):
            return F * i + (s - LAG) // a.pv_every if (s - LAG) % a.pv_every == 0 else None

        def pv_until(i, s):
            return F * i + (s - LAG) // a.pv_every + 1

        def pv_of(i, s, n):
            return F * i + s // a.pv_every + 1 if not isinstance(n, int) or n - T_LAG - KEPT >= 0 else 0

        def run(eng, step):
            sweep(eng, STEPS, -1, 2, BATCHES - 1, BATCHES + 1, step)

        def tri(bank):
            return bank.rearrange("p (b t) -> p b t", t=HALF)[:, 0:4:2, :]

        @block.tensor
        def _(pe):
            pe.wait_ge(presets, 1)

            def transpose(i, s, heads):
                n = STEPS * i + s
                if live(n - T_LAG, STEPS_ALL):
                    for hh in heads:
                        bank = b_t[hh % len(b_t)]
                        if hh == 0:
                            hold(pe, probs_ready, n - T_LAG + 1)
                            hold(pe, pt1_ready if EARLY else pt0_ready, n - T_LAG)
                        elif EARLY:
                            hold(pe, pt0_ready, n - T_LAG + 1)
                        else:
                            hold(pe, pt1_ready, n - T_LAG)
                        for b in range(3):
                            last = nc.tensor.transpose(bank[:, b * P:(b + 1) * P],
                                                       probs[:, (s - T_LAG) % KEPT, hh, b * P:(b + 1) * P], c.ident[:, :])
                        last.then_inc(t_done, 1)

            def project(i, s, which):
                if not live(STEPS * i + s + AHEAD, STEPS_ALL):
                    return
                for e, tile in events(i, s + AHEAD)[which]:
                    hold(pe, xs_ready, i + (2 if s + AHEAD >= STEPS else 1))
                    hold(pe, ops_ready, e + 1 - len(projs))
                    proj = projs[tile % len(projs)]
                    cols = slice(tile * P, (tile + 1) * P)
                    for q, wt in enumerate((wq, wk)):
                        out = proj[:, q * SEQ:(q + 1) * SEQ]
                        for m, (wi, xi) in enumerate(((0, 0), (0, 1), (1, 0))):
                            last = nc.tensor.matmul(out, wt[wi][:, cols], xs[xi][:, :], start=m == 0 and q == 0,
                                                    stop=m == 2, skip_group_check=True)
                        if a.biased:
                            last = nc.tensor.matmul(out, aug[q][0:3, cols], c.aug_x[0:3, :], start=False, stop=True,
                                                    skip_group_check=True)
                    last.then_inc(proj_done, 1)

            def step(i, s):
                n = STEPS * i + s
                if s in a.v_slots and live(i, BATCHES):
                    j = a.v_slots.index(s)
                    hold(pe, xs_ready, i + 1)
                    hold(pe, v_ready, NV * i + j)
                    hold(pe, o_ready, pv_until(i, s - 1))
                    hold(pe, y_ready, i if s > PV_LAG else i - 1)
                    first, width, tbs = v_chunk(a, j)
                    for q, tb in enumerate(tbs):
                        out = b_o[:, q * width:(q + 1) * width]
                        for m, (xi, wi) in enumerate(((0, 0), (1, 0), (0, 1))):
                            last = nc.tensor.matmul(out, xs[xi][:, tb * HALF:(tb + 1) * HALF],
                                                    wv[wi][:, first * a.dim:first * a.dim + width],
                                                    start=m == 0 and q == 0, stop=m == 2, skip_group_check=True)
                    last.then_inc(v_done, 1)
                if s == PV_LAG and live(i - 1, BATCHES):
                    hold(pe, o_ready, F * i)
                    hold(pe, v_ready, NV * i + sum(v <= PV_LAG for v in a.v_slots) * live(i, BATCHES))
                    for g in range(a.o_tiles):
                        last = nc.tensor.matmul(b_o[:, 0:SEQ], wo[:, g, :], ot[:, g, :], start=g == 0,
                                                stop=g == a.o_tiles - 1)
                    last.then_inc(f_done, 1)
                if EARLY:
                    transpose(i, s, (0,))
                    project(i, s, slice(0, 1))
                if live(n, STEPS_ALL):
                    hold(pe, exp_ready, 2 * (n - 1))
                    hold(pe, ops_ready, events_until(i, s))
                    for hh in range(2):
                        nc.tensor.matmul(tri(scores[s % 2][:, hh * BANK:(hh + 1) * BANK]), c.ident_b[:, :],
                                         c.mask_q[:, :, :], start=True, stop=True, skip_group_check=True)
                    for hh in range(2):
                        op, rows = head(s, hh)
                        bank = scores[s % 2][:, hh * BANK:(hh + 1) * BANK]
                        for qb in range(2):
                            for key in ((1, 3) if R == P else (3,)):
                                last = nc.tensor.matmul(bank[:, qb * HALF:HALF + qb * SEQ], op[rows, 2, qb * HALF:(qb + 1) * HALF],
                                                        op[rows, key, 0:(qb + 1) * HALF], start=False, stop=True,
                                                        skip_group_check=True)
                    last.then_inc(s_done, 1)
                if not EARLY:
                    project(i, s, slice(0, 1))
                    transpose(i, s, (0, 1))
                if EARLY:
                    project(i, s, slice(1, 2))
                    transpose(i, s, (1,))
                f = pv_event(i, s)
                if f is not None and live(n - LAG, STEPS_ALL):
                    hold(pe, pt0_ready, n - PV_LAG + 1)
                    hold(pe, pt1_ready, n - PV_LAG + 1)
                    hold(pe, v_ready, NV * i + sum(v <= s for v in a.v_slots) * live(i, BATCHES))
                    hold(pe, o_ready, f)
                    if s >= PV_LAG:
                        hold(pe, y_ready, i)
                    heads = [(2 * ((s - PV_LAG - d) % STEPS) + hh, (s - PV_LAG - d) % KEPT, hh)
                             for d in range(a.pv_every - 1, -1, -1) for hh in range(2)]
                    for kb in range(2):
                        for g, (h, kept, hh) in enumerate(heads):
                            last = nc.tensor.matmul(b_o[g * VW:(g + 1) * VW, kb * HALF:SEQ], vb[:, kb, h, :],
                                                    probs_t[:, kept, hh, kb * SEQ:kb * SEQ + SEQ - kb * HALF],
                                                    start=kb == 0, stop=kb == 1, skip_group_check=True)
                    last.then_inc(pv_done, 1)
            run(pe, step)

        @block.gpsimd
        def _(pool):
            nc.gpsimd.memset(vb[:, :, :, :], 0.0).then_inc(presets, 1)

            def step(i, s):
                n = STEPS * i + s
                if live(n - 1, STEPS_ALL):
                    hold(pool, inv_ready, n)
                    kept, scale = (s - 1) % KEPT, inv[(s - 1) % 2]
                    nc.gpsimd.tensor_tensor(probs[:, kept, :, 0:HALF], probs[:, kept, :, 0:HALF],
                                            scale[:, 0, :].unsqueeze(2).to_broadcast([P, 2, HALF]), ALU.mult)
                    nc.gpsimd.tensor_tensor(probs[:, kept, :, HALF:3 * HALF], probs[:, kept, :, HALF:3 * HALF],
                                            scale[:, 1, :].unsqueeze(2).to_broadcast([P, 2, SEQ]),
                                            ALU.mult).then_inc(probs_ready, 1)
            run(pool, step)

        @block.scalar
        def _(act):
            act.wait_ge(presets, 1)

            def round_parts(i, s, which):
                n = STEPS * i + s
                for e, tile in events(i, s + AHEAD)[which]:
                    hold(act, proj_done, e + 1)
                    hold(act, s_done, n if E < STEPS else n - 1)
                    op, proj = ops[tile % a.buffers], projs[tile % len(projs)]
                    for q in range(2):
                        last = nc.scalar.activation(op[:, q, :], proj[:, q * SEQ:(q + 1) * SEQ], ACT.Copy,
                                                    scale=c.low_rows[:, a.low_cols[q]:a.low_cols[q] + 1])
                    last.then_inc(t_ready, 1)

            def copy_first(i, s):
                n = STEPS * i + s
                if live(n - T_LAG, STEPS_ALL):
                    hold(act, t_done, 2 * (n - T_LAG) + 1)
                    hold(act, pv_done, pv_of(i, s - T_LAG - KEPT, n))
                    nc.scalar.activation(probs_t[:, (s - T_LAG) % KEPT, 0, :], b_t[0][:, 0:3 * HALF],
                                         ACT.Copy).then_inc(pt0_ready, 1)

            def step(i, s):
                n = STEPS * i + s
                if s in a.v_slots and live(i, BATCHES):
                    j = a.v_slots.index(s)
                    first, width, tbs = v_chunk(a, j)
                    act.wait_ge(v_done, NV * i + j + 1)
                    hold(act, pv_done, F * i - (F // 2 if NV == 4 and j < 2 else 0))
                    nc.scalar.activation(vb[:, tbs[0]:tbs[-1] + 1, first:first + width // a.dim, 0:a.dim],
                                         b_o[:, 0:len(tbs) * width].rearrange("p (b h d) -> p b h d", b=len(tbs), d=a.dim),
                                         ACT.Copy).then_inc(v_ready, 1)
                if EARLY:
                    copy_first(i, s)
                for hh in range(2):
                    if EARLY and live(n + AHEAD, STEPS_ALL):
                        round_parts(i, s, slice(hh, hh + 1))
                    if live(n - 1, STEPS_ALL):
                        hold(act, scaled_ready, n)
                        hold(act, t_done, 2 * (n - 1 - KEPT + 1))
                        hold(act, inv_ready, n - 2)
                        for qb in range(2):
                            cols = slice(qb * HALF, HALF + qb * SEQ)
                            last = nc.scalar.activation(probs[:, (s - 1) % KEPT, hh, cols],
                                                        scores[(s - 1) % 2][:, hh * BANK + cols.start:hh * BANK + cols.stop],
                                                        ACT.Exp, bias=top_scaled[(s - 1) % 2][:, qb, hh:hh + 1], scale=a.scale,
                                                        accum_out=total[(s - 1) % 2][:, qb, hh:hh + 1])
                        last.then_inc(exp_ready, 1)
                if not EARLY and live(n + AHEAD, STEPS_ALL):
                    round_parts(i, s, slice(0, 1))
                if not EARLY:
                    copy_first(i, s)
            run(act, step)

        @block.vector
        def _(dve):
            def subtract_parts(i, s, which):
                for e, tile in events(i, s + AHEAD)[which]:
                    op, proj = ops[tile % a.buffers], projs[tile % len(projs)]
                    dve.wait_ge(t_ready, e + 1)
                    nc.vector.tensor_tensor(op[:, 2:4, :], proj[:, :].rearrange("p (q t) -> p q t", t=SEQ),
                                            op[:, 0:2, :].bitcast(FP32), ALU.subtract).then_inc(ops_ready, 1)

            def step(i, s):
                n = STEPS * i + s
                if s == PV_LAG and live(i - 1, BATCHES):
                    hold(dve, f_done, i)
                    xb = x[:, bass.ds((i - 1) * SEQ, SEQ)]
                    if a.biased:
                        last = nc.vector.scalar_tensor_tensor(xb, b_o[:, 0:SEQ], fbias[:, 0:1], xb, ALU.add, ALU.add)
                    else:
                        last = nc.vector.tensor_tensor(xb, b_o[:, 0:SEQ], xb, ALU.add)
                    last.then_inc(y_ready, 1)
                if s == STEPS - AHEAD and live(i + 1, BATCHES):
                    hold(dve, proj_done, E * (i + 1))
                    hold(dve, v_done, NV * (i + 1))
                    xb = x[:, bass.ds((i + 1) * SEQ, SEQ)]
                    nc.vector.tensor_scalar(xs[0][:, :], xb, 1.0, None, ALU.mult).then_inc(xs_high, 1)
                    hold(dve, xs_high, i + 2)
                    nc.vector.tensor_tensor(xs[1][:, :], xb, xs[0][:, :].bitcast(FP32), ALU.subtract).then_inc(xs_ready, 1)
                if EARLY and live(n + AHEAD, STEPS_ALL):
                    subtract_parts(i, s, slice(0, 1))
                if live(n, STEPS_ALL):
                    mine = top[s % 2]
                    banks = scores[s % 2][:, :].rearrange("p (h t) -> p h t", t=BANK)
                    dve.wait_ge(s_done, n + 1)
                    hold(dve, exp_ready, 2 * (n - 1))
                    hold(dve, scaled_ready, n - 1)
                    nc.vector.tensor_reduce(mine[:, 0, :], banks[:, :, 0:HALF], AX.X, ALU.max, negate=True)
                    nc.vector.tensor_reduce(mine[:, 1, :], banks[:, :, HALF:3 * HALF], AX.X, ALU.max,
                                            negate=True).then_inc(top_ready, 1)
                    dve.wait_ge(top_ready, n + 1)
                    nc.vector.tensor_scalar(top_scaled[s % 2][:, :, :], mine[:, :, :], a.scale, None,
                                            ALU.mult).then_inc(scaled_ready, 1)
                if EARLY and live(n + AHEAD, STEPS_ALL):
                    subtract_parts(i, s, slice(1, 2))
                if live(n - 1, STEPS_ALL):
                    hold(dve, exp_ready, 2 * n)
                    hold(dve, probs_ready, n - 2)
                    nc.vector.reciprocal(inv[(s - 1) % 2][:, :, :], total[(s - 1) % 2][:, :, :]).then_inc(inv_ready, 1)
                if not EARLY and live(n + AHEAD, STEPS_ALL):
                    subtract_parts(i, s, slice(0, 1))
                if live(n - T_LAG, STEPS_ALL):
                    hold(dve, t_done, 2 * (n - T_LAG + 1))
                    hold(dve, pv_done, pv_of(i, s - T_LAG - KEPT, n))
                    nc.vector.tensor_copy(probs_t[:, (s - T_LAG) % KEPT, 1, :], b_t[-1][:, 0:3 * HALF]).then_inc(pt1_ready, 1)
                f = pv_event(i, s)
                if f is not None and live(n - LAG, STEPS_ALL):
                    g = ((s - LAG) % STEPS) // a.pv_every
                    hold(dve, pv_done, f + 1)
                    hold(dve, f_done, i if s >= LAG else i - 1)
                    nc.vector.tensor_copy(ot[:, g, :], b_o[:, 0:SEQ]).then_inc(o_ready, 1)
            run(dve, step)


def v_chunk(a, j):
    if len(a.v_slots) == 1:
        return 0, HEADS * a.dim, (0, 1)
    return j // 2 * 8, HEADS * a.dim // 2, (j % 2,)


def reglu(nc, layer, c, x, w):
    with ExitStack() as stack:
        k = Scope(nc, stack, layer)
        wm = k.sb("wm", [P, 2, 2, 2, P], F32R)
        wv = k.sb("wv", [P, P])
        with ExitStack() as staging:
            ks = Scope(nc, staging, layer + "_s")
            raw, mu = ks.sb("raw", [P, 2, P]), ks.sb("mu", [P, 2])
            rest, mixed = ks.sb("rest", [P, 2]), ks.sb("mixed", [P, 2, 2, P])
            loaded, rest_ready, mixed_ready, high_ready = (
                ks.sem(n) for n in ("loaded", "rest_ready", "mixed_ready", "high_ready"))
            with ks.block() as block:
                @block.sync
                def _(sp):
                    for dst, src in ((raw[:, :, :], w["w"]), (mu[:, :], w["mu"]), (wv[:, :], w["wv"])):
                        sp.dma_start(dst, src).then_inc(loaded, 16)

                @block.vector
                def _(dve):
                    dve.wait_ge(loaded, 48)
                    nc.vector.tensor_scalar(rest[:, :], mu[:, :], -1.0, 1.0, ALU.mult, ALU.add).then_inc(rest_ready, 1)
                    dve.wait_ge(rest_ready, 1)
                    for m in range(2):
                        for t, share in enumerate((mu, rest)):
                            nc.vector.tensor_scalar(mixed[:, m, t, :], raw[:, m, :], share[:, m:m + 1], None,
                                                    ALU.mult).then_inc(mixed_ready, 1)
                    dve.wait_ge(mixed_ready, 4)
                    nc.vector.tensor_copy(wm[:, :, :, 0, :], mixed[:, :, :, :]).then_inc(high_ready, 1)
                    dve.wait_ge(high_ready, 1)
                    nc.vector.tensor_tensor(wm[:, :, :, 1, :], mixed[:, :, :, :], wm[:, :, :, 0, :].bitcast(FP32), ALU.subtract)

        xs = [[k.sb(f"xs{b}{p}", [P, 2, SEQ + 1], F32R) for p in range(2)] for b in range(2)]
        kr = k.sb("kr", [P, UNIT])
        kk = [k.sb(f"kk{b}", [P, UNIT]) for b in range(2)]
        sg = [k.sb(f"sg{b}", [P, UNIT]) for b in range(2)]
        gated = k.sb("gated", [P, UNIT])
        b_k, b_r, b_v = k.bank("b_k"), k.bank("b_r"), k.bank("b_v")
        presets, xs_high, xs_ready, k_done, r_done, kr_ready, kk_ready, sg_ready, v_done, gated_ready, y_ready = (
            k.sem(n) for n in ("presets", "xs_high", "xs_ready", "k_done", "r_done", "kr_ready", "kk_ready", "sg_ready",
                               "v_done", "gated_ready", "y_ready"))
        block = stack.enter_context(k.block())

        def run(eng, step):
            sweep(eng, 2, -1, 2, UNITS // 2 - 1, UNITS // 2 + 1, step)

        @block.gpsimd
        def _(pool):
            for b in range(2):
                for p in range(2):
                    nc.gpsimd.memset(xs[b][p][:, :, 0:1].bitcast(FP32), 0.0).then_inc(presets, 1)

        @block.tensor
        def _(pe):
            pe.wait_ge(presets, 4)

            def step(i, s):
                n, b = 2 * i + s, s % 2
                if live(n, UNITS):
                    hold(pe, xs_ready, n + 1)
                    for m, bank, done in ((1, b_k, k_done), (0, b_r, r_done)):
                        hold(pe, kk_ready if m else sg_ready, n)
                        q = 0
                        for t, off in ((0, 1), (1, 0)):
                            for wi, xi in ((0, 0), (0, 1), (1, 0)):
                                last = nc.tensor.matmul(bank[:, :], wm[:, m, t, wi, :], xs[b][xi][:, :, off:off + SEQ],
                                                        start=q == 0, stop=q == 5)
                                q += 1
                        last.then_inc(done, 1)
                if live(n - 1, UNITS):
                    hold(pe, kk_ready, n)
                    hold(pe, gated_ready, n - 1)
                    nc.tensor.matmul(b_v[:, :], wv[:, :], kk[1 - b][:, :], start=True, stop=True).then_inc(v_done, 1)
            run(pe, step)

        @block.scalar
        def _(act):
            def step(i, s):
                n, b = 2 * i + s, s % 2
                if live(n, UNITS):
                    hold(act, k_done, n + 1)
                    hold(act, kk_ready, n)
                    nc.scalar.activation(kr[:, :], b_k[:, :], ACT.Relu).then_inc(kr_ready, 1)
                    hold(act, r_done, n + 1)
                    hold(act, gated_ready, n - 1)
                    nc.scalar.activation(sg[b][:, :], b_r[:, :], ACT.Sigmoid).then_inc(sg_ready, 1)
            run(act, step)

        @block.vector
        def _(dve):
            def step(i, s):
                n, b = 2 * i + s, s % 2
                if live(n + 1, UNITS):
                    hold(dve, r_done, n)
                    xb = x[:, bass.ds((n + 1) * UNIT, UNIT)].rearrange("p (b t) -> p b t", t=SEQ)
                    high, low = xs[1 - b][0][:, :, 1:SEQ + 1], xs[1 - b][1][:, :, 1:SEQ + 1]
                    nc.vector.tensor_scalar(high, xb, 1.0, None, ALU.mult).then_inc(xs_high, 1)
                    hold(dve, xs_high, n + 2)
                    nc.vector.tensor_tensor(low, xb, high.bitcast(FP32), ALU.subtract).then_inc(xs_ready, 1)
                if live(n, UNITS):
                    hold(dve, kr_ready, n + 1)
                    hold(dve, v_done, n - 1)
                    nc.vector.tensor_tensor(kk[b][:, :], b_k[:, :], kr[:, :], ALU.mult).then_inc(kk_ready, 1)
                if live(n - 1, UNITS):
                    hold(dve, sg_ready, n)
                    hold(dve, v_done, n)
                    hold(dve, y_ready, n - 1)
                    nc.vector.tensor_tensor(gated[:, :], b_v[:, :], sg[1 - b][:, :], ALU.mult).then_inc(gated_ready, 1)
                    hold(dve, gated_ready, n)
                    xb = x[:, bass.ds((n - 1) * UNIT, UNIT)]
                    nc.vector.tensor_tensor(xb, gated[:, :], xb, ALU.add).then_inc(y_ready, 1)
            run(dve, step)


def mlp(nc, layer, c, src, x, w1, w2, kind, b1, out_scale, out_bias):
    M = 4
    with ExitStack() as stack:
        k = Scope(nc, stack, layer)
        xs = [[k.sb(f"xs{b}{p}", [P, UNIT], F32R) for p in range(2)] for b in range(2)]
        hid = k.sb("hid", [P, M, UNIT])
        relu = k.sb("relu", [P, 2, UNIT])
        b_h = [k.bank(f"b_h{m}") for m in range(M)]
        b_z = [k.bank(f"b_z{m}") for m in range(2)]
        xs_high, xs_ready, h_done, relu_ready, hid_ready, z_done, y_ready = (
            k.sem(n) for n in ("xs_high", "xs_ready", "h_done", "relu_ready", "hid_ready", "z_done", "y_ready"))
        block = stack.enter_context(k.block())

        def run(eng, step):
            sweep(eng, 2, -1, 2, UNITS // 2 - 1, UNITS // 2 + 1, step)

        @block.tensor
        def _(pe):
            def step(i, s):
                n, b = 2 * i + s, s % 2
                if live(n - 1, UNITS):
                    hold(pe, y_ready, n - 2)
                    for m in range(M):
                        hold(pe, hid_ready, M * (n - 1) + m + 1)
                        last = nc.tensor.matmul(b_z[1 - b][:, :], w2[:, m, :], hid[:, m, :], start=m == 0, stop=m == M - 1)
                    last.then_inc(z_done, 1)
                if live(n, UNITS):
                    hold(pe, xs_ready, n + 1)
                    for m in range(M):
                        hold(pe, hid_ready, M * (n - 1) + m + 1)
                        for q, (wi, xi) in enumerate(((0, 0), (0, 1), (1, 0))):
                            last = nc.tensor.matmul(b_h[m][:, :], w1[wi][:, m * P:(m + 1) * P], xs[b][xi][:, :],
                                                    start=q == 0, stop=q == 2)
                        last.then_inc(h_done, 1)
            run(pe, step)

        @block.scalar
        def _(act):
            def step(i, s):
                n, b = 2 * i + s, s % 2
                if live(n, UNITS):
                    for m in range(M):
                        hold(act, h_done, M * n + m + 1)
                        if kind == "silu":
                            hold(act, z_done, n)
                            nc.scalar.activation(hid[:, m, :], b_h[m][:, :], ACT.Silu, bias=b1[:, m:m + 1])\
                                .then_inc(hid_ready, 1)
                        else:
                            hold(act, hid_ready, M * n + m - 1)
                            nc.scalar.activation(relu[:, m % 2, :], b_h[m][:, :], ACT.Relu).then_inc(relu_ready, 1)
            run(act, step)

        @block.vector
        def _(dve):
            def step(i, s):
                n, b = 2 * i + s, s % 2
                if live(n + 1, UNITS):
                    hold(dve, h_done, M * n)
                    xb = src[:, bass.ds((n + 1) * UNIT, UNIT)]
                    nc.vector.tensor_scalar(xs[1 - b][0][:, :], xb, 1.0, None, ALU.mult).then_inc(xs_high, 1)
                    hold(dve, xs_high, n + 2)
                    nc.vector.tensor_tensor(xs[1 - b][1][:, :], xb, xs[1 - b][0][:, :].bitcast(FP32),
                                            ALU.subtract).then_inc(xs_ready, 1)
                if live(n - 1, UNITS):
                    hold(dve, z_done, n)
                    xb = x[:, bass.ds((n - 1) * UNIT, UNIT)]
                    if out_bias is None:
                        nc.vector.scalar_tensor_tensor(xb, b_z[1 - b][:, :], out_scale[:, 0:1], xb, ALU.mult, ALU.add)\
                            .then_inc(y_ready, 1)
                    else:
                        nc.vector.scalar_tensor_tensor(xb, b_z[1 - b][:, :], out_bias[:, 0:1], xb, ALU.add, ALU.add)\
                            .then_inc(y_ready, 1)
                if live(n, UNITS) and kind == "relu2":
                    for m in range(M):
                        hold(dve, relu_ready, M * n + m + 1)
                        hold(dve, z_done, n)
                        nc.vector.tensor_tensor(hid[:, m, :], b_h[m][:, :], relu[:, m % 2, :], ALU.mult)\
                            .then_inc(hid_ready, 1)
            run(dve, step)


def quantised_mlp(nc, c, x, w):
    layer = "l1f"
    with ExitStack() as stack:
        k = Scope(nc, stack, layer)
        w1 = [k.sb(f"w1{p}", [P, 4 * P], F32R) for p in range(2)]
        w2 = k.sb("w2", [P, 4, P])
        b1, b2 = k.sb("b1", [P, 4]), k.sb("b2", [P, 1])
        with ExitStack() as staging:
            ks = Scope(nc, staging, layer + "_s")
            q1, q2 = ks.sb("q1", [P, 4 * P], I32), ks.sb("q2", [P, 4, P], I32)
            s1, s2 = ks.sb("s1", [P, 4 * P]), ks.sb("s2", [P, 4, P])
            b1_raw, gamma, beta, b2_raw = ks.sb("b1r", [P, 4]), ks.sb("gamma", [P, 1]), ks.sb("beta", [P, 1]), ks.sb("b2r", [P, 1])
            d1, d2, full = ks.sb("d1", [P, 4 * P]), ks.sb("d2", [P, 4, P]), ks.sb("full", [P, 4 * P])
            pb = ks.bank("pb")
            loaded, chain, beta_done = ks.sem("loaded"), ks.sem("dequantised"), ks.sem("beta_done")
            pairs = ((q1[:, :], "fc1_q"), (q2[:, :, :], "fc2_q"), (s1[:, :], "fc1_s"), (s2[:, :, :], "fc2_s"),
                     (b1_raw[:, :], "b1"), (gamma[:, :], "gamma"), (beta[:, :], "beta"), (b2_raw[:, :], "b2"))
            with ks.block() as block:
                @block.sync
                def _(sp):
                    for dst, name in pairs:
                        sp.dma_start(dst, w[name]).then_inc(loaded, 16)

                @block.vector
                def _(dve):
                    dve.wait_ge(loaded, 16 * len(pairs))
                    nc.vector.tensor_scalar(d1[:, :], q1[:, :], -128.0, None, ALU.add).then_inc(chain, 1)
                    nc.vector.tensor_scalar(d2[:, :, :], q2[:, :, :], -128.0, 0.25, ALU.add, ALU.mult).then_inc(chain, 1)
                    nc.vector.tensor_scalar(b2[:, :], b2_raw[:, :], 0.25, None, ALU.mult)
                    dve.wait_ge(chain, 2)
                    nc.vector.tensor_tensor(full[:, :], d1[:, :], s1[:, :], ALU.mult).then_inc(chain, 1)
                    nc.vector.tensor_tensor(w2[:, :, :], d2[:, :, :], s2[:, :, :], ALU.mult)
                    dve.wait_ge(chain, 3)
                    nc.vector.tensor_scalar(s1[:, :], full[:, :], gamma[:, 0:1], None, ALU.mult).then_inc(chain, 1)
                    dve.wait_ge(chain, 4)
                    nc.vector.tensor_copy(w1[0][:, :], s1[:, :]).then_inc(chain, 1)
                    dve.wait_ge(chain, 5)
                    nc.vector.tensor_tensor(w1[1][:, :], s1[:, :], w1[0][:, :].bitcast(FP32), ALU.subtract)
                    dve.wait_ge(beta_done, 1)
                    nc.vector.tensor_tensor(b1[:, :], pb[:, 0:4], b1_raw[:, :], ALU.add)

                @block.tensor
                def _(pe):
                    pe.wait_ge(chain, 3)
                    for m in range(4):
                        last = nc.tensor.matmul(pb[:, m:m + 1], full[:, m * P:(m + 1) * P], beta[:, 0:1], start=m == 0,
                                                stop=True, skip_group_check=True)
                    last.then_inc(beta_done, 1)
        h = k.sb("h", [P, TOKENS])
        layer_norm(nc, layer + "n", c, x, h)
        mlp(nc, layer, c, h, x, w1, w2, "silu", b1, None, b2)


ROUND = 1.5 * 2.0 ** 23


def ternary_mlp(nc, c, x, w):
    layer = "l3f"
    with ExitStack() as stack:
        k = Scope(nc, stack, layer)
        w1 = [k.sb(f"w1{p}", [P, 4 * P], F32R) for p in range(2)]
        w2 = k.sb("w2", [P, 4, P])
        scale2 = k.sb("scale2", [P, 1])
        with ExitStack() as staging:
            ks = Scope(nc, staging, layer + "_s")
            fc, proj = ks.sb("fc", [P, 4 * P]), ks.sb("proj", [P, 4 * P])
            size_fc, size_proj = ks.sb("size_fc", [P, 4 * P]), ks.sb("size_proj", [P, 4 * P])
            scale, inverse = ks.sb("scale", [P, 5 * P]), ks.sb("inverse", [P, 5 * P])
            r1, r2, low_rank = ks.sb("r1", [P, 4 * P]), ks.sb("r2", [P, 4 * P]), ks.sb("low_rank", [P, 4 * P])
            bt, v, ut, bv = ks.sb("bt", [16, 16]), ks.sb("v", [16, P]), ks.sb("ut", [16, 4 * P]), ks.sb("bv", [16, P])
            gate = ks.sb("gate", [P, 1])
            b_fc, b_proj, b_col, b_bv, b_low = (ks.bank("b_" + n) for n in ("fc", "proj", "col", "bv", "low"))
            loaded, sizes, means, bv_done, bv_ready, low_done, chain = (
                ks.sem("s_" + n) for n in ("loaded", "sizes", "means", "bv_done", "bv_ready", "low_done", "rounded"))
            pairs = ((fc[:, :], "w_fc"), (proj[:, :], "w_proj"), (bt[:, :], "bt"), (v[:, :], "v"), (ut[:, :], "ut"),
                     (gate[:, :], "gate"))
            with ks.block() as block:
                @block.sync
                def _(sp):
                    for dst, name in pairs:
                        sp.dma_start(dst, w[name]).then_inc(loaded, 16)

                @block.scalar
                def _(act):
                    act.wait_ge(loaded, 16 * len(pairs))
                    nc.scalar.activation(size_fc[:, :], fc[:, :], ACT.Abs).then_inc(sizes, 1)
                    nc.scalar.activation(size_proj[:, :], proj[:, :], ACT.Abs).then_inc(sizes, 1)

                @block.tensor
                def _(pe):
                    pe.wait_ge(loaded, 16 * len(pairs))
                    nc.tensor.matmul(b_bv[0:16, 0:P], bt[:, :], v[:, :], start=True, stop=True).then_inc(bv_done, 1)
                    pe.wait_ge(sizes, 2)
                    nc.tensor.matmul(b_fc[:, :], c.mean[:, :], size_fc[:, :], start=True, stop=True).then_inc(means, 1)
                    for m in range(4):
                        last = nc.tensor.matmul(b_proj[:, 0:P], c.mean[:, :], size_proj[:, m * P:(m + 1) * P],
                                                start=m == 0, stop=m == 3)
                    last.then_inc(means, 1)
                    for m in range(4):
                        last = nc.tensor.matmul(b_col[:, 0:1], size_proj[:, m * P:(m + 1) * P], c.mean[:, 0:1],
                                                start=m == 0, stop=m == 3)
                    last.then_inc(means, 1)
                    pe.wait_ge(bv_ready, 1)
                    nc.tensor.matmul(b_low[:, :], bv[:, :], ut[:, :], start=True, stop=True).then_inc(low_done, 1)

                @block.vector
                def _(dve):
                    dve.wait_ge(bv_done, 1)
                    nc.vector.tensor_copy(bv[:, :], b_bv[0:16, 0:P]).then_inc(bv_ready, 1)
                    dve.wait_ge(means, 3)
                    nc.vector.tensor_scalar(scale[:, 0:4 * P], b_fc[:, :], 1e-5, None, ALU.max).then_inc(chain, 1)
                    nc.vector.tensor_scalar(scale[:, 4 * P:5 * P], b_proj[:, 0:P], 0.25, 1e-5, ALU.mult, ALU.max).then_inc(chain, 1)
                    nc.vector.tensor_scalar(scale2[:, :], b_col[:, 0:1], 0.25, 1e-5, ALU.mult, ALU.max)
                    dve.wait_ge(chain, 2)
                    nc.vector.reciprocal(inverse[:, :], scale[:, :]).then_inc(chain, 1)
                    dve.wait_ge(chain, 3)
                    nc.vector.tensor_tensor(r1[:, :], fc[:, :], inverse[:, 0:4 * P], ALU.mult).then_inc(chain, 1)
                    for m in range(4):
                        nc.vector.tensor_tensor(r2[:, m * P:(m + 1) * P], proj[:, m * P:(m + 1) * P],
                                                inverse[:, 4 * P:5 * P], ALU.mult).then_inc(chain, 1)
                    dve.wait_ge(chain, 8)
                    for n, (r, t) in enumerate(((r1, size_fc), (r2, size_proj))):
                        nc.vector.tensor_scalar(t[:, :], r[:, :], -1.0, 1.0, ALU.max, ALU.min).then_inc(chain, 1)
                        dve.wait_ge(chain, 9 + 2 * n)
                        nc.vector.tensor_scalar(r[:, :], t[:, :], ROUND, None, ALU.add).then_inc(chain, 1)
                        dve.wait_ge(chain, 10 + 2 * n)
                    nc.vector.tensor_scalar(size_fc[:, :], r1[:, :], -ROUND, None, ALU.add).then_inc(chain, 1)
                    nc.vector.tensor_scalar(w2[:, :, :], r2[:, :].rearrange("p (m o) -> p m o", m=4), -ROUND, None, ALU.add)
                    dve.wait_ge(low_done, 1)
                    nc.vector.tensor_scalar(low_rank[:, :], b_low[:, :], gate[:, 0:1], None, ALU.mult).then_inc(chain, 1)
                    dve.wait_ge(chain, 14)
                    nc.vector.tensor_tensor(r1[:, :], size_fc[:, :], scale[:, 0:4 * P], ALU.mult).then_inc(chain, 1)
                    dve.wait_ge(chain, 15)
                    nc.vector.tensor_tensor(fc[:, :], r1[:, :], low_rank[:, :], ALU.add).then_inc(chain, 1)
                    dve.wait_ge(chain, 16)
                    nc.vector.tensor_copy(w1[0][:, :], fc[:, :]).then_inc(chain, 1)
                    dve.wait_ge(chain, 17)
                    nc.vector.tensor_tensor(w1[1][:, :], fc[:, :], w1[0][:, :].bitcast(FP32), ALU.subtract)
        mlp(nc, layer, c, x, x, w1, w2, "relu2", None, scale2, None)


def gated_mlp(nc, c, x, w):
    layer = "l2f"
    M = 4
    with ExitStack() as stack:
        k = Scope(nc, stack, layer)
        w12 = [k.sb(f"w12{p}", [P, 8 * P], F32R) for p in range(2)]
        wh = [[k.sb(f"wh{n}{p}", [P, 16 * P], F32R) for p in range(2)] for n in range(2)]
        w3 = [k.sb(f"w3{p}", [P, 4 * P], F32R) for p in range(2)]
        scales = k.sb("scales", [P, 17])
        half_s1, half_s12 = k.sb("half_s1", [P, 4]), k.sb("half_s12", [P, 4])
        with ExitStack() as staging:
            ks = Scope(nc, staging, layer + "_s")
            s12 = ks.sb("w12", [P, 8 * P])
            sh = [ks.sb(f"wh{n}", [P, 16 * P]) for n in range(2)]
            s3 = ks.sb("w3", [P, 4 * P])
            load_and_split(nc, ks, "load", [
                (w["w12"], s12[:, :], w12[0][:, :], w12[1][:, :]),
                (w["h1"], sh[0][:, :], wh[0][0][:, :], wh[0][1][:, :]),
                (w["h2"], sh[1][:, :], wh[1][0][:, :], wh[1][1][:, :]),
                (w["w3"], s3[:, :], w3[0][:, :], w3[1][:, :]),
                (w["scales"], scales[:, :], None, None)])
            halved = ks.sem("halved")
            with ks.block() as block:
                @block.vector
                def _(dve):
                    nc.vector.tensor_scalar(half_s1[:, :], scales[:, 0:4], 0.5, None, ALU.mult).then_inc(halved, 1)
                    dve.wait_ge(halved, 1)
                    nc.vector.tensor_tensor(half_s12[:, :], half_s1[:, :], scales[:, 4:8], ALU.mult)

        xs = [[k.sb(f"xs{b}{p}", [P, UNIT], F32R) for p in range(2)] for b in range(2)]
        act_out = [[k.sb(f"act{n}{p}", [P, M, UNIT], F32R) for p in range(2)] for n in range(3)]
        tanh = k.sb("tanh", [P, 2, UNIT])
        half = k.sb("half", [P, 2, UNIT])
        prod = k.sb("prod", [P, 2, UNIT])
        gelu = k.sb("gelu", [P, 2, UNIT])
        b_h = [k.bank(f"b_h{m}") for m in range(2)]
        b_a = [[k.bank(f"b_a{m}{q}") for q in range(2)] for m in range(2)]
        b_z = k.bank("b_z")
        (xs_high, xs_ready, a_done, tanh_ready, half_ready, prod_ready, a_high, a_ready, h_done, gelu_ready, h_high,
         h_ready, z_done, y_ready) = (
            k.sem(n) for n in ("xs_high", "xs_ready", "a_done", "tanh_ready", "half_ready", "prod_ready", "a_high",
                               "a_ready", "h_done", "gelu_ready", "h_high", "h_ready", "z_done", "y_ready"))
        block = stack.enter_context(k.block())
        PASSES = ((0, 0), (0, 1), (1, 0))

        def run(eng, step):
            sweep(eng, 2, -1, 2, UNITS // 2 - 1, UNITS // 2 + 2, step)

        def h1_tiles(n):
            if isinstance(n, int):
                return M * min(max(n - 2, 0), UNITS) + M * min(max(n - 1, 0), UNITS)
            return 2 * M * n - 3 * M

        @block.tensor
        def _(pe):
            def step(i, s):
                n, b = 2 * i + s, s % 2
                if live(n - 3, UNITS):
                    hold(pe, h_ready, h1_tiles(n - 1) + (M if live(n - 3, UNITS) else 0))
                    hold(pe, y_ready, n - 3)
                    q = 0
                    for m in range(M):
                        for wi, xi in PASSES:
                            last = nc.tensor.matmul(b_z[:, :], w3[wi][:, m * P:(m + 1) * P], act_out[2][xi][:, m, :],
                                                    start=q == 0, stop=q == 3 * M - 1)
                            q += 1
                    last.then_inc(z_done, 1)
                done = h1_tiles(n)
                for layer_n, unit in ((1, n - 2), (0, n - 1)):
                    if not live(unit, UNITS):
                        continue
                    if layer_n == 1:
                        hold(pe, h_ready, h1_tiles(n))
                    else:
                        hold(pe, a_ready, M * n)
                    for m in range(M):
                        hold(pe, h_ready, done - 1)
                        q = 0
                        for kt in range(M):
                            for wi, xi in PASSES:
                                last = nc.tensor.matmul(b_h[m % 2][:, :], wh[layer_n][wi][:, (m * M + kt) * P:(m * M + kt + 1) * P],
                                                        act_out[layer_n][xi][:, kt, :], start=q == 0, stop=q == 3 * M - 1)
                                q += 1
                        last.then_inc(h_done, 1)
                        done = done + 1
                if live(n, UNITS):
                    hold(pe, xs_ready, n + 1)
                    for m in range(M):
                        hold(pe, prod_ready, M * n + m - 1)
                        for side in range(2):
                            for q, (wi, xi) in enumerate(PASSES):
                                tile = slice((side * M + m) * P, (side * M + m + 1) * P)
                                last = nc.tensor.matmul(b_a[m % 2][side][:, :], w12[wi][:, tile], xs[b][xi][:, :],
                                                        start=q == 0, stop=q == 2)
                        last.then_inc(a_done, 1)
            run(pe, step)

        @block.scalar
        def _(act):
            def step(i, s):
                n = 2 * i + s
                done = h1_tiles(n)
                for layer_n, unit in ((1, n - 2), (0, n - 1)):
                    if not live(unit, UNITS):
                        continue
                    for m in range(M):
                        hold(act, h_done, done + 1)
                        hold(act, h_ready, done - 1)
                        nc.scalar.activation(gelu[:, m % 2, :], b_h[m % 2][:, :], ACT.Gelu,
                                             scale=scales[:, 8 + 4 * layer_n + m:9 + 4 * layer_n + m]).then_inc(gelu_ready, 1)
                        done = done + 1
                        hold(act, gelu_ready, done)
                        if layer_n == 1:
                            hold(act, z_done, n - 2)
                        else:
                            hold(act, h_done, h1_tiles(n) + (M if live(n - 2, UNITS) else 0))
                        nc.scalar.activation(act_out[layer_n + 1][0][:, m, :], gelu[:, m % 2, :], ACT.Copy)\
                            .then_inc(h_high, 1)
                if live(n, UNITS):
                    for m in range(M):
                        hold(act, a_done, M * n + m + 1)
                        hold(act, half_ready, M * n + m - 1)
                        nc.scalar.activation(tanh[:, m % 2, :], b_a[m % 2][0][:, :], ACT.Tanh,
                                             scale=half_s1[:, m:m + 1]).then_inc(tanh_ready, 1)
                        hold(act, prod_ready, M * n + m + 1)
                        hold(act, h_done, h1_tiles(n + 1))
                        nc.scalar.activation(act_out[0][0][:, m, :], prod[:, m % 2, :], ACT.Copy).then_inc(a_high, 1)
            run(act, step)

        @block.vector
        def _(dve):
            def step(i, s):
                n, b = 2 * i + s, s % 2
                if live(n + 1, UNITS):
                    hold(dve, a_done, M * n)
                    xb = x[:, bass.ds((n + 1) * UNIT, UNIT)]
                    nc.vector.tensor_scalar(xs[1 - b][0][:, :], xb, 1.0, None, ALU.mult).then_inc(xs_high, 1)
                    hold(dve, xs_high, n + 2)
                    nc.vector.tensor_tensor(xs[1 - b][1][:, :], xb, xs[1 - b][0][:, :].bitcast(FP32),
                                            ALU.subtract).then_inc(xs_ready, 1)
                if live(n - 3, UNITS):
                    hold(dve, z_done, n - 2)
                    xb = x[:, bass.ds((n - 3) * UNIT, UNIT)]
                    nc.vector.scalar_tensor_tensor(xb, b_z[:, :], scales[:, 16:17], xb, ALU.mult, ALU.add)\
                        .then_inc(y_ready, 1)
                done = h1_tiles(n)
                for layer_n, unit in ((1, n - 2), (0, n - 1)):
                    if not live(unit, UNITS):
                        continue
                    for m in range(M):
                        hold(dve, h_high, done + 1)
                        nc.vector.tensor_tensor(act_out[layer_n + 1][1][:, m, :], gelu[:, m % 2, :],
                                                act_out[layer_n + 1][0][:, m, :].bitcast(FP32), ALU.subtract)\
                            .then_inc(h_ready, 1)
                        done = done + 1
                if live(n, UNITS):
                    for m in range(M):
                        hold(dve, tanh_ready, M * n + m + 1)
                        nc.vector.scalar_tensor_tensor(half[:, m % 2, :], tanh[:, m % 2, :], 1.0, b_a[m % 2][0][:, :],
                                                       ALU.add, ALU.mult).then_inc(half_ready, 1)
                        hold(dve, half_ready, M * n + m + 1)
                        hold(dve, a_high, M * n + m - 1)
                        nc.vector.scalar_tensor_tensor(prod[:, m % 2, :], b_a[m % 2][1][:, :], half_s12[:, m:m + 1],
                                                       half[:, m % 2, :], ALU.mult, ALU.mult).then_inc(prod_ready, 1)
                        hold(dve, a_high, M * n + m + 1)
                        nc.vector.tensor_tensor(act_out[0][1][:, m, :], prod[:, m % 2, :],
                                                act_out[0][0][:, m, :].bitcast(FP32), ALU.subtract).then_inc(a_ready, 1)
            run(dve, step)


def chunked_attention(nc, c, x, w):
    layer = "l3a"
    H, CHUNK = 8, 64
    WIDTH = H * P
    PAIRS = H // 2
    with ExitStack() as stack:
        k = Scope(nc, stack, layer)
        wqkv = [[k.sb(f"w{n}{p}", [P, WIDTH], F32R) for p in range(2)] for n in ("q", "k", "v")]
        wg = [k.sb(f"wg{p}", [P, H], F32R) for p in range(2)]
        wo = k.sb("wo", [P, H, P])
        bg, gain = k.sb("bg", [P, H]), k.sb("gain", [P, 1])
        between = k.sb("between", [P, 3, P])
        first_half = k.sb("first_half", [P, 1])
        mask = k.sb("mask", [P, H, CHUNK], BF16)
        with ExitStack() as staging:
            ks = Scope(nc, staging, layer + "_s")
            raw = [ks.sb(f"raw{n}", [P, WIDTH]) for n in range(3)]
            rawg, rawm = ks.sb("rawg", [P, H]), ks.sb("rawm", [P, CHUNK])
            load_and_split(nc, ks, "load",
                           [(w[name], raw[n][:, :], wqkv[n][0][:, :], wqkv[n][1][:, :]) for n, name in enumerate(("wq", "wk", "wv"))]
                           + [(w["wg"], rawg[:, :], wg[0][:, :], wg[1][:, :]), (w["wo"], wo[:, :, :], None, None),
                              (w["bg"], bg[:, :], None, None), (w["gain"], gain[:, :], None, None),
                              (w["between"], between[:, :, :], None, None), (w["first_half"], first_half[:, :], None, None),
                              (w["mask"], rawm[:, :], None, None)])
            with ks.block() as block:
                @block.vector
                def _(dve):
                    for h in range(H):
                        nc.vector.tensor_copy(mask[:, h, :], rawm[:, :])

        xs = [k.sb(f"xs{p}", [P, SEQ], F32R) for p in range(2)]
        sq = k.sb("sq", [P, WIDTH])
        ss, root, rms = k.sb("ss", [P, H]), k.sb("root", [P, H]), k.sb("rms", [P, H])
        rms_gain = k.sb("rms_gain", [P, H])
        qkn = [k.sb(f"qkn{n}", [P, WIDTH]) for n in range(4)]
        vt = k.sb("vt", [P, 2, WIDTH])
        qt, kt = k.sb("qt", [P, H, SEQ]), k.sb("kt", [P, H, SEQ])
        z, ze, lg = k.sb("z", [P, 2, H]), k.sb("ze", [P, 2, H]), k.sb("lg", [P, 2, H])
        decay = k.sb("decay", [P, 3, H])
        centred, probs = k.sb("centred", [P, 2, H, CHUNK]), k.sb("probs", [P, 2, H, CHUNK])
        top, total, inv = k.sb("top", [P, 2, H]), k.sb("total", [P, 2, H]), k.sb("inv", [P, 2, H])
        pn = [k.sb(f"pn{tb}", [P, H, P]) for tb in range(2)]
        ptt = k.sb("ptt", [P, H, 3 * HALF])
        yt = k.sb("yt", [P, H, SEQ])
        ring = [k.bank(f"ring{n}", 2) for n in range(2)]
        b_d = [k.bank(f"b_d{n}") for n in range(2)]
        b_x = [k.bank(f"b_x{n}") for n in range(2)]
        (presets, xs_high, xs_ready, g_done, z_ready, z_low, ze_ready, lg_ready, l_done, decay_ready, qk_done, sq_ready,
         ss_ready, root_ready, rms_ready, rg_ready, qk_ready, d_done, top_ready, c_ready, probs_ready, total_ready,
         inv_ready, pn_ready, x_done, x_ready, pt_done, pt_ready, y_done, y_ready, f_done, f_ready, v_done, v_ready,
         tr_done, qt_ready, kt_ready) = (k.sem(n) for n in (
             "presets", "xs_high", "xs_ready", "g_done", "z_ready", "z_low", "ze_ready", "lg_ready", "l_done", "decay_ready",
             "qk_done", "sq_ready", "ss_ready", "root_ready", "rms_ready", "rg_ready", "qk_ready", "d_done", "top_ready",
             "c_ready", "probs_ready", "total_ready", "inv_ready", "pn_ready", "x_done", "x_ready", "pt_done",
             "pt_ready", "y_done", "y_ready", "f_done", "f_ready", "v_done", "v_ready", "tr_done", "qt_ready", "kt_ready"))
        block = stack.enter_context(k.block())
        B = BATCHES

        def run(eng, step):
            sweep(eng, 1, -1, 2, B - 1, B + 1, lambda i, s: step(i))

        def at(i, count_now, count_before):
            return count_now if live(i, B) else count_before

        @block.gpsimd
        def _(pool):
            for tb in range(2):
                nc.gpsimd.memset(pn[tb][:, :, :], 0.0).then_inc(presets, 1)

        @block.tensor
        def _(pe):
            pe.wait_ge(presets, 2)

            def project(bank, weights, tb):
                for half in range(2):
                    for q, (xi, wi) in enumerate(((0, 0), (1, 0), (0, 1))):
                        last = nc.tensor.matmul(bank[:, half * BANK:(half + 1) * BANK], xs[xi][:, tb * P:(tb + 1) * P],
                                                weights[wi][:, half * BANK:(half + 1) * BANK], start=q == 0, stop=q == 2)
                return last

            def step(i):
                j = i - 1
                if live(i, B):
                    hold(pe, xs_ready, i + 1)
                    hold(pe, decay_ready, i)
                    hold(pe, x_ready, PAIRS * (i - 1))
                    for tb in range(2):
                        for q, (xi, wi) in enumerate(((0, 0), (1, 0), (0, 1))):
                            last = nc.tensor.matmul(b_x[1][:, tb * H:(tb + 1) * H], xs[xi][:, tb * P:(tb + 1) * P], wg[wi][:, :],
                                                    start=q == 0 and tb == 0, stop=q == 2, skip_group_check=True)
                    last.then_inc(g_done, 1)
                if live(j, B):
                    hold(pe, qt_ready, 2 * i)
                    hold(pe, kt_ready, 2 * i)
                    hold(pe, y_ready, PAIRS * j)
                    for tb in range(2):
                        nc.tensor.matmul(b_d[tb][:, :], c.ident_b[:, :], mask[:, :, :], start=True, stop=True,
                                         skip_group_check=True)
                        for h in range(H):
                            for half in range(2):
                                t = slice(tb * P + half * CHUNK, tb * P + (half + 1) * CHUNK)
                                last = nc.tensor.matmul(b_d[tb][half * CHUNK:(half + 1) * CHUNK, h * CHUNK:(h + 1) * CHUNK],
                                                        qt[:, h, t], kt[:, h, t], start=False, stop=True,
                                                        skip_group_check=True)
                        last.then_inc(d_done, 1)
                    hold(pe, z_ready, at(i, i + 1, i))
                    hold(pe, decay_ready, i)
                    hold(pe, f_ready, j)
                    for p in range(PAIRS):
                        hold(pe, x_ready, PAIRS * j + p - 1)
                        bank = b_x[p % 2]
                        for hh in range(2):
                            h = 2 * p + hh
                            nc.tensor.matmul(bank[:, hh * SEQ:hh * SEQ + 192], kt[:, h, 0:HALF], qt[:, h, CHUNK:SEQ],
                                             start=hh == 0, stop=True, skip_group_check=True)
                            last = nc.tensor.matmul(bank[:, hh * SEQ + 192:(hh + 1) * SEQ], kt[:, h, HALF:SEQ],
                                                    qt[:, h, 192:SEQ], start=False, stop=True, skip_group_check=True)
                        last.then_inc(x_done, 1)
                if live(i, B):
                    for n in range(4):
                        if n < 2:
                            hold(pe, (qt_ready, kt_ready)[n], 2 * i)
                        else:
                            hold(pe, qk_ready, 4 * i + n - 1)
                        project(ring[n % 2], wqkv[n % 2], n // 2).then_inc(qk_done, 1)
                if live(j, B):
                    for tb in range(2):
                        hold(pe, pn_ready, 4 * j + 2 * tb + 2)
                        hold(pe, qk_ready, at(i, 4 * i + 3 + tb, 4 * i))
                        for h in range(H):
                            last = nc.tensor.transpose(ring[tb][:, h * P:(h + 1) * P], pn[tb][:, h, :], c.ident[:, :])
                        last.then_inc(pt_done, 1)
                    hold(pe, pt_ready, 2 * i)
                    hold(pe, c_ready, 2 * i)
                    for p in range(PAIRS):
                        hold(pe, y_ready, PAIRS * j + p - 1)
                        for hh in range(2):
                            h = 2 * p + hh
                            nc.tensor.matmul(b_d[p % 2][:, hh * SEQ:(hh + 1) * SEQ], vt[:, 0, h * P:(h + 1) * P], ptt[:, h, 0:SEQ],
                                             start=hh == 0, stop=True, skip_group_check=True)
                            last = nc.tensor.matmul(b_d[p % 2][:, hh * SEQ + HALF:(hh + 1) * SEQ], vt[:, 1, h * P:(h + 1) * P],
                                                    ptt[:, h, SEQ:3 * HALF], start=False, stop=True, skip_group_check=True)
                        last.then_inc(y_done, 1)
                    hold(pe, x_ready, PAIRS * i)
                    hold(pe, y_ready, PAIRS * i)
                    for h in range(H):
                        last = nc.tensor.matmul(b_x[0][:, 0:SEQ], wo[:, h, :], yt[:, h, :], start=h == 0, stop=h == H - 1)
                    last.then_inc(f_done, 1)
                if live(i, B):
                    for tb in range(2):
                        hold(pe, pt_ready, 2 * i - 1 + tb if not isinstance(i, int) or i > 0 else 0)
                        hold(pe, qk_ready, 4 * i + 3 + tb)
                        project(ring[tb], wqkv[2], tb).then_inc(v_done, 1)
                    hold(pe, lg_ready, i + 1)
                    hold(pe, x_ready, PAIRS * i)
                    for q, (n, tb, col) in enumerate(((0, 0, 0), (1, 0, 1), (2, 1, 1))):
                        last = nc.tensor.matmul(b_x[1][:, BANK // 2 + col * H:BANK // 2 + (col + 1) * H], between[:, n, :],
                                                lg[:, tb, :], start=q == 0, stop=q != 1, skip_group_check=True)
                    last.then_inc(l_done, 1)
                    for n in range(4):
                        hold(pe, qk_ready, 4 * i + n + 1)
                        if n < 2:
                            hold(pe, v_ready, 2 * i + n + 1)
                        else:
                            hold(pe, (qt_ready, kt_ready)[n - 2], 2 * i + 1)
                        for h in range(H):
                            last = nc.tensor.transpose(ring[n % 2][:, h * P:(h + 1) * P], qkn[n][:, h * P:(h + 1) * P], c.ident[:, :])
                        last.then_inc(tr_done, 1)
            run(pe, step)

        @block.scalar
        def _(act):
            act.wait_ge(presets, 2)

            def step(i):
                j = i - 1
                if live(i, B):
                    hold(act, z_low, i + 1)
                    nc.scalar.activation(ze[:, :, :], z[:, :, :], ACT.Exp, scale=-1.0).then_inc(ze_ready, 1)
                if live(j, B):
                    for tb in range(2):
                        hold(act, c_ready, 2 * j + tb + 1)
                        hold(act, pn_ready, 4 * j + 2 * tb - 2)
                        nc.scalar.activation(probs[:, tb, :, :], centred[:, tb, :, :], ACT.Exp,
                                             scale=P ** -0.5).then_inc(probs_ready, 1)
                if live(i, B):
                    for n in range(4):
                        hold(act, qk_done, 4 * i + n + 1)
                        hold(act, ss_ready, 4 * i + n)
                        nc.scalar.activation(sq[:, :], ring[n % 2][:, :], ACT.Square).then_inc(sq_ready, 1)
                        hold(act, ss_ready, 4 * i + n + 1)
                        hold(act, rms_ready, 4 * i + n)
                        nc.scalar.activation(root[:, :], ss[:, :], ACT.Sqrt, scale=1.0 / P, bias=c.eps[:, 1:2])\
                            .then_inc(root_ready, 1)
                    hold(act, ze_ready, i + 1)
                    hold(act, l_done, i)
                    nc.scalar.activation(lg[:, :, :], ze[:, :, :], ACT.Ln, bias=1.0).then_inc(lg_ready, 1)
                if live(j, B):
                    hold(act, f_done, j)
                    for p in range(PAIRS):
                        hold(act, y_done, PAIRS * j + p + 1)
                        nc.scalar.activation(yt[:, 2 * p:2 * p + 2, :], b_d[p % 2][:, :].rearrange("p (h t) -> p h t", t=SEQ),
                                             ACT.Copy).then_inc(y_ready, 1)
                if live(i, B):
                    for tb in range(2):
                        hold(act, v_done, 2 * i + tb + 1)
                        nc.scalar.activation(vt[:, tb, :], ring[tb][:, :], ACT.Copy).then_inc(v_ready, 1)
                    hold(act, l_done, i + 1)
                    hold(act, x_ready, PAIRS * i)
                    nc.scalar.activation(decay[:, 1:3, :], b_x[1][:, BANK // 2:BANK // 2 + 2 * H].rearrange("p (c h) -> p c h", h=H),
                                         ACT.Exp, scale=-1.0).then_inc(decay_ready, 1)
                    for tb in range(2):
                        hold(act, tr_done, 4 * i + 2 * tb + 1)
                        hold(act, x_done, PAIRS * i)
                        nc.scalar.activation(qt[:, :, tb * P:(tb + 1) * P], ring[0][:, :].rearrange("p (h t) -> p h t", t=P),
                                             ACT.Copy).then_inc(qt_ready, 1)
            run(act, step)

        @block.vector
        def _(dve):
            nc.vector.tensor_scalar(decay[:, 0, :], bg[:, :], 0.0, first_half[:, 0:1], ALU.mult, ALU.add).then_inc(rg_ready, 1)
            dve.wait_ge(presets, 2)

            def step(i):
                j = i - 1
                if live(i, B):
                    hold(dve, g_done, i + 1)
                    hold(dve, ze_ready, i)
                    nc.vector.tensor_tensor(z[:, :, :], b_x[1][:, 0:2 * H].rearrange("p (b h) -> p b h", h=H),
                                            bg[:, :].unsqueeze(1).to_broadcast([P, 2, H]), ALU.add).then_inc(z_ready, 1)
                    hold(dve, z_ready, i + 1)
                    nc.vector.tensor_scalar(z[:, :, :], z[:, :, :], -85.0, None, ALU.max).then_inc(z_low, 1)
                if live(j, B):
                    for tb in range(2):
                        u = 2 * j + tb
                        hold(dve, d_done, u + 1)
                        scores = b_d[tb][:, :].rearrange("p (h s) -> p h s", s=CHUNK)
                        hold(dve, c_ready, u - 1)
                        nc.vector.tensor_reduce(top[:, tb, :], scores, AX.X, ALU.max).then_inc(top_ready, 1)
                        hold(dve, top_ready, u + 1)
                        hold(dve, probs_ready, u - 1)
                        nc.vector.tensor_tensor(centred[:, tb, :, :], scores, top[:, tb, :].unsqueeze(2).to_broadcast([P, H, CHUNK]),
                                                ALU.subtract).then_inc(c_ready, 1)
                    hold(dve, decay_ready, i)
                    hold(dve, y_done, PAIRS * j)
                    for p in range(PAIRS):
                        hold(dve, x_done, PAIRS * j + p + 1)
                        bank = b_x[p % 2][:, :].rearrange("p (h c t) -> p h c t", h=2, t=CHUNK)
                        for hh in range(2):
                            h = 2 * p + hh
                            nc.vector.tensor_tensor(ptt[:, h, CHUNK:SEQ].rearrange("p (c t) -> p c t", t=CHUNK), bank[:, hh, 0:3, :],
                                                    decay[:, :, h:h + 1].to_broadcast([P, 3, CHUNK]), ALU.mult)
                        nc.vector.tensor_scalar(ptt[:, 2 * p:2 * p + 2, SEQ + CHUNK:3 * HALF], bank[:, :, 3, :],
                                                first_half[:, 0:1], None, ALU.mult).then_inc(x_ready, 1)
                    for tb in range(2):
                        u = 2 * j + tb
                        hold(dve, probs_ready, u + 1)
                        hold(dve, inv_ready, u - 1)
                        nc.vector.tensor_reduce(total[:, tb, :], probs[:, tb, :, :], AX.X, ALU.add).then_inc(total_ready, 1)
                    for tb in range(2):
                        u = 2 * j + tb
                        hold(dve, total_ready, u + 1)
                        hold(dve, pn_ready, 2 * u - 2)
                        nc.vector.reciprocal(inv[:, tb, :], total[:, tb, :]).then_inc(inv_ready, 1)
                    for tb in range(2):
                        u = 2 * j + tb
                        hold(dve, inv_ready, u + 1)
                        hold(dve, pt_done, u - 1)
                        for half in range(2):
                            rows = slice(half * CHUNK, (half + 1) * CHUNK)
                            nc.vector.tensor_tensor(pn[tb][rows, :, half * CHUNK:(half + 1) * CHUNK], probs[rows, tb, :, :],
                                                    inv[rows, tb, :].unsqueeze(2).to_broadcast([CHUNK, H, CHUNK]),
                                                    ALU.mult).then_inc(pn_ready, 1)
                if live(i, B):
                    for n in range(4):
                        hold(dve, sq_ready, 4 * i + n + 1)
                        hold(dve, root_ready, 4 * i + n)
                        nc.vector.tensor_reduce(ss[:, :], sq[:, :].rearrange("p (h d) -> p h d", d=P), AX.X, ALU.add).then_inc(ss_ready, 1)
                        hold(dve, root_ready, 4 * i + n + 1)
                        hold(dve, qk_ready, 4 * i + n)
                        nc.vector.reciprocal(rms[:, :], root[:, :]).then_inc(rms_ready, 1)
                        hold(dve, rms_ready, 4 * i + n + 1)
                        scale = rms
                        if n % 2 == 0:
                            nc.vector.tensor_scalar(rms_gain[:, :], rms[:, :], gain[:, 0:1], None, ALU.mult).then_inc(rg_ready, 1)
                            hold(dve, rg_ready, 2 * i + n // 2 + 2)
                            scale = rms_gain
                        hold(dve, tr_done, 4 * (i - 1) + n + 1)
                        nc.vector.tensor_tensor(qkn[n][:, :].rearrange("p (h d) -> p h d", d=P),
                                                ring[n % 2][:, :].rearrange("p (h d) -> p h d", d=P),
                                                scale[:, :].unsqueeze(2).to_broadcast([P, H, P]), ALU.mult).then_inc(qk_ready, 1)
                if live(j, B):
                    hold(dve, x_ready, PAIRS * i)
                    for tb in range(2):
                        hold(dve, pt_done, 2 * j + tb + 1)
                        bank = ring[tb][:, :].rearrange("p (h t) -> p h t", t=P)
                        nc.vector.tensor_copy(ptt[:, :, tb * SEQ:tb * SEQ + CHUNK], bank[:, :, 0:CHUNK])
                        own = ptt[:, :, tb * SEQ + CHUNK:tb * SEQ + P]
                        nc.vector.tensor_tensor(own, bank[:, :, CHUNK:P], own, ALU.add).then_inc(pt_ready, 1)
                    hold(dve, f_done, i)
                    xb = x[:, bass.ds(j * SEQ, SEQ)]
                    nc.vector.tensor_tensor(xb, b_x[0][:, 0:SEQ], xb, ALU.add).then_inc(f_ready, 1)
                if live(i + 1, B):
                    hold(dve, v_done, 2 * (i + 1))
                    xb = x[:, bass.ds((i + 1) * SEQ, SEQ)]
                    nc.vector.tensor_scalar(xs[0][:, :], xb, 1.0, None, ALU.mult).then_inc(xs_high, 1)
                    hold(dve, xs_high, i + 2)
                    nc.vector.tensor_tensor(xs[1][:, :], xb, xs[0][:, :].bitcast(FP32), ALU.subtract).then_inc(xs_ready, 1)
                if live(i, B):
                    for tb in range(2):
                        hold(dve, tr_done, 4 * i + 2 * tb + 2)
                        hold(dve, x_done, PAIRS * i)
                        nc.vector.tensor_copy(kt[:, :, tb * P:(tb + 1) * P],
                                              ring[1][:, :].rearrange("p (h t) -> p h t", t=P)).then_inc(kt_ready, 1)
            run(dve, step)


class Constants:

    def __init__(self, nc, stack, dram):
        k = Scope(nc, stack, "const")
        self.centre = k.sb("centre", [P, P])
        self.mean = k.sb("mean", [P, P])
        self.ones = k.sb("ones", [P, 64])
        self.eps = k.sb("eps", [P, 3])
        self.low_rows = k.sb("low_rows", [P, 6])
        self.aug_low = k.sb("aug_low", [3, 1])
        self.ident_r = k.sb("ident_r", [P, P], F32R)
        self.ident = k.sb("ident", [P, P])
        self.ident_b = k.sb("ident_b", [P, P], BF16)
        self.mask_q = k.sb("mask_q", [P, 2, P], BF16)
        self.mask_k = k.sb("mask_k", [P, 2, P], BF16)
        self.aug_x = k.sb("aug_x", [3, SEQ], F32R)
        with ExitStack() as staging:
            ks = Scope(nc, staging, "const_s")
            mq, mk, ax = ks.sb("mq", [P, P]), ks.sb("mk", [P, P]), ks.sb("ax", [3, SEQ])
            loaded = ks.sem("loaded")
            pairs = [(self.centre, "centre"), (self.ident, "ident"), (mq, "mask_q"), (mk, "mask_k"),
                     (ax, "aug_x"), (self.low_rows, "low_rows"), (self.aug_low, "aug_low")]
            with ks.block() as block:
                @block.sync
                def _(sp):
                    for dst, name in pairs:
                        sp.dma_start(dst[:, :], dram[name]).then_inc(loaded, 16)
                    sp.wait_ge(loaded, 16 * len(pairs))

                @block.vector
                def _(dve):
                    nc.vector.memset(self.mean[:, :], 1.0 / P)
                    nc.vector.memset(self.ones[:, :], 1.0)
                    nc.vector.memset(self.eps[:, 0:1], EPS)
                    nc.vector.memset(self.eps[:, 1:2], 1e-6)
                    nc.vector.memset(self.eps[:, 2:3], EPS / 4)
                    dve.wait_ge(loaded, 16 * len(pairs))
                    nc.vector.tensor_copy(self.ident_r[:, :], self.ident[:, :])
                    nc.vector.tensor_copy(self.ident_b[:, :], self.ident[:, :])
                    nc.vector.tensor_copy(self.aug_x[:, :], ax[:, :])
                    for b in range(2):
                        nc.vector.tensor_copy(self.mask_q[:, b, :], mq[:, :])
                        nc.vector.tensor_copy(self.mask_k[:, b, :], mk[:, :])


L0_SHAPE = AttentionShape(dim=8, rows=32, v_width=32, scale=8 ** -0.5, biased=True, v_slots=(3,), o_tiles=4,
                          low_cols=(0, 1))
L1_SHAPE = AttentionShape(dim=64, rows=128, v_width=64, scale=0.125, biased=False, v_slots=(1, 2, 5, 6), o_tiles=8, lag=3,
                          low_cols=(4, 5))
L2_SHAPE = AttentionShape(dim=16, rows=64, v_width=32, scale=8 ** -0.5, biased=False, v_slots=(3,), o_tiles=4,
                          low_cols=(2, 3))


def program(nc, d, out):
    with ExitStack() as stack:
        k = Scope(nc, stack, "model")
        x = k.sb("x", [P, TOKENS])
        x_loaded, stored = k.sem("x_loaded"), k.sem("stored")
        c = Constants(nc, stack, d)
        with nc.Block() as block:
            @block.sync
            def _(sp):
                sp.dma_start(x[:, :], d["x"]).then_inc(x_loaded, 16)
                sp.wait_ge(x_loaded, 16)
        for run in STAGES:
            run(nc, c, x, d)
        with nc.Block() as block:
            @block.sync
            def _(sp):
                sp.dma_start(out, x[:, :]).then_inc(stored, 16)
                sp.wait_ge(stored, 16)


def group(d, prefix):
    return {name[len(prefix):]: ap for name, ap in d.items() if name.startswith(prefix)}


STAGES = [
    lambda nc, c, x, d: attention(nc, "l0a", c, x, group(d, "l0a_"), L0_SHAPE),
    lambda nc, c, x, d: layer_norm(nc, "ln0", c, x, x),
    lambda nc, c, x, d: reglu(nc, "l0f", c, x, group(d, "l0f_")),
    lambda nc, c, x, d: layer_norm(nc, "ln1", c, x, x),
    lambda nc, c, x, d: attention(nc, "l1a", c, x, group(d, "l1a_"), L1_SHAPE),
    lambda nc, c, x, d: layer_norm(nc, "ln2", c, x, x),
    lambda nc, c, x, d: quantised_mlp(nc, c, x, group(d, "l1f_")),
    lambda nc, c, x, d: layer_norm(nc, "ln3", c, x, x, eps=2),
    lambda nc, c, x, d: attention(nc, "l2a", c, x, group(d, "l2a_"), L2_SHAPE),
    lambda nc, c, x, d: layer_norm(nc, "ln4", c, x, x),
    lambda nc, c, x, d: gated_mlp(nc, c, x, group(d, "l2f_")),
    lambda nc, c, x, d: layer_norm(nc, "ln5", c, x, x),
    lambda nc, c, x, d: chunked_attention(nc, c, x, group(d, "l3a_")),
    lambda nc, c, x, d: layer_norm(nc, "ln6", c, x, x),
    lambda nc, c, x, d: ternary_mlp(nc, c, x, group(d, "l3f_")),
    lambda nc, c, x, d: layer_norm(nc, "ln7", c, x, x),
]


def head_tiles(np, w, rows, copies):
    dim = w.shape[2]
    tiles = np.zeros((w.shape[0], 16, rows), w.dtype)
    for n in range(copies):
        tiles[:, :, n * dim:(n + 1) * dim] = w
    return tiles.reshape(w.shape[0], 16 * rows)


def n_rows(np):
    return np.arange(P)


def layout(np, a):
    h = {}
    n = np.arange(P)
    h["x"] = a["L0_attn_x"].transpose(2, 0, 1).reshape(P, TOKENS)
    h["centre"] = (np.eye(P) - 1.0 / P).astype(np.float32)
    h["ident"] = np.eye(P, dtype=np.float32)
    h["mask_q"] = np.where(n[None, :] > n[:, None], MASKED, 0.0).astype(np.float32)
    h["mask_k"] = np.ascontiguousarray(h["mask_q"].T)
    h["aug_x"] = np.stack([np.ones(SEQ), np.ones(SEQ), np.arange(SEQ)]).astype(np.float32)
    h["aug_low"] = np.array([[0], [1], [0]], np.float32)
    low = np.zeros((P, 6), np.float32)
    low[:, 0] = ((n % 32 >= 16) & (n % 32 < 24)) | (n % 32 == 27)
    low[:, 1] = (n % 32 >= 8) & (n % 32 < 16)
    low[:, 2] = (n % 64 >= 32) & (n % 64 < 48)
    low[:, 3] = (n % 64 >= 16) & (n % 64 < 32)
    low[:, 4] = n >= 64
    low[:, 5] = 1
    h["low_rows"] = low

    def wo_tiles(w, width):
        padded = np.zeros((16, width, P), np.float32)
        padded[:, :w.shape[1]] = w
        return padded.reshape(-1, P, P).transpose(1, 0, 2)

    for p in ("q", "k"):
        h["l0a_w" + p] = head_tiles(np, a["L0_attn_W" + p].T.reshape(P, 16, 8), 32, 3)
    h["l0a_wv"] = a["L0_attn_Wv"].T
    h["l0a_wo"] = wo_tiles(a["L0_attn_Wo"].T.reshape(16, 8, P), 32)
    bv = np.zeros((16, 32), np.float32)
    bv[:, :8] = a["L0_attn_bv"].reshape(16, 8)
    h["l0a_bv"] = bv.reshape(4, P).T
    h["l0a_bo"] = a["L0_attn_bo"].reshape(P, 1)
    slopes = np.power(np.float32(2.0), -8.0 * np.arange(1, 17, dtype=np.float32) / 16).astype(np.float32)
    aug = np.zeros((3, 16, 32), np.float32)
    for n3 in range(3):
        aug[0:2, :, n3 * 8:n3 * 8 + 8] = a["L0_attn_bq"].reshape(1, 16, 8)
    aug[0:2, :, 26:28] = (slopes * np.float32(8 ** 0.5))[None, :, None]
    h["l0a_aug_q"] = aug.reshape(3, 512)
    aug = np.zeros((3, 16, 32), np.float32)
    for n3 in range(3):
        aug[0:2, :, n3 * 8:n3 * 8 + 8] = a["L0_attn_bk"].reshape(1, 16, 8)
    aug[2, :, 26:28] = 1.0
    h["l0a_aug_k"] = aug.reshape(3, 512)

    for p in ("q", "k"):
        h["l1a_w" + p] = head_tiles(np, a["L1_attn_w_" + p].transpose(2, 0, 1), 128, 2)
    h["l1a_wv"] = a["L1_attn_w_v"].transpose(2, 0, 1).reshape(P, 1024)
    h["l1a_wo"] = a["L1_attn_w_o"].reshape(8, P, P).transpose(1, 0, 2)

    for p in ("q", "k"):
        h["l2a_w" + p] = head_tiles(np, a["L2_attn_W" + p].reshape(P, 16, 16), 64, 3)
    h["l2a_wv"] = a["L2_attn_Wv"]
    h["l2a_wo"] = wo_tiles(a["L2_attn_Wo"].reshape(16, 16, P), 32)

    h["l0f_w"] = np.stack([a["L0_ffn_W_r"].T, a["L0_ffn_W_k"].T], axis=1)
    h["l0f_mu"] = np.stack([a["L0_ffn_mu_r"], a["L0_ffn_mu_k"]], axis=1)
    h["l0f_wv"] = a["L0_ffn_W_v"].T

    def columns(v):
        return v.reshape(-1, P).T

    def k_tiles(w):
        return w.reshape(-1, P, w.shape[1]).transpose(1, 0, 2)

    h["l1f_fc1_q"] = a["L1_ffn_fc1_q"]
    h["l1f_fc2_q"] = k_tiles(a["L1_ffn_fc2_q"])
    h["l1f_fc1_s"] = np.broadcast_to(a["L1_ffn_fc1_scales"], (P, 512))
    h["l1f_fc2_s"] = np.broadcast_to(a["L1_ffn_fc2_scales"][None], (P, 4, P))
    h["l1f_b1"] = columns(a["L1_ffn_fc1_bias"])
    h["l1f_b2"] = columns(a["L1_ffn_fc2_bias"])
    h["l1f_gamma"] = columns(a["L1_ffn_ln_gamma"])
    h["l1f_beta"] = columns(a["L1_ffn_ln_beta"])

    h["l2f_w12"] = np.concatenate([a["L2_ffn_w1_w"].T, a["L2_ffn_w2_w"].T], axis=1)
    for n in ("1", "2"):
        h["l2f_h" + n] = a["L2_ffn_h" + n + "_w"].reshape(4, P, 4, P).transpose(3, 0, 2, 1).reshape(P, 16 * P)
    h["l2f_w3"] = k_tiles(a["L2_ffn_w3_w"].T).reshape(P, 4 * P)
    h["l2f_scales"] = np.concatenate([columns(a["L2_ffn_" + n]) for n in ("w1_s", "w2_s", "h1_s", "h2_s", "w3_s")], axis=1)

    for n in ("q", "k", "v", "g"):
        h["l3a_w" + n] = a["L3_attn_W" + n].T
    h["l3a_wo"] = k_tiles(a["L3_attn_Wo"].T)
    h["l3a_bg"] = np.broadcast_to(a["L3_attn_bg"], (P, 8))
    h["l3a_gain"] = np.broadcast_to(a["L3_attn_qk_gain"].reshape(1, 1), (P, 1))
    chunk = np.arange(P) // 64
    between = np.zeros((P, 3, P), np.float32)
    between[:, 0] = between[:, 1] = (chunk[:, None] == 1) & (chunk[None, :] == 0)
    between[:, 2] = chunk[:, None] == 0
    h["l3a_between"] = between
    h["l3a_first_half"] = (chunk == 0).astype(np.float32).reshape(P, 1)
    h["l3a_mask"] = np.where(np.arange(64)[None, :] > (n_rows(np) % 64)[:, None], MASKED, 0.0).astype(np.float32)

    h["l3f_w_fc"] = a["L3_ffn_w_fc"].T
    h["l3f_w_proj"] = k_tiles(a["L3_ffn_w_proj"].T).reshape(P, 4 * P)
    h["l3f_bt"] = a["L3_ffn_fast_b"].T
    h["l3f_v"] = a["L3_ffn_v"]
    h["l3f_ut"] = a["L3_ffn_u"].T
    h["l3f_gate"] = np.broadcast_to(a["L3_ffn_gate"].reshape(1, 1), (P, 1))
    return h


def kernel(**inputs):
    import numpy as _np
    import concourse.bacc as _bacc
    from concourse import mybir as _mybir
    from concourse.bass_utils import run_bass_kernel_spmd as _run

    nc = _bacc.Bacc("TRN2", target_bir_lowering=False, num_devices=1)
    arrays, d = {}, {}
    for name, value in layout(_np, {n: _np.asarray(v) for n, v in inputs.items()}).items():
        value = _np.ascontiguousarray(value)
        arrays["in_" + name] = value
        d[name] = nc.dram_tensor("in_" + name, value.shape, _mybir.dt.from_np(value.dtype), kind="ExternalInput").ap()
    out = nc.dram_tensor("out", (P, TOKENS), _mybir.dt.float32, kind="ExternalOutput").ap()
    program(nc, d, out)
    r = _run(nc, [arrays], core_ids=[0])
    return _np.ascontiguousarray(r.results[0]["out"].reshape(P, BATCHES, SEQ).transpose(1, 2, 0))
```
